# Optimizing a Trainium2 kernel written in Bass

```python
import numpy as np
import jax
import jax.numpy as jnp

def _softmax(x, axis=-1):
    return jax.nn.softmax(x, axis=axis)

def _gelu(x):
    return jax.nn.gelu(x, approximate=True)

def _silu(x):
    return jax.nn.silu(x)

def _sigmoid(x):
    return jax.nn.sigmoid(x)

def _layernorm(x, axis=-1, eps=1e-05):
    m = jnp.mean(x, axis=axis, keepdims=True)
    v = jnp.var(x, axis=axis, keepdims=True)
    return (x - m) / jnp.sqrt(v + eps)

def _scatter_add(tgt, idx, src, axis=0):
    return tgt.at[idx].add(src)

def _segment_sum(src, seg, n):
    return jax.ops.segment_sum(src, seg, n)
kernel_name = 'mk_flamingo_gated_d4_seqx_r8_288157'

def setup_inputs(seed: int=0):
    np.random.seed(seed)
    _w = jnp.asarray

    def _rec_inputs():
        import jax
        import jax.numpy as jnp
        _rk = jax.random.key(seed)
        x = -0.0002928 + 1 * jax.random.normal(jax.random.fold_in(_rk, 1), (32, 128, 128), jnp.float32)
        _lenS = 128 - jax.random.randint(jax.random.fold_in(_rk, 7), (32,), 0, max(1, 128 // 4) + 1, jnp.int32)
        _lenS2 = 128 - jax.random.randint(jax.random.fold_in(_rk, 8), (32,), 0, max(1, 128 // 4) + 1, jnp.int32)
        _ctx_1024P = jax.random.normal(jax.random.fold_in(_rk, 11), (32, 16, 128), jnp.float32)
        _ctx_1024c = jax.random.dirichlet(jax.random.fold_in(_rk, 511), 0.3 * jnp.ones((16,), jnp.float32), (32, 128))
        _ctx_1024t = jnp.einsum('bsk,bkd->bsd', _ctx_1024c, _ctx_1024P)
        _ctx_1024t = _ctx_1024t * jax.lax.rsqrt(jnp.mean(jnp.square(_ctx_1024t)) + 1e-12) * 0.953939
        ctx_1024 = -1.39393e-06 + 0.999914 * (_ctx_1024t + 0.3 * jax.random.normal(jax.random.fold_in(_rk, 611), (32, 128, 128), jnp.float32))
        _g = jax.random.normal(jax.random.fold_in(_rk, 9001), (2, 4), jnp.float32)
        _g = jnp.sign(_g) * jnp.maximum(jnp.abs(_g), 1.0) + (_g == 0) * 1.0
        g_xattn = _g[0]
        g_ffn = _g[1]
        return (x, ctx_1024, g_xattn, g_ffn)
    x, ctx_1024, g_xattn, g_ffn = _rec_inputs()

    def _L0_xattn_setup():
        import jax, jax.numpy as jnp
        import numpy as np
        D_MODEL = 128
        HEADS = 16
        D_K = 64
        B, S = (2, 256)
        key = jax.random.key(seed)
        ks = jax.random.split(key, 12)
        s = 0.02
        return {'query': jax.random.normal(ks[0], (B, S, D_MODEL), dtype=jnp.float32), 'key': jax.random.normal(ks[1], (B, S, D_MODEL), dtype=jnp.float32), 'value': jax.random.normal(ks[2], (B, S, D_MODEL), dtype=jnp.float32), 'Wq': jax.random.normal(ks[3], (D_MODEL, HEADS * D_K), dtype=jnp.float32) * s, 'bq': jnp.zeros((HEADS * D_K,), dtype=jnp.float32), 'Wk': jax.random.normal(ks[4], (D_MODEL, HEADS * D_K), dtype=jnp.float32) * s, 'bk': jnp.zeros((HEADS * D_K,), dtype=jnp.float32), 'Wv': jax.random.normal(ks[5], (D_MODEL, HEADS * D_K), dtype=jnp.float32) * s, 'bv': jnp.zeros((HEADS * D_K,), dtype=jnp.float32), 'Wo': jax.random.normal(ks[6], (HEADS * D_K, D_MODEL), dtype=jnp.float32) * s, 'bo': jnp.zeros((D_MODEL,), dtype=jnp.float32)}
    _L0_xattn_all = _L0_xattn_setup()
    _L0_xattn_in = {k: v for k, v in _L0_xattn_all.items() if k in ('Wq', 'bq', 'Wk', 'bk', 'Wv', 'bv', 'Wo', 'bo')}
    del _L0_xattn_all

    def _L0_ffn_setup():
        import jax, jax.numpy as jnp
        import numpy as np
        D = 128
        H = 128
        E = 8
        K = 2
        I = 2 * 128
        ROUTE_SCALE = 1.0
        key = jax.random.key(seed)
        ks = jax.random.split(key, 12)
        s = lambda *sh: 1.0 / np.sqrt(sh[-1])
        return {'x': jax.random.normal(ks[0], (1, 256, D), jnp.float32), 'gate_w': jax.random.normal(ks[1], (E, D), jnp.float32) * s(E, D), 'w1': jax.random.normal(ks[2], (E, H, D), jnp.float32) * s(H, D), 'b1': jax.random.normal(ks[3], (E, H), jnp.float32) * 0.01, 'w2': jax.random.normal(ks[4], (E, D, H), jnp.float32) * s(D, H), 'b2': jax.random.normal(ks[5], (E, D), jnp.float32) * 0.01, 'w3': jax.random.normal(ks[6], (E, H, D), jnp.float32) * s(H, D), 'b3': jax.random.normal(ks[7], (E, H), jnp.float32) * 0.01, 'sw1': jax.random.normal(ks[8], (I, D), jnp.float32) * s(I, D), 'sw2': jax.random.normal(ks[9], (I, D), jnp.float32) * s(I, D), 'sw3': jax.random.normal(ks[10], (D, I), jnp.float32) * s(D, I)}
    _L0_ffn_all = _L0_ffn_setup()
    _L0_ffn_in = {k: v for k, v in _L0_ffn_all.items() if k in ('gate_w', 'w1', 'b1', 'w2', 'b2', 'w3', 'b3', 'sw1', 'sw2', 'sw3')}
    del _L0_ffn_all

    def _L1_xattn_setup():
        import jax, jax.numpy as jnp
        import numpy as np
        B, S, E, NH = (2, 256, 128, 4)
        HD = E // NH

        def _mlstm_head(q, k, v, ig, fg, eps=1e-06):
            s, dh = q.shape
            log_f = jax.nn.log_sigmoid(fg)
            cs = jnp.concatenate([jnp.zeros((1, 1), log_f.dtype), jnp.cumsum(log_f, axis=0)], axis=0)
            neg = jnp.asarray(-0.7 * jnp.finfo(cs.dtype).max, cs.dtype)
            log_d = jnp.where(jnp.tri(s, dtype=bool), (cs - cs.T)[1:, 1:] + ig.T, neg)
            m = jnp.max(log_d, axis=-1, keepdims=True)
            d = jnp.exp(log_d - m)
            c = q @ (k.T / jnp.sqrt(dh)) * d
            n = jnp.maximum(jnp.sum(c, axis=-1, keepdims=True), jnp.exp(-m))
            return c / (n + eps) @ v
        key = jax.random.key(seed)
        ks = jax.random.split(key, 8)
        return {'q': jax.random.normal(ks[0], (B, S, E), jnp.float32), 'k': jax.random.normal(ks[1], (B, S, E), jnp.float32), 'v': jax.random.normal(ks[2], (B, S, E), jnp.float32), 'igate_kernel': jax.random.normal(ks[3], (3 * E, NH), jnp.float32) * 0.02, 'igate_bias': jax.random.normal(ks[4], (NH,), jnp.float32) * 0.1, 'fgate_kernel': jax.random.normal(ks[5], (3 * E, NH), jnp.float32) * 0.02, 'fgate_bias': jnp.linspace(3.0, 6.0, NH, dtype=jnp.float32), 'rms_scale': jax.random.normal(ks[6], (HD,), jnp.float32) * 0.02}
    _L1_xattn_all = _L1_xattn_setup()
    _L1_xattn_in = {k: v for k, v in _L1_xattn_all.items() if k in ('igate_kernel', 'igate_bias', 'fgate_kernel', 'fgate_bias', 'rms_scale')}
    del _L1_xattn_all

    def _L1_ffn_setup():
        import jax, jax.numpy as jnp
        import numpy as np
        H = 128
        I = 64
        E = 8
        K = 2
        SI = I * 2
        B, S = (2, 128)

        def _mlp(x, gw, uw, dw):
            return jax.nn.silu(x @ gw.T) * (x @ uw.T) @ dw.T
        key = jax.random.key(seed)
        ks = jax.random.split(key, 9)
        s = 0.02
        return {'x': jax.random.normal(ks[0], (B, S, H), jnp.float32), 'gate_w': jax.random.normal(ks[1], (E, H), jnp.float32) * s, 'lb_bias': jnp.zeros((E,), jnp.float32), 'expert_gate_w': jax.random.normal(ks[2], (E, I, H), jnp.float32) * s, 'expert_up_w': jax.random.normal(ks[3], (E, I, H), jnp.float32) * s, 'expert_down_w': jax.random.normal(ks[4], (E, H, I), jnp.float32) * s, 'shared_gate_w': jax.random.normal(ks[5], (SI, H), jnp.float32) * s, 'shared_up_w': jax.random.normal(ks[6], (SI, H), jnp.float32) * s, 'shared_down_w': jax.random.normal(ks[7], (H, SI), jnp.float32) * s}
    _L1_ffn_all = _L1_ffn_setup()
    _L1_ffn_in = {k: v for k, v in _L1_ffn_all.items() if k in ('gate_w', 'lb_bias', 'expert_gate_w', 'expert_up_w', 'expert_down_w', 'shared_gate_w', 'shared_up_w', 'shared_down_w')}
    del _L1_ffn_all

    def _L2_xattn_setup():
        import jax, jax.numpy as jnp
        import numpy as np
        EPS = 1e-05

        def layer_norm(x, g, b):
            mu = jnp.mean(x, axis=-1, keepdims=True)
            var = jnp.var(x, axis=-1, keepdims=True)
            return (x - mu) * jax.lax.rsqrt(var + EPS) * g + b
        key = jax.random.key(seed)
        ks = jax.random.split(key, 8)
        dim, heads, dim_head = (128, 16, 64)
        inner = heads * dim_head
        b, n, m = (8, 512, 64)
        s = dim ** (-0.5)
        return {'x': jax.random.normal(ks[0], (b, n, dim), jnp.float32), 'latents': jax.random.normal(ks[1], (b, m, dim), jnp.float32), 'ln_m_g': jnp.ones((dim,), jnp.float32), 'ln_m_b': jnp.zeros((dim,), jnp.float32), 'ln_l_g': jnp.ones((dim,), jnp.float32), 'ln_l_b': jnp.zeros((dim,), jnp.float32), 'Wq': jax.random.normal(ks[2], (dim, inner), jnp.float32) * s, 'Wkv': jax.random.normal(ks[3], (dim, 2 * inner), jnp.float32) * s, 'Wout': jax.random.normal(ks[4], (inner, dim), jnp.float32) * s}
    _L2_xattn_all = _L2_xattn_setup()
    _L2_xattn_in = {k: v for k, v in _L2_xattn_all.items() if k in ('ln_m_g', 'ln_m_b', 'ln_l_g', 'ln_l_b', 'Wq', 'Wkv', 'Wout')}
    del _L2_xattn_all

    def _L2_ffn_setup():
        import jax, jax.numpy as jnp
        import numpy as np
        B, T, C = (8, 256, 128)
        E, K = (8, 2)
        H = 4 * C
        CAP_FACTOR = 1.2
        EPS = 1e-09
        key = jax.random.key(seed)
        ks = jax.random.split(key, 6)
        x = jax.random.normal(ks[0], (B, T, C), dtype=jnp.float32)
        router_w = jax.random.normal(ks[1], (E, C), dtype=jnp.float32) * 0.02
        router_b = jnp.zeros((E,), dtype=jnp.float32)
        fc1_w = jax.random.normal(ks[2], (E, H, C), dtype=jnp.float32) * (1.0 / np.sqrt(C))
        fc1_b = jnp.zeros((E, H), dtype=jnp.float32)
        fc2_w = jax.random.normal(ks[3], (E, C, H), dtype=jnp.float32) * (1.0 / np.sqrt(H))
        fc2_b = jnp.zeros((E, C), dtype=jnp.float32)
        layer_scale = jnp.full((E, C), 0.1, dtype=jnp.float32)
        return {'x': x, 'router_w': router_w, 'router_b': router_b, 'fc1_w': fc1_w, 'fc1_b': fc1_b, 'fc2_w': fc2_w, 'fc2_b': fc2_b, 'layer_scale': layer_scale}
    _L2_ffn_all = _L2_ffn_setup()
    _L2_ffn_in = {k: v for k, v in _L2_ffn_all.items() if k in ('router_w', 'router_b', 'fc1_w', 'fc1_b', 'fc2_w', 'fc2_b', 'layer_scale')}
    del _L2_ffn_all

    def _L3_xattn_setup():
        import jax, jax.numpy as jnp
        import numpy as np
        NUM_HEADS = 16
        DIM_HIDDEN = 128
        DIM_ATTN = DIM_HIDDEN // NUM_HEADS
        SCALE = DIM_ATTN ** (-0.5)
        TOP_K = 32

        def _split_heads(x, b, s):
            return x.reshape(b, s, NUM_HEADS, DIM_ATTN).transpose(0, 2, 1, 3)
        rng = jax.random.key(seed)
        k1, k2, k3, k4, k5 = jax.random.split(rng, 5)
        b, sq, sk, d = (2, 256, 256, DIM_HIDDEN)
        lim = 1.0 / np.sqrt(d)
        return {'query': jax.random.normal(k1, (b, sq, d), jnp.float32), 'key': jax.random.normal(k2, (b, sk, d), jnp.float32), 'value': jax.random.normal(k3, (b, sk, d), jnp.float32), 'Wq': jax.random.uniform(k4, (d, d), jnp.float32, -lim, lim), 'Wk': jax.random.uniform(k5, (d, d), jnp.float32, -lim, lim)}
    _L3_xattn_all = _L3_xattn_setup()
    _L3_xattn_in = {k: v for k, v in _L3_xattn_all.items() if k in ('Wq', 'Wk')}
    del _L3_xattn_all

    def _L3_ffn_setup():
        import jax, jax.numpy as jnp
        import numpy as np
        NH, NKV, E, K = (16, 4, 8, 2)
        CAP_FACTOR = 1.25
        LN_EPS = 1e-05

        def _layer_norm(x, w, b):
            mu = jnp.mean(x, axis=-1, keepdims=True)
            var = jnp.mean(jnp.square(x - mu), axis=-1, keepdims=True)
            return (x - mu) * jax.lax.rsqrt(var + LN_EPS) * w + b
        key = jax.random.key(seed)
        ks = jax.random.split(key, 6)
        S, B, H, F = (256, 1, 128, 256)
        HD = H // NH
        qkv_out = NKV * (NH // NKV + 2) * HD
        f32 = jnp.float32
        return {'hidden_states': jax.random.normal(ks[0], (S, B, H), f32), 'ln1_weight': jnp.ones((H,), f32), 'ln1_bias': jnp.zeros((H,), f32), 'ln2_weight': jnp.ones((H,), f32), 'ln2_bias': jnp.zeros((H,), f32), 'qkv_weight': jax.random.normal(ks[1], (qkv_out, H), f32) * 0.02, 'proj_weight': jax.random.normal(ks[2], (H, H), f32) * 0.02, 'router_weight': jax.random.normal(ks[3], (H, E), f32) * 0.02, 'moe_w1': jax.random.normal(ks[4], (E, H, F), f32) * 0.02, 'moe_w2': jax.random.normal(ks[5], (F and E, F, H), f32)[:E] * 0.02 if False else jax.random.normal(ks[5], (E, F, H), f32) * 0.02}
    _L3_ffn_all = _L3_ffn_setup()
    _L3_ffn_in = {k: v for k, v in _L3_ffn_all.items() if k in ('ln1_weight', 'ln1_bias', 'ln2_weight', 'ln2_bias', 'qkv_weight', 'proj_weight', 'router_weight', 'moe_w1', 'moe_w2')}
    del _L3_ffn_all
    return {'x': x, 'ctx_1024': ctx_1024, 'g_xattn': g_xattn, 'g_ffn': g_ffn, 'L0_xattn_Wq': _L0_xattn_in['Wq'], 'L0_xattn_bq': _L0_xattn_in['bq'], 'L0_xattn_Wk': _L0_xattn_in['Wk'], 'L0_xattn_bk': _L0_xattn_in['bk'], 'L0_xattn_Wv': _L0_xattn_in['Wv'], 'L0_xattn_bv': _L0_xattn_in['bv'], 'L0_xattn_Wo': _L0_xattn_in['Wo'], 'L0_xattn_bo': _L0_xattn_in['bo'], 'L0_ffn_gate_w': _L0_ffn_in['gate_w'], 'L0_ffn_w1': _L0_ffn_in['w1'], 'L0_ffn_b1': _L0_ffn_in['b1'], 'L0_ffn_w2': _L0_ffn_in['w2'], 'L0_ffn_b2': _L0_ffn_in['b2'], 'L0_ffn_w3': _L0_ffn_in['w3'], 'L0_ffn_b3': _L0_ffn_in['b3'], 'L0_ffn_sw1': _L0_ffn_in['sw1'], 'L0_ffn_sw2': _L0_ffn_in['sw2'], 'L0_ffn_sw3': _L0_ffn_in['sw3'], 'L1_xattn_igate_kernel': _L1_xattn_in['igate_kernel'], 'L1_xattn_igate_bias': _L1_xattn_in['igate_bias'], 'L1_xattn_fgate_kernel': _L1_xattn_in['fgate_kernel'], 'L1_xattn_fgate_bias': _L1_xattn_in['fgate_bias'], 'L1_xattn_rms_scale': _L1_xattn_in['rms_scale'], 'L1_ffn_gate_w': _L1_ffn_in['gate_w'], 'L1_ffn_lb_bias': _L1_ffn_in['lb_bias'], 'L1_ffn_expert_gate_w': _L1_ffn_in['expert_gate_w'], 'L1_ffn_expert_up_w': _L1_ffn_in['expert_up_w'], 'L1_ffn_expert_down_w': _L1_ffn_in['expert_down_w'], 'L1_ffn_shared_gate_w': _L1_ffn_in['shared_gate_w'], 'L1_ffn_shared_up_w': _L1_ffn_in['shared_up_w'], 'L1_ffn_shared_down_w': _L1_ffn_in['shared_down_w'], 'L2_xattn_ln_m_g': _L2_xattn_in['ln_m_g'], 'L2_xattn_ln_m_b': _L2_xattn_in['ln_m_b'], 'L2_xattn_ln_l_g': _L2_xattn_in['ln_l_g'], 'L2_xattn_ln_l_b': _L2_xattn_in['ln_l_b'], 'L2_xattn_Wq': _L2_xattn_in['Wq'], 'L2_xattn_Wkv': _L2_xattn_in['Wkv'], 'L2_xattn_Wout': _L2_xattn_in['Wout'], 'L2_ffn_router_w': _L2_ffn_in['router_w'], 'L2_ffn_router_b': _L2_ffn_in['router_b'], 'L2_ffn_fc1_w': _L2_ffn_in['fc1_w'], 'L2_ffn_fc1_b': _L2_ffn_in['fc1_b'], 'L2_ffn_fc2_w': _L2_ffn_in['fc2_w'], 'L2_ffn_fc2_b': _L2_ffn_in['fc2_b'], 'L2_ffn_layer_scale': _L2_ffn_in['layer_scale'], 'L3_xattn_Wq': _L3_xattn_in['Wq'], 'L3_xattn_Wk': _L3_xattn_in['Wk'], 'L3_ffn_ln1_weight': _L3_ffn_in['ln1_weight'], 'L3_ffn_ln1_bias': _L3_ffn_in['ln1_bias'], 'L3_ffn_ln2_weight': _L3_ffn_in['ln2_weight'], 'L3_ffn_ln2_bias': _L3_ffn_in['ln2_bias'], 'L3_ffn_qkv_weight': _L3_ffn_in['qkv_weight'], 'L3_ffn_proj_weight': _L3_ffn_in['proj_weight'], 'L3_ffn_router_weight': _L3_ffn_in['router_weight'], 'L3_ffn_moe_w1': _L3_ffn_in['moe_w1'], 'L3_ffn_moe_w2': _L3_ffn_in['moe_w2']}

def reference(x, ctx_1024, g_xattn, g_ffn, L0_xattn_Wq, L0_xattn_bq, L0_xattn_Wk, L0_xattn_bk, L0_xattn_Wv, L0_xattn_bv, L0_xattn_Wo, L0_xattn_bo, L0_ffn_gate_w, L0_ffn_w1, L0_ffn_b1, L0_ffn_w2, L0_ffn_b2, L0_ffn_w3, L0_ffn_b3, L0_ffn_sw1, L0_ffn_sw2, L0_ffn_sw3, L1_xattn_igate_kernel, L1_xattn_igate_bias, L1_xattn_fgate_kernel, L1_xattn_fgate_bias, L1_xattn_rms_scale, L1_ffn_gate_w, L1_ffn_lb_bias, L1_ffn_expert_gate_w, L1_ffn_expert_up_w, L1_ffn_expert_down_w, L1_ffn_shared_gate_w, L1_ffn_shared_up_w, L1_ffn_shared_down_w, L2_xattn_ln_m_g, L2_xattn_ln_m_b, L2_xattn_ln_l_g, L2_xattn_ln_l_b, L2_xattn_Wq, L2_xattn_Wkv, L2_xattn_Wout, L2_ffn_router_w, L2_ffn_router_b, L2_ffn_fc1_w, L2_ffn_fc1_b, L2_ffn_fc2_w, L2_ffn_fc2_b, L2_ffn_layer_scale, L3_xattn_Wq, L3_xattn_Wk, L3_ffn_ln1_weight, L3_ffn_ln1_bias, L3_ffn_ln2_weight, L3_ffn_ln2_bias, L3_ffn_qkv_weight, L3_ffn_proj_weight, L3_ffn_router_weight, L3_ffn_moe_w1, L3_ffn_moe_w2):
    import jax
    import jax.numpy as jnp

    def _L0_xattn_ref(query, key, value, Wq, bq, Wk, bk, Wv, bv, Wo, bo):
        import jax, jax.numpy as jnp
        import numpy as np
        D_MODEL = 128
        HEADS = 16
        D_K = 64
        B, S = (2, 256)
        b, s, _ = query.shape
        scale = 1.0 / np.sqrt(D_K).astype(np.float32)
        q = (query @ Wq + bq).reshape(b, s, HEADS, D_K)
        k = (key @ Wk + bk).reshape(b, s, HEADS, D_K)
        v = (value @ Wv + bv).reshape(b, s, HEADS, D_K)
        scores = jnp.einsum('bihd,bjhd->bijh', q, k) * scale
        attn = jax.nn.softmax(scores, axis=1)
        x = jnp.einsum('bijh,bjhd->bihd', attn, v).reshape(b, s, HEADS * D_K)
        return x @ Wo + bo

    def _L0_ffn_ref(x, gate_w, w1, b1, w2, b2, w3, b3, sw1, sw2, sw3):
        import jax, jax.numpy as jnp
        import numpy as np
        D = 128
        H = 128
        E = 8
        K = 2
        I = 2 * 128
        ROUTE_SCALE = 1.0
        B, S, _ = x.shape
        xt = x.reshape(-1, D)
        logits = xt @ gate_w.T
        scores = jax.nn.softmax(logits.astype(jnp.float32), axis=-1)
        top_vals, idx = jax.lax.top_k(scores, K)
        weights = jnp.take_along_axis(scores, idx, axis=1).astype(x.dtype) * ROUTE_SCALE
        xs = xt[:, None, :] * weights[:, :, None]
        y = jnp.zeros_like(xt)
        for e in range(E):
            mask = (idx == e).astype(x.dtype)
            h = jax.nn.silu(jnp.einsum('tkd,hd->tkh', xs, w1[e]) + b1[e])
            x2 = jnp.einsum('tkh,dh->tkd', h, w2[e]) + b2[e]
            x3 = jnp.einsum('tkd,hd->tkh', xs, w3[e]) + b3[e]
            y = y + jnp.sum(x2 * x3 * mask[:, :, None], axis=1)
        z = jax.nn.silu(xt @ sw1.T) * (xt @ sw2.T) @ sw3.T
        return (y + z).reshape(B, S, D)

    def _L1_xattn_ref(q, k, v, igate_kernel, igate_bias, fgate_kernel, fgate_bias, rms_scale):
        import jax, jax.numpy as jnp
        import numpy as np
        B, S, E, NH = (2, 256, 128, 4)
        HD = E // NH

        def _mlstm_head(q, k, v, ig, fg, eps=1e-06):
            s, dh = q.shape
            log_f = jax.nn.log_sigmoid(fg)
            cs = jnp.concatenate([jnp.zeros((1, 1), log_f.dtype), jnp.cumsum(log_f, axis=0)], axis=0)
            neg = jnp.asarray(-0.7 * jnp.finfo(cs.dtype).max, cs.dtype)
            log_d = jnp.where(jnp.tri(s, dtype=bool), (cs - cs.T)[1:, 1:] + ig.T, neg)
            m = jnp.max(log_d, axis=-1, keepdims=True)
            d = jnp.exp(log_d - m)
            c = q @ (k.T / jnp.sqrt(dh)) * d
            n = jnp.maximum(jnp.sum(c, axis=-1, keepdims=True), jnp.exp(-m))
            return c / (n + eps) @ v
        b, s, e = q.shape
        nh = igate_kernel.shape[1]
        hd = e // nh
        gate_in = jnp.concatenate((q, k, v), axis=-1)
        ig = (gate_in @ igate_kernel + igate_bias).swapaxes(-1, -2)[..., None]
        fg = (gate_in @ fgate_kernel + fgate_bias).swapaxes(-1, -2)[..., None]
        qh = q.reshape(b, s, nh, hd).swapaxes(1, 2)
        kh = k.reshape(b, s, nh, hd).swapaxes(1, 2)
        vh = v.reshape(b, s, nh, hd).swapaxes(1, 2)
        h = jax.vmap(jax.vmap(_mlstm_head))(qh, kh, vh, ig, fg)
        var = jnp.mean(jnp.square(h.astype(jnp.float32)), axis=-1, keepdims=True)
        h = (h * jax.lax.rsqrt(var + 1e-06)).astype(h.dtype) * (1.0 + rms_scale)
        return h.swapaxes(1, 2).reshape(b, s, e)

    def _L1_ffn_ref(x, gate_w, lb_bias, expert_gate_w, expert_up_w, expert_down_w, shared_gate_w, shared_up_w, shared_down_w):
        import jax, jax.numpy as jnp
        import numpy as np
        H = 128
        I = 64
        E = 8
        K = 2
        SI = I * 2
        B, S = (2, 128)

        def _mlp(x, gw, uw, dw):
            return jax.nn.silu(x @ gw.T) * (x @ uw.T) @ dw.T
        b, s, h = x.shape
        xf = x.reshape(-1, h)
        logits = xf @ gate_w.T + lb_bias
        scores = jax.nn.sigmoid(logits.astype(jnp.float32))
        topw, topi = jax.lax.top_k(scores, K)
        topw = (topw / (topw.sum(-1, keepdims=True) + 1e-08)).astype(x.dtype)
        out = jnp.zeros_like(xf)
        for e in range(E):
            m = topi == e
            sel = m.any(axis=-1)
            cnt = m.sum()
            wmean = (topw * m).sum() / jnp.maximum(cnt, 1).astype(topw.dtype)
            y = _mlp(xf, expert_gate_w[e], expert_up_w[e], expert_down_w[e])
            out = out + jnp.where(sel[:, None], y * wmean, jnp.zeros((), x.dtype))
        out = out.reshape(b, s, h)
        out = out + _mlp(x, shared_gate_w, shared_up_w, shared_down_w)
        return out

    def _L2_xattn_ref(x, latents, ln_m_g, ln_m_b, ln_l_g, ln_l_b, Wq, Wkv, Wout):
        import jax, jax.numpy as jnp
        import numpy as np
        EPS = 1e-05

        def layer_norm(x, g, b):
            mu = jnp.mean(x, axis=-1, keepdims=True)
            var = jnp.var(x, axis=-1, keepdims=True)
            return (x - mu) * jax.lax.rsqrt(var + EPS) * g + b
        heads, dim_head = (16, 64)
        scale = dim_head ** (-0.5)
        x = layer_norm(x, ln_m_g, ln_m_b)
        lat = layer_norm(latents, ln_l_g, ln_l_b)
        b, m, _ = lat.shape
        q = lat @ Wq
        kv_input = jnp.concatenate([x, lat], axis=1)
        kv = kv_input @ Wkv
        k, v = jnp.split(kv, 2, axis=-1)

        def split_heads(t):
            return t.reshape(t.shape[0], t.shape[1], heads, dim_head).transpose(0, 2, 1, 3)
        q, k, v = (split_heads(q), split_heads(k), split_heads(v))
        dots = jnp.einsum('bhid,bhjd->bhij', q, k) * scale
        attn = jax.nn.softmax(dots, axis=-1)
        out = jnp.einsum('bhij,bhjd->bhid', attn, v)
        out = out.transpose(0, 2, 1, 3).reshape(b, m, heads * dim_head)
        return out @ Wout

    def _L2_ffn_ref(x, router_w, router_b, fc1_w, fc1_b, fc2_w, fc2_b, layer_scale):
        import jax, jax.numpy as jnp
        import numpy as np
        B, T, C = (8, 256, 128)
        E, K = (8, 2)
        H = 4 * C
        CAP_FACTOR = 1.2
        EPS = 1e-09
        Bb, Tt, Cc = x.shape
        N = Bb * Tt
        KN = K * N
        capacity = int(CAP_FACTOR * (N // E + 1))
        xf = x.reshape(N, Cc)
        logits = xf @ router_w.T + router_b
        probs = jax.nn.softmax(logits, axis=-1)
        top_vals, top_inds = jax.lax.top_k(probs, K)
        top_vals = top_vals / (jnp.sum(top_vals, axis=-1, keepdims=True) + EPS)
        e_flat = top_inds.T.reshape(-1)
        w_flat = top_vals.T.reshape(-1)
        valid = w_flat > EPS
        onehot = (e_flat[:, None] == jnp.arange(E)[None, :]) & valid[:, None]
        pos = jnp.cumsum(onehot.astype(jnp.int32), axis=0) - 1
        pos_own = jnp.take_along_axis(pos, e_flat[:, None], axis=1)[:, 0]
        keep = valid & (pos_own < capacity)
        scores = jnp.where(keep[None, :] & (e_flat[None, :] == jnp.arange(E)[:, None]), jnp.arange(KN)[None, :], KN)
        sel = jnp.sort(scores, axis=1)[:, :capacity]
        slot_valid = sel < KN
        sel_c = jnp.where(slot_valid, sel, 0)
        tok = sel_c % N
        wgt = jnp.where(slot_valid, w_flat[sel_c], 0.0)
        toks = xf[tok]
        h = jax.nn.gelu(jnp.einsum('etc,ehc->eth', toks, fc1_w) + fc1_b[:, None, :], approximate=False)
        y = jnp.einsum('eth,ech->etc', h, fc2_w) + fc2_b[:, None, :]
        y = toks + y * layer_scale[:, None, :]
        out = jnp.zeros((N, Cc), dtype=x.dtype)
        out = out.at[tok.reshape(-1)].add((wgt[..., None] * y).reshape(-1, Cc))
        return out.reshape(Bb, Tt, Cc)

    def _L3_xattn_ref(query, key, value, Wq, Wk):
        import jax, jax.numpy as jnp
        import numpy as np
        NUM_HEADS = 16
        DIM_HIDDEN = 128
        DIM_ATTN = DIM_HIDDEN // NUM_HEADS
        SCALE = DIM_ATTN ** (-0.5)
        TOP_K = 32

        def _split_heads(x, b, s):
            return x.reshape(b, s, NUM_HEADS, DIM_ATTN).transpose(0, 2, 1, 3)
        b, sq, d = query.shape
        sk = key.shape[1]
        q = _split_heads(query @ Wq.T, b, sq)
        k = _split_heads(key @ Wk.T, b, sk)
        v = _split_heads(value, b, sk)
        scores = jnp.einsum('bhqa,bhka->bhqk', q, k) * SCALE
        top_vals = jax.lax.top_k(scores, TOP_K)[0]
        cutoff = top_vals[..., -1:]
        masked = jnp.where(scores >= cutoff, scores, -jnp.inf)
        w = jax.nn.softmax(masked, axis=-1)
        e = jnp.einsum('bhqk,bhka->bhqa', w, v)
        return e.transpose(0, 2, 1, 3).reshape(b, sq, d)

    def _L3_ffn_ref(hidden_states, ln1_weight, ln1_bias, ln2_weight, ln2_bias, qkv_weight, proj_weight, router_weight, moe_w1, moe_w2):
        import jax, jax.numpy as jnp
        import numpy as np
        NH, NKV, E, K = (16, 4, 8, 2)
        CAP_FACTOR = 1.25
        LN_EPS = 1e-05

        def _layer_norm(x, w, b):
            mu = jnp.mean(x, axis=-1, keepdims=True)
            var = jnp.mean(jnp.square(x - mu), axis=-1, keepdims=True)
            return (x - mu) * jax.lax.rsqrt(var + LN_EPS) * w + b
        S, B, H = hidden_states.shape
        HD = H // NH
        q_per_kv = NH // NKV
        ln1 = _layer_norm(hidden_states, ln1_weight, ln1_bias)
        qkv = jnp.einsum('sbh,oh->sbo', ln1, qkv_weight)
        qkv = qkv.reshape(S, B, NKV, (q_per_kv + 2) * HD)
        q = qkv[..., :q_per_kv * HD].reshape(S, B, NH, HD)
        k = qkv[..., q_per_kv * HD:(q_per_kv + 1) * HD]
        v = qkv[..., (q_per_kv + 1) * HD:]
        qb = jnp.transpose(q, (1, 2, 0, 3)).reshape(B, NKV, q_per_kv, S, HD)
        kb = jnp.transpose(k, (1, 2, 0, 3))
        vb = jnp.transpose(v, (1, 2, 0, 3))
        scale = 1.0 / np.sqrt(HD).astype(np.float32)
        scores = jnp.einsum('bgqsd,bgtd->bgqst', qb, kb) * scale
        causal = jnp.tril(jnp.ones((S, S), bool))
        scores = jnp.where(causal, scores, jnp.finfo(scores.dtype).min)
        attn = jax.nn.softmax(scores, axis=-1)
        ao = jnp.einsum('bgqst,bgtd->bgqsd', attn, vb)
        ao = ao.reshape(B, NH, S, HD)
        ao = jnp.transpose(ao, (2, 0, 1, 3)).reshape(S, B, H)
        proj = jnp.einsum('sbh,oh->sbo', ao, proj_weight)
        h1 = hidden_states + proj
        ln2 = _layer_norm(h1, ln2_weight, ln2_bias)
        x = ln2.reshape(-1, H)
        N = x.shape[0]
        logits = x @ router_weight
        probs = jax.nn.softmax(logits, axis=-1)
        top_p, top_i = jax.lax.top_k(probs, K)
        top_p = top_p / jnp.sum(top_p, axis=-1, keepdims=True)
        exp_idx = top_i.reshape(-1)
        exp_p = top_p.reshape(-1)
        order = jnp.argsort(exp_idx, stable=True)
        sorted_exp = exp_idx[order]
        counts = jnp.bincount(exp_idx, length=E)
        offsets = jnp.concatenate([jnp.zeros((1,), counts.dtype), jnp.cumsum(counts)[:-1]])
        within = jnp.arange(N * K) - offsets[sorted_exp]
        cap = int(np.ceil(N * K / E * CAP_FACTOR))
        T = E * cap
        valid = within < cap
        dst = jnp.where(valid, sorted_exp * cap + within, T)
        padded_tokens = jnp.zeros((T, H), x.dtype).at[dst].set(x[order // K], mode='drop')
        padded_probs = jnp.zeros((T,), exp_p.dtype).at[dst].set(exp_p[order], mode='drop')
        padded_tid = jnp.zeros((T,), jnp.int32).at[dst].set((order // K).astype(jnp.int32), mode='drop')
        xt = padded_tokens.reshape(E, cap, H)
        fc1 = jax.nn.gelu(jnp.einsum('ech,ehf->ecf', xt, moe_w1))
        fc2 = jnp.einsum('ecf,efh->ech', fc1, moe_w2).reshape(T, H)
        weighted = fc2 * padded_probs[:, None]
        moe_out = jnp.zeros((N, H), hidden_states.dtype).at[padded_tid].add(weighted)
        return h1 + moe_out.reshape(S, B, H)
    x = x + jnp.tanh(g_xattn[0]) * _L0_xattn_ref(_layernorm(x, axis=-1), ctx_1024, ctx_1024, L0_xattn_Wq, L0_xattn_bq, L0_xattn_Wk, L0_xattn_bk, L0_xattn_Wv, L0_xattn_bv, L0_xattn_Wo, L0_xattn_bo)
    x = x + jnp.tanh(g_ffn[0]) * _L0_ffn_ref(_layernorm(x, axis=-1), L0_ffn_gate_w, L0_ffn_w1, L0_ffn_b1, L0_ffn_w2, L0_ffn_b2, L0_ffn_w3, L0_ffn_b3, L0_ffn_sw1, L0_ffn_sw2, L0_ffn_sw3)
    x = x + jnp.tanh(g_xattn[1]) * _L1_xattn_ref(_layernorm(x, axis=-1), ctx_1024, ctx_1024, L1_xattn_igate_kernel, L1_xattn_igate_bias, L1_xattn_fgate_kernel, L1_xattn_fgate_bias, L1_xattn_rms_scale)
    x = x + jnp.tanh(g_ffn[1]) * _L1_ffn_ref(_layernorm(x, axis=-1), L1_ffn_gate_w, L1_ffn_lb_bias, L1_ffn_expert_gate_w, L1_ffn_expert_up_w, L1_ffn_expert_down_w, L1_ffn_shared_gate_w, L1_ffn_shared_up_w, L1_ffn_shared_down_w)
    x = x + jnp.tanh(g_xattn[2]) * _L2_xattn_ref(ctx_1024, _layernorm(x, axis=-1), L2_xattn_ln_m_g, L2_xattn_ln_m_b, L2_xattn_ln_l_g, L2_xattn_ln_l_b, L2_xattn_Wq, L2_xattn_Wkv, L2_xattn_Wout)
    x = x + jnp.tanh(g_ffn[2]) * _L2_ffn_ref(_layernorm(x, axis=-1), L2_ffn_router_w, L2_ffn_router_b, L2_ffn_fc1_w, L2_ffn_fc1_b, L2_ffn_fc2_w, L2_ffn_fc2_b, L2_ffn_layer_scale)
    x = x + jnp.tanh(g_xattn[3]) * _L3_xattn_ref(_layernorm(x, axis=-1), ctx_1024, ctx_1024, L3_xattn_Wq, L3_xattn_Wk)
    x = x + jnp.tanh(g_ffn[3]) * _L3_ffn_ref(_layernorm(x, axis=-1), L3_ffn_ln1_weight, L3_ffn_ln1_bias, L3_ffn_ln2_weight, L3_ffn_ln2_bias, L3_ffn_qkv_weight, L3_ffn_proj_weight, L3_ffn_router_weight, L3_ffn_moe_w1, L3_ffn_moe_w2)
    return x

_drawn_inputs = setup_inputs


def setup_inputs(seed=0):
    import zlib

    import numpy as np

    out = dict(_drawn_inputs(seed))
    spreads = {'L0_xattn_bq': (0.0, 2.0),
     'L0_xattn_bk': (0.0, 0.367),
     'L0_xattn_bv': (0.0, 0.1),
     'L0_xattn_bo': (0.0, 0.1),
     'L1_ffn_lb_bias': (0.0, 0.665),
     'L2_xattn_ln_m_g': (1.0, 0.2),
     'L2_xattn_ln_m_b': (0.0, 0.1),
     'L2_xattn_ln_l_g': (1.0, 0.2),
     'L2_xattn_ln_l_b': (0.0, 0.1),
     'L2_ffn_router_b': (0.0, 0.1),
     'L2_ffn_fc1_b': (0.0, 0.8),
     'L2_ffn_fc2_b': (0.0, 0.701),
     'L2_ffn_layer_scale': (0.10000000149011612, 0.6),
     'L3_ffn_ln1_weight': (1.0, 0.6),
     'L3_ffn_ln1_bias': (0.0, 0.8),
     'L3_ffn_ln2_weight': (1.0, 0.6),
     'L3_ffn_ln2_bias': (0.0, 0.8)}
    factors = {'g_ffn': 11.321,
     'L0_xattn_Wq': 2.905,
     'L0_xattn_Wk': 3.125,
     'L0_ffn_b1': 3.776,
     'L0_ffn_b2': 2.726,
     'L0_ffn_b3': 3.69,
     'L1_xattn_igate_bias': 64.0,
     'L1_ffn_gate_w': 4.842,
     'L1_ffn_expert_gate_w': 3.307,
     'L1_ffn_expert_up_w': 3.286,
     'L1_ffn_expert_down_w': 4.235,
     'L1_ffn_shared_gate_w': 2.69,
     'L1_ffn_shared_up_w': 3.124,
     'L1_ffn_shared_down_w': 3.144,
     'L3_ffn_qkv_weight': 5.9,
     'L3_ffn_proj_weight': 5.393,
     'L3_ffn_router_weight': 5.044,
     'L3_ffn_moe_w1': 4.398,
     'L3_ffn_moe_w2': 4.308}
    for name, (base, spread) in spreads.items():
        noise = np.random.default_rng([zlib.crc32(name.encode()), seed]).standard_normal(out[name].shape)
        drawn = base * np.exp(spread * noise) if base else spread * noise
        out[name] = jnp.asarray(drawn.astype(out[name].dtype))
    for name, factor in factors.items():
        out[name] = (out[name] * factor).astype(out[name].dtype)
    return out
```

```python
from contextlib import ExitStack

import concourse.bass as bass
from concourse import mybir

F32 = mybir.dt.float32
BF16 = mybir.dt.bfloat16
ALU = mybir.AluOpType
ACT = mybir.ActivationFunctionType
AX = mybir.AxisListType
ds = bass.ds

P = 128
NB = 32
D = 128
G4 = 4
NG = NB // G4
E = 8
BANK = 512
LN_EPS = 1e-5


class Chain:

    def __init__(self, eng, sem, base=0):
        self.eng, self.sem, self.base, self.n = eng, sem, base, 0

    def __call__(self, ins):
        ins.then_inc(self.sem, 1)
        self.n += 1
        self.eng.wait_ge(self.sem, self.base + self.n)

    def steps(self, n):
        assert self.n == n, (self.n, n)


def wait_apart(eng, sem):
    eng.sem_inc(sem, 1)


def per_row(ap, n):
    return ap.unsqueeze(2).to_broadcast([ap.shape[0], ap.shape[1], n])


def per_group(ap, n):
    return ap.unsqueeze(1).to_broadcast([ap.shape[0], n, ap.shape[1]])


class Shared:
    pass


class Stage:

    def __init__(self, held):
        self.sems, self.held = [], held


class Space:

    def __init__(self, nc, ctx, name, k=None):
        self.nc, self.ctx, self.name = nc, ctx, name
        self.sem_ctx = ctx
        if k is not None:
            self.sem_ctx = k.finals.enter_context(ExitStack())
            k.stages.append(Stage(self.sem_ctx))
            self.stage = k.stages[-1]

    def sb(self, name, shape, dt=F32):
        return self.ctx.enter_context(self.nc.sbuf_tensor(f"{self.name}_{name}", shape, dt))

    def ps(self, name, shape, dt=F32):
        return self.ctx.enter_context(self.nc.psum_tensor(f"{self.name}_{name}_ps", shape, dt))

    def sem(self, name):
        sem = self.sem_ctx.enter_context(self.nc.semaphore(f"{self.name}_{name}"))
        if self.sem_ctx is not self.ctx:
            self.stage.sems.append(sem)
        return sem


def zero_last_stage(block, k):
    if len(k.stages) < 2:
        return
    if len(k.stages) > 2:
        k.stages.pop(0).held.close()
    last = k.stages[0].sems

    @block.sync
    def _(sp):
        for sem in last:
            sp.sem_clear(sem)


def setup(nc, k):
    with ExitStack() as ctx:
        s = Space(nc, ctx, "setup", k)
        gates_raw = s.sb("gates_raw", [P, 8])
        x_in, gates_in, filled, made, tanh_done = (s.sem(n) for n in (
            "x_in", "gates_in", "filled", "made", "tanh_done"))
        with nc.Block() as block:
            zero_last_stage(block, k)

            @block.sync
            def _(sp):
                sp.dma_start(k.x[:, :, :], k.d["x"].rearrange("b p d -> p b d")).then_inc(x_in, 16)
                sp.dma_start(gates_raw[:, 0:4], k.d["g_xattn"].partition_broadcast(P)).then_inc(gates_in, 16)
                sp.dma_start(gates_raw[:, 4:8], k.d["g_ffn"].partition_broadcast(P)).then_inc(gates_in, 16)
                sp.dma_start(k.gates_w[:, :, :], k.d["routers"]).then_inc(x_in, 16)
                sp.wait_ge(x_in, 32)

            @block.scalar
            def _(act):
                act.wait_ge(gates_in, 32)
                act.activation(k.tg[:, :], gates_raw[:, :], ACT.Tanh).then_inc(tanh_done, 1)
                act.wait_ge(tanh_done, 1)

            @block.gpsimd
            def _(pool):
                pool.memset(k.ident[:, :], 0.0).then_inc(filled, 1)
                pool.memset(k.lower[:, :], 1.0).then_inc(filled, 1)
                pool.memset(k.upto[:, :], 1.0).then_inc(filled, 1)
                pool.memset(k.ones[:, :], 1.0).then_inc(filled, 1)
                pool.memset(k.neg_half[:, :], -0.5).then_inc(filled, 1)
                for e in range(E):
                    pool.memset(k.rank[:, e:e + 1], float(E - e)).then_inc(filled, 1)
                pool.wait_ge(filled, 5 + E)
                pool.affine_select(out=k.ident[:, :], in_=k.ident[:, :], compare_op=ALU.not_equal, fill=1.0,
                                   base=0, pattern=[[-1, P]], channel_multiplier=1).then_inc(made, 1)
                pool.affine_select(out=k.upto[:, :], in_=k.upto[:, :], compare_op=ALU.is_ge, fill=0.0,
                                   base=0, pattern=[[1, P]], channel_multiplier=-1).then_inc(made, 1)
                pool.affine_select(out=k.lower[:, :], in_=k.lower[:, :], compare_op=ALU.is_ge, fill=0.0,
                                   base=0, pattern=[[-1, P]], channel_multiplier=1).then_inc(made, 1)
                pool.wait_ge(made, 3)


def load_weights(nc, k, name, loads):
    with ExitStack() as ctx:
        s = Space(nc, ctx, name, k)
        weights_in = s.sem("weights_in")
        with nc.Block() as block:
            zero_last_stage(block, k)

            @block.sync
            def _(sp):
                for dst, src in loads:
                    sp.dma_start(dst, src).then_inc(weights_in, 16)
                sp.wait_ge(weights_in, 16 * len(loads))


def normalise(nc, k, name, source="x", twice=False, gain=None, shift=None, keep_rows=False,
              gate_w=None, columns=None, logits=None):
    columns = k.cols if columns is None else columns
    with ExitStack() as ctx:
        s = Space(nc, ctx, name, k)
        from_dram = not isinstance(source, str)
        raw = s.sb("raw", [P, NB, D]) if from_dram else {"x": k.x, "rows": k.rows}[source]
        stats = s.sb("stats", [P, NB, 6])
        mean, var, dif, rstd, rstd2, veps = (s.sb(n, [P, NB]) for n in (
            "mean", "var", "dif", "rstd", "rstd2", "veps"))
        stage = [s.sb(f"stage{i}", [P, G4, D]) for i in range(2)]
        stage_rows = [s.sb(f"stage_rows{i}", [P, G4, D]) for i in range(2)]
        stage_t = [s.sb(f"stage_t{i}", [P, G4 * P]) for i in range(2)]
        turned_ps = [s.ps(f"turned{i}", [P, BANK]) for i in range(2)]
        logit_ps = [s.ps(f"logit{i}", [P, BANK]) for i in range(2)]
        (raw_in, chain, veps_ready, rstd_ready, normed, turned, evacuated, stored, rows_stored,
         logit_mm, logit_out, stats_done) = (s.sem(n) for n in (
             "raw_in", "chain", "veps_ready", "rstd_ready", "normed", "turned", "evacuated", "stored",
             "rows_stored", "logit_mm", "logit_out", "stats_done"))
        with nc.Block() as block:
            zero_last_stage(block, k)

            @block.sync
            def _(sp):
                if from_dram:
                    sp.dma_start(raw[:, :, :], source.rearrange("b p d -> p b d")).then_inc(raw_in, 16)

            @block.vector
            def _(dve):
                if from_dram:
                    dve.wait_ge(raw_in, 16)
                with dve.Fori(0, NG) as g:
                    for j in range(G4):
                        dve.bn_stats(stats[:, ds(g * G4 + j, 1), :].rearrange("p o s -> p (o s)"),
                                     raw[:, ds(g * G4 + j, 1), :].rearrange("p o d -> p (o d)")).then_inc(stats_done, 1)
                dve.wait_ge(stats_done, NB)
                link = Chain(dve, chain)
                even_mean, even_m2, odd_mean, odd_m2 = (stats[:, :, i] for i in (1, 2, 4, 5))
                link(dve.tensor_tensor(dif[:, :], even_mean, odd_mean, ALU.subtract))
                link(dve.tensor_tensor(mean[:, :], even_mean, odd_mean, ALU.add))
                link(dve.tensor_tensor(var[:, :], even_m2, odd_m2, ALU.add))
                link(dve.tensor_scalar(mean[:, :], mean[:, :], 0.5, None, ALU.mult))
                link(dve.scalar_tensor_tensor(out=dif[:, :], in0=dif[:, :], scalar=0.25, in1=dif[:, :],
                                              op0=ALU.mult, op1=ALU.mult))
                link(dve.scalar_tensor_tensor(out=var[:, :], in0=var[:, :], scalar=1.0 / D, in1=dif[:, :],
                                              op0=ALU.mult, op1=ALU.add))
                dve.tensor_scalar(veps[:, :], var[:, :], LN_EPS, None, ALU.add).then_inc(veps_ready, 1)
                dve.wait_ge(rstd_ready, 1)
                scale = rstd
                if twice:
                    link(dve.tensor_tensor(dif[:, :], var[:, :], rstd[:, :], ALU.mult))
                    link(dve.tensor_tensor(dif[:, :], dif[:, :], rstd[:, :], ALU.mult))
                    dve.tensor_scalar(veps[:, :], dif[:, :], LN_EPS, None, ALU.add).then_inc(veps_ready, 1)
                    dve.wait_ge(rstd_ready, 2)
                    link(dve.tensor_tensor(rstd2[:, :], rstd2[:, :], rstd[:, :], ALU.mult))
                    scale = rstd2
                with dve.Fori(0, NG // 2) as g:
                    for h in range(2):
                        if keep_rows:
                            dve.wait_ge(rows_stored, g * 2 + h - 1 if h else g * 2)
                        for j in range(G4):
                            t = g * 2 * G4 + h * G4 + j
                            if j == 0:
                                dve.wait_ge(turned, g * 2)
                            dve.tensor_scalar(stage[h][:, j, :], raw[:, ds(t, 1), :].rearrange("p o d -> p (o d)"),
                                              mean[:, ds(t, 1)], scale[:, ds(t, 1)], ALU.subtract, ALU.mult
                                              ).then_inc(normed, 1)
                        if keep_rows and twice:
                            for j in range(G4):
                                t = g * 2 * G4 + h * G4 + j
                                dve.tensor_scalar(stage_rows[h][:, j, :],
                                                  raw[:, ds(t, 1), :].rearrange("p o d -> p (o d)"),
                                                  mean[:, ds(t, 1)], rstd[:, ds(t, 1)], ALU.subtract, ALU.mult
                                                  ).then_inc(stats_done, 1)
                        if gate_w is not None and h:
                            dve.wait_ge(logit_mm, g * 2 + 1)
                            dve.tensor_copy(logits[:, ds(g * 2 * G4, G4), :],
                                            logit_ps[0][:, 0:G4 * E].rearrange("p (t e) -> p t e", e=E)
                                            ).then_inc(logit_out, 1)
                    if gate_w is not None:
                        dve.wait_ge(logit_mm, g * 2 + 2)
                        dve.tensor_copy(logits[:, ds(g * 2 * G4 + G4, G4), :],
                                        logit_ps[1][:, 0:G4 * E].rearrange("p (t e) -> p t e", e=E)
                                        ).then_inc(logit_out, 1)

            @block.tensor
            def _(pe):
                with pe.Fori(0, NG // 2) as g:
                    for h in range(2):
                        pe.wait_ge(normed, (g * 2 + h + 1) * G4)
                        pe.wait_ge(evacuated, g * 2)
                        for j in range(G4):
                            ins = pe.transpose(turned_ps[h][:, j * P:(j + 1) * P], stage[h][:, j, :], k.ident[:, :])
                        ins.then_inc(turned, 1)
                        if gate_w is not None:
                            pe.wait_ge(evacuated, g * 2 + h + 1)
                            pe.wait_ge(logit_out, g * 2)
                            for j in range(G4):
                                ins = pe.matmul(logit_ps[h][:, j * E:(j + 1) * E], stage_t[h][:, j * P:(j + 1) * P],
                                                gate_w, start=True, stop=True)
                            ins.then_inc(logit_mm, 1)

            @block.scalar
            def _(act):
                with act.Fori(0, NG // 2) as g:
                    for h in range(2):
                        act.wait_ge(turned, g * 2 + h + 1)
                        act.wait_ge(stored, g * 2)
                        if gate_w is not None:
                            act.wait_ge(logit_mm, g * 2)
                        if gain is None:
                            act.activation(stage_t[h][:, :], turned_ps[h][:, :], ACT.Copy).then_inc(evacuated, 1)
                        else:
                            act.activation(stage_t[h][:, :], turned_ps[h][:, :], ACT.Identity,
                                           scale=gain, bias=shift).then_inc(evacuated, 1)

            @block.gpsimd
            def _(pool):
                pool.wait_ge(veps_ready, 1)
                pool.tensor_tensor(rstd[:, :], veps[:, :], k.neg_half[:, :], ALU.pow).then_inc(rstd_ready, 1)
                if twice:
                    pool.wait_ge(veps_ready, 2)
                    pool.tensor_tensor(rstd2[:, :], veps[:, :], k.neg_half[:, :], ALU.pow).then_inc(rstd_ready, 1)
                with pool.Fori(0, NG // 2) as g:
                    for h in range(2):
                        if keep_rows:
                            kept = stage_rows if twice else stage
                            if twice:
                                pool.wait_ge(stats_done, NB + (g * 2 + h + 1) * G4)
                            else:
                                pool.wait_ge(normed, (g * 2 + h + 1) * G4)
                            pool.tensor_copy(k.rows[:, ds((g * 2 + h) * G4, G4), :], kept[h][:, :, :]
                                             ).then_inc(rows_stored, 1)
                        pool.wait_ge(evacuated, g * 2 + h + 1)
                        pool.tensor_copy(columns[:, ds((g * 2 + h) * G4 * P, G4 * P)], stage_t[h][:, :]
                                         ).then_inc(stored, 1)


def l0_attention(nc, k):
    H, DK = 16, 64
    C = H * DK // P
    SC = 1.0 / DK ** 0.5
    with ExitStack() as ctx:
        s = Space(nc, ctx, "l0a", k)
        wq, wk, wv = (s.sb(n, [P, C * P]) for n in ("wq", "wk", "wv"))
        wo = s.sb("wo", [P, C, D])
        bq, bk = s.sb("bq", [P, C]), s.sb("bk", [P, C])
        bv = s.sb("bv", [P, H * DK])
        bo = s.sb("bo", [1, D])
        k_in = s.sb("k_in", [P, P])
        v_in = s.sb("v_in", [P, P])
        qT, kT = s.sb("qT", [P, C, P]), s.sb("kT", [P, C, P])
        v = s.sb("v", [P, H, DK])
        probs = s.sb("probs", [P, H, P])
        oT = s.sb("oT", [P, C, P])
        mx, nm, sums, inv = (s.sb(n, [P, H]) for n in ("mx", "nm", "sums", "inv"))
        score = [s.ps(f"score{i}", [P, BANK]) for i in range(4)]
        proj = [s.ps(f"proj{i}", [P, BANK]) for i in range(2)]
        y_ps = s.ps("y", [P, BANK])
        (w_in, kin_in, vin_in, s_mm, v_mm, q_mm, k_mm, av_mm, y_mm, nm_ready, probs_done, v_out, q_ready,
         k_ready, v_ready, o_ready, y_used, chain) = (s.sem(n) for n in (
             "w_in", "kin_in", "vin_in", "s_mm", "v_mm", "q_mm", "k_mm", "av_mm", "y_mm", "nm_ready",
             "probs_done", "v_out", "q_ready", "k_ready", "v_ready", "o_ready", "y_used", "chain"))

        def heads(g):
            half, odd = g // 2, g % 2
            return [(8 * half + 2 * i + odd, 4 * half + i, i, 64 * odd) for i in range(4)]

        loads = [(wq[:, :], k.d["L0_xattn_Wq"]), (wk[:, :], k.d["L0_xattn_Wk"]), (wv[:, :], k.d["L0_xattn_Wv"]),
                 (wo[:, :, :], k.d["L0_xattn_Wo"].rearrange("(c p) n -> p c n", p=P)),
                 (bq[:, :], k.d["L0_xattn_bq_cols"]), (bk[:, :], k.d["L0_xattn_bk_cols"]),
                 (bv[:, :], k.d["L0_xattn_bv"].partition_broadcast(P)),
                 (bo[:, :], k.d["L0_xattn_bo"].rearrange("(o n) -> o n", o=1))]
        with nc.Block() as block:
            zero_last_stage(block, k)

            @block.sync
            def _(sp):
                for dst, src in loads:
                    sp.dma_start(dst, src).then_inc(w_in, 16)
                with sp.Fori(0, NB) as b:
                    sp.wait_ge(k_mm, 2 * b)
                    sp.dma_start(k_in[:, :], k.d["ctxT"][ds(b, 1), :, :].rearrange("o p d -> (o p) d")
                                 ).then_inc(kin_in, 16)
                    sp.wait_ge(v_mm, 2 * b)
                    sp.dma_start(v_in[:, :], k.d["ctxT"][ds(b, 1), :, :].rearrange("o p d -> (o p) d")
                                 ).then_inc(vin_in, 16)
                sp.wait_ge(k_mm, 2 * NB)
                sp.dma_start(k_in[:, :], k.d["ctxT"][0, :, :]).then_inc(kin_in, 16)

            @block.tensor
            def _(pe):
                def project_q(n, first):
                    for half in range(2):
                        if not first:
                            pe.wait_ge(v_out, 2 * (n - 1) + half + 1)
                        for i in range(4):
                            c = 4 * half + i
                            ins = pe.matmul(proj[half][:, i * P:(i + 1) * P], wq[:, c * P:(c + 1) * P],
                                            k.cols[:, ds((n % NB) * P, P)], start=True, stop=True)
                        ins.then_inc(q_mm, 1)

                def project_k(n):
                    pe.wait_ge(kin_in, 16 * (n + 1))
                    for half in range(2):
                        pe.wait_ge(q_ready, 2 * n + half + 1)
                        for i in range(4):
                            c = 4 * half + i
                            ins = pe.matmul(proj[half][:, i * P:(i + 1) * P], wk[:, c * P:(c + 1) * P],
                                            k_in[:, :], start=True, stop=True)
                        ins.then_inc(k_mm, 1)

                pe.wait_ge(w_in, 16 * len(loads))
                project_q(0, True)
                project_k(0)
                with pe.Fori(0, NB) as b:
                    pe.wait_ge(q_ready, 2 * (b + 1))
                    pe.wait_ge(k_ready, 2 * (b + 1))
                    for g in range(4):
                        for h, c, i, p0 in heads(g):
                            ins = pe.matmul(score[g][:, i * P:(i + 1) * P], kT[p0:p0 + DK, c, :],
                                            qT[p0:p0 + DK, c, :], start=True, stop=True)
                        ins.then_inc(s_mm, 1)
                    pe.wait_ge(vin_in, 16 * (b + 1))
                    for half in range(2):
                        pe.matmul(proj[half][:, :], v_in[:, :], wv[:, half * BANK:(half + 1) * BANK],
                                  start=True, stop=True).then_inc(v_mm, 1)
                    project_q(b + 1, False)
                    project_k(b + 1)
                    pe.wait_ge(probs_done, H * (b + 1))
                    pe.wait_ge(v_ready, b + 1)
                    for half in range(2):
                        for i in range(4):
                            c = 4 * half + i
                            for odd in range(2):
                                ins = pe.matmul(score[half][64 * odd:64 * odd + DK, i * P:(i + 1) * P],
                                                v[:, 2 * c + odd, :], probs[:, 2 * c + odd, :], start=True, stop=True)
                        ins.then_inc(av_mm, 1)
                    pe.wait_ge(y_used, b)
                    pe.matmul(y_ps[:, 0:D], k.ones[0:1, :], bo[:, :], start=True, stop=False)
                    for c in range(C):
                        if c % 4 == 0:
                            pe.wait_ge(o_ready, 2 * b + c // 4 + 1)
                        ins = pe.matmul(y_ps[:, 0:D], oT[:, c, :], wo[:, c, :], start=False, stop=(c == C - 1))
                    ins.then_inc(y_mm, 1)

            @block.scalar
            def _(act):
                def evacuate_k(n):
                    for c in range(C):
                        if c % 4 == 0:
                            act.wait_ge(k_mm, 2 * n + c // 4 + 1)
                        ins = act.activation(kT[:, c, :], proj[c // 4][:, (c % 4) * P:(c % 4 + 1) * P],
                                             ACT.Identity, bias=bk[:, c:c + 1])
                        if c % 4 == 3:
                            ins.then_inc(k_ready, 1)

                act.wait_ge(w_in, 16 * len(loads))
                evacuate_k(0)
                with act.Fori(0, NB) as b:
                    act.wait_ge(av_mm, 2 * b)
                    for g in range(4):
                        act.wait_ge(nm_ready, 4 * b + g + 1)
                        for h, c, i, p0 in heads(g):
                            act.activation(probs[:, h, :], score[g][:, i * P:(i + 1) * P], ACT.Exp,
                                           bias=nm[:, h:h + 1], scale=SC, accum_out=sums[:, h:h + 1]
                                           ).then_inc(probs_done, 1)
                    evacuate_k(b + 1)
                    for half in range(2):
                        act.wait_ge(av_mm, 2 * b + half + 1)
                        act.activation(oT[:, 4 * half:4 * half + 4, :],
                                       score[half][:, :].rearrange("p (c n) -> p c n", c=4), ACT.Copy
                                       ).then_inc(o_ready, 1)

            @block.vector
            def _(dve):
                def evacuate_q(n):
                    for half in range(2):
                        dve.wait_ge(q_mm, 2 * n + half + 1)
                        dve.tensor_tensor(qT[:, 4 * half:4 * half + 4, :],
                                          proj[half][:, :].rearrange("p (c n) -> p c n", c=4),
                                          per_row(bq[:, 4 * half:4 * half + 4], P), ALU.add).then_inc(q_ready, 1)

                dve.wait_ge(w_in, 16 * len(loads))
                evacuate_q(0)
                STEPS = 5
                with dve.Fori(0, NB) as b:
                    link = Chain(dve, chain, b * STEPS)
                    for g in range(4):
                        first = 8 * (g // 2) + g % 2
                        dve.wait_ge(s_mm, 4 * b + g + 1)
                        link(dve.tensor_reduce(mx[:, first:first + 7:2],
                                               score[g][:, :].rearrange("p (h n) -> p h n", h=4), AX.X, ALU.max))
                        dve.tensor_scalar(nm[:, first:first + 7:2], mx[:, first:first + 7:2], -SC, None, ALU.mult
                                          ).then_inc(nm_ready, 1)
                    for half in range(2):
                        dve.wait_ge(v_mm, 2 * b + half + 1)
                        dve.tensor_tensor(v[:, 8 * half:8 * half + 8, :],
                                          proj[half][:, :].rearrange("p (h n) -> p h n", h=8),
                                          bv[:, half * BANK:(half + 1) * BANK].rearrange("p (h n) -> p h n", h=8),
                                          ALU.add).then_inc(v_out, 1)
                    evacuate_q(b + 1)
                    dve.wait_ge(probs_done, H * (b + 1))
                    link(dve.reciprocal(inv[:, :], sums[:, :]))
                    dve.wait_ge(v_out, 2 * (b + 1))
                    dve.tensor_tensor(v[:, :, :], v[:, :, :], per_row(inv[:, :], DK), ALU.mult).then_inc(v_ready, 1)
                    dve.wait_ge(y_mm, b + 1)
                    xt = k.x[:, ds(b, 1), :].rearrange("p o d -> p (o d)")
                    dve.scalar_tensor_tensor(out=xt, in0=y_ps[:, 0:D], scalar=k.tg[:, 0:1], in1=xt,
                                             op0=ALU.mult, op1=ALU.add).then_inc(y_used, 1)
                    link.steps(STEPS)


def top_two(link, dve, k, p, rest, eq, first, best, sel):
    for i, src in enumerate((p, rest)):
        link(dve.tensor_reduce(best[i][:, :], src[:, :, :], AX.X, ALU.max))
        link(dve.tensor_tensor(eq[:, :, :], src[:, :, :], per_row(best[i][:, :], E), ALU.is_equal))
        link(dve.tensor_tensor(eq[:, :, :], eq[:, :, :], per_group(k.rank[:, :], NB), ALU.mult))
        link(dve.tensor_reduce(first[:, :], eq[:, :, :], AX.X, ALU.max))
        link(dve.tensor_tensor(sel[i][:, :, :], eq[:, :, :], per_row(first[:, :], E), ALU.is_equal))
        if i == 0:
            link(dve.scalar_tensor_tensor(out=rest[:, :, :], in0=sel[0][:, :, :], scalar=-1e9, in1=p[:, :, :],
                                          op0=ALU.mult, op1=ALU.add))


def l0_route(nc, k):
    with ExitStack() as ctx:
        s = Space(nc, ctx, "l0r", k)
        p, work, eq, mask = (s.sb(n, [P, NB, E]) for n in ("p", "work", "eq", "mask"))
        sel = [s.sb(f"sel{i}", [P, NB, E]) for i in range(2)]
        best = [s.sb(f"best{i}", [P, NB]) for i in range(2)]
        red = s.sb("red", [P, NB])
        turned_ps = [s.ps(f"turned{i}", [P, BANK]) for i in range(8)]
        chain, shifted, exped, mask_ready, turned = (s.sem(n) for n in (
            "chain", "shifted", "exped", "mask_ready", "turned"))
        with nc.Block() as block:
            zero_last_stage(block, k)

            @block.vector
            def _(dve):
                link = Chain(dve, chain)
                link(dve.tensor_reduce(red[:, :], k.logits[:, :, :], AX.X, ALU.max))
                dve.tensor_tensor(p[:, :, :], k.logits[:, :, :], per_row(red[:, :], E), ALU.subtract).then_inc(shifted, 1)
                dve.wait_ge(exped, 1)
                link(dve.tensor_reduce(red[:, :], p[:, :, :], AX.X, ALU.add))
                link(dve.reciprocal(red[:, :], red[:, :]))
                link(dve.tensor_tensor(p[:, :, :], p[:, :, :], per_row(red[:, :], E), ALU.mult))
                top_two(link, dve, k, p, work, eq, red, best, sel)
                link(dve.tensor_tensor(mask[:, :, :], sel[0][:, :, :], sel[1][:, :, :], ALU.add))
                dve.tensor_tensor(k.weight[:, :, :], p[:, :, :], mask[:, :, :], ALU.mult).then_inc(mask_ready, 1)
                dve.wait_ge(mask_ready, 1)
                for g in range(NG):
                    dve.wait_ge(turned, g + 1)
                    ins = dve.tensor_copy(k.mask_rows[:, g * BANK:(g + 1) * BANK], turned_ps[g][0:E, :])
                ins.then_inc(mask_ready, 1)
                dve.wait_ge(mask_ready, 2)

            @block.scalar
            def _(act):
                act.wait_ge(shifted, 1)
                act.activation(p[:, :, :], p[:, :, :], ACT.Exp).then_inc(exped, 1)

            @block.tensor
            def _(pe):
                pe.wait_ge(mask_ready, 1)
                for g in range(NG):
                    for j in range(G4):
                        ins = pe.transpose(turned_ps[g][0:E, j * P:(j + 1) * P], mask[:, g * G4 + j, :], k.ident[:, :])
                    ins.then_inc(turned, 1)


def l0_mixture(nc, k):
    SH = 2
    HU = SH + E
    with ExitStack() as ctx:
        s = Space(nc, ctx, "l0f", k)
        w1, w2, w3 = (s.sb(n, [P, E, P]) for n in ("w1", "w2", "w3"))
        sw1, sw2, sw3 = (s.sb(n, [P, SH, P]) for n in ("sw1", "sw2", "sw3"))
        b1, b2, b3 = (s.sb(n, [P, E]) for n in ("b1", "b2", "b3"))
        picker = s.sb("picker", [E, E, P], BF16)
        xs = [s.sb(f"xs{i}", [P, G4, D]) for i in range(2)]
        xsT = [s.sb(f"xsT{i}", [P, BANK]) for i in range(2)]
        hidden, x3, z, acc = (s.sb(n, [P, BANK]) for n in ("hidden", "x3", "z", "acc"))
        s_gate = s.sb("s_gate", [P, SH, BANK])
        s_hidden = s.sb("s_hidden", [P, SH, BANK])
        xsT_ps, h_ps, x3_ps, x2_ps, m_ps, y_ps = (s.ps(n, [P, BANK]) for n in (
            "xsT", "h", "x3", "x2", "m", "y"))
        (w_in, picker_filled, picker_made, xs_ready, xsT_mm, h_mm, x3_mm, x2_mm, m_mm, y_mm, silu_done,
         xsT_ready, x3_ready, shared_ready, x2_out, masked, summed, y_used) = (s.sem(n) for n in (
             "w_in", "picker_filled", "picker_made", "xs_ready", "xsT_mm", "h_mm", "x3_mm", "x2_mm", "m_mm",
             "y_mm", "silu_done", "xsT_ready", "x3_ready", "shared_ready", "x2_out", "masked", "summed",
             "y_used"))
        loads = [(w1[:, :, :], k.d["L0_w1T"]), (w2[:, :, :], k.d["L0_w2T"]), (w3[:, :, :], k.d["L0_w3T"]),
                 (sw1[:, :, :], k.d["L0_sw1T"]), (sw2[:, :, :], k.d["L0_sw2T"]), (sw3[:, :, :], k.d["L0_sw3T"]),
                 (b1[:, :], k.d["L0_b1T"]), (b2[:, :], k.d["L0_b2T"]), (b3[:, :], k.d["L0_b3T"])]
        with nc.Block() as block:
            zero_last_stage(block, k)

            @block.sync
            def _(sp):
                for dst, src in loads:
                    sp.dma_start(dst, src).then_inc(w_in, 16)

            @block.gpsimd
            def _(pool):
                pool.memset(picker[:, :, :], 1.0).then_inc(picker_filled, 1)
                pool.wait_ge(picker_filled, 1)
                pool.affine_select(out=picker[:, :, :], in_=picker[:, :, :], compare_op=ALU.is_equal, fill=0.0,
                                   base=0, pattern=[[-1, E], [0, P]], channel_multiplier=1).then_inc(picker_made, 1)
                with pool.Fori(0, NG) as g:
                    for e in range(E):
                        pool.wait_ge(xsT_mm, g * E + max(e - 1, 0))
                        pool.tensor_tensor(xs[e % 2][:, :, :], k.rows[:, ds(g * G4, G4), :],
                                           k.weight[:, ds(g * G4, G4), e:e + 1].to_broadcast([P, G4, D]), ALU.mult
                                           ).then_inc(xs_ready, 1)

            @block.tensor
            def _(pe):
                pe.wait_ge(w_in, 16 * len(loads))
                pe.wait_ge(picker_made, 1)
                with pe.Fori(0, NG) as g:
                    cols = k.cols[:, ds(g * BANK, BANK)]

                    def turn(e):
                        pe.wait_ge(xs_ready, g * E + e + 1)
                        pe.wait_ge(xsT_ready, g * E + e)
                        for j in range(G4):
                            ins = pe.transpose(xsT_ps[:, j * P:(j + 1) * P], xs[e % 2][:, j, :], k.ident[:, :])
                        ins.then_inc(xsT_mm, 1)

                    for c in range(SH):
                        pe.wait_ge(silu_done, g * HU + c)
                        pe.matmul(h_ps[:, :], sw1[:, c, :], cols, start=True, stop=True).then_inc(h_mm, 1)
                        if c == 0:
                            pe.wait_ge(x3_ready, g * E)
                        else:
                            pe.wait_ge(shared_ready, g * SH + c)
                        pe.matmul(x3_ps[:, :], sw2[:, c, :], cols, start=True, stop=True).then_inc(x3_mm, 1)
                    turn(0)
                    pe.wait_ge(x2_out, g * (E + 1))
                    for c in range(SH):
                        pe.wait_ge(shared_ready, g * SH + c + 1)
                        ins = pe.matmul(x2_ps[:, :], sw3[:, c, :], s_hidden[:, c, :], start=(c == 0), stop=(c == SH - 1))
                    ins.then_inc(x2_mm, 1)
                    for e in range(E):
                        pe.wait_ge(xsT_ready, g * E + e + 1)
                        pe.wait_ge(silu_done, g * HU + SH + e)
                        pe.matmul(h_ps[:, :], w1[:, e, :], xsT[e % 2][:, :], start=True, stop=True).then_inc(h_mm, 1)
                        if e + 1 < E:
                            turn(e + 1)
                        pe.wait_ge(x3_ready, g * E + e)
                        pe.matmul(x3_ps[:, :], w3[:, e, :], xsT[e % 2][:, :], start=True, stop=True).then_inc(x3_mm, 1)
                        pe.wait_ge(masked, g * E + e)
                        wait_apart(pe, k.waited_pe)
                        pe.matmul(m_ps[:, :], picker[:, e, :], k.mask_rows[:, ds(g * BANK, BANK)],
                                  start=True, stop=True).then_inc(m_mm, 1)
                        pe.wait_ge(silu_done, g * HU + SH + e + 1)
                        pe.wait_ge(x2_out, g * (E + 1) + e + 1)
                        pe.matmul(x2_ps[:, :], w2[:, e, :], hidden[:, :], start=True, stop=True).then_inc(x2_mm, 1)
                    pe.wait_ge(summed, (g + 1) * (E + 1))
                    pe.wait_ge(y_used, g)
                    for j in range(G4):
                        ins = pe.transpose(y_ps[:, j * P:(j + 1) * P], acc[:, j * P:(j + 1) * P], k.ident[:, :])
                    ins.then_inc(y_mm, 1)

            @block.scalar
            def _(act):
                act.wait_ge(w_in, 16 * len(loads))
                with act.Fori(0, NG) as g:
                    def evacuate_xs(e):
                        act.wait_ge(xsT_mm, g * E + e + 1)
                        act.wait_ge(x3_mm, g * HU + (SH + e - 1 if e >= 2 else 0))
                        act.activation(xsT[e % 2][:, :], xsT_ps[:, :], ACT.Copy).then_inc(xsT_ready, 1)

                    for c in range(SH):
                        act.wait_ge(h_mm, g * HU + c + 1)
                        act.activation(s_gate[:, c, :], h_ps[:, :], ACT.Silu).then_inc(silu_done, 1)
                    evacuate_xs(0)
                    for e in range(E):
                        act.wait_ge(h_mm, g * HU + SH + e + 1)
                        act.activation(hidden[:, :], h_ps[:, :], ACT.Silu, bias=b1[:, e:e + 1]).then_inc(silu_done, 1)
                        if e + 1 < E:
                            evacuate_xs(e + 1)
                        act.wait_ge(x3_mm, g * HU + SH + e + 1)
                        act.wait_ge(x2_out, g * (E + 1) + e + 1)
                        act.activation(x3[:, :], x3_ps[:, :], ACT.Identity, bias=b3[:, e:e + 1]).then_inc(x3_ready, 1)

            @block.vector
            def _(dve):
                dve.wait_ge(w_in, 16 * len(loads))
                with dve.Fori(0, NG) as g:
                    for c in range(SH):
                        dve.wait_ge(silu_done, g * HU + c + 1)
                        dve.wait_ge(x3_mm, g * HU + c + 1)
                        dve.tensor_tensor(s_hidden[:, c, :], x3_ps[:, :], s_gate[:, c, :], ALU.mult
                                          ).then_inc(shared_ready, 1)
                    dve.wait_ge(x2_mm, g * (E + 1) + 1)
                    dve.wait_ge(y_mm, g)
                    dve.tensor_copy(acc[:, :], x2_ps[:, :]).then_inc(x2_out, 1)
                    dve.wait_ge(x2_out, g * (E + 1) + 1)
                    dve.sem_inc(summed, 1)
                    for e in range(E):
                        dve.wait_ge(x2_mm, g * (E + 1) + e + 2)
                        dve.wait_ge(x3_ready, g * E + e + 1)
                        dve.wait_ge(summed, g * (E + 1) + e + 1)
                        dve.scalar_tensor_tensor(out=z[:, :], in0=x2_ps[:, :], scalar=b2[:, e:e + 1], in1=x3[:, :],
                                                 op0=ALU.add, op1=ALU.mult).then_inc(x2_out, 1)
                        dve.wait_ge(m_mm, g * E + e + 1)
                        dve.wait_ge(x2_out, g * (E + 1) + e + 2)
                        dve.tensor_tensor(z[:, :], z[:, :], m_ps[:, :], ALU.mult).then_inc(masked, 1)
                        dve.wait_ge(masked, g * E + e + 1)
                        dve.tensor_tensor(acc[:, :], acc[:, :], z[:, :], ALU.add).then_inc(summed, 1)
                    dve.wait_ge(y_mm, g + 1)
                    xt = k.x[:, ds(g * G4, G4), :]
                    dve.scalar_tensor_tensor(out=xt, in0=y_ps[:, :].rearrange("p (t d) -> p t d", t=G4),
                                             scalar=k.tg[:, 4:5], in1=xt, op0=ALU.mult, op1=ALU.add
                                             ).then_inc(y_used, 1)



def l1_gates(nc, k):
    NH = 4
    with ExitStack() as ctx:
        s = Space(nc, ctx, "l1g", k)
        ctx_cols = s.sb("ctx_cols", [P, NB * P])
        w = s.sb("w", [P, 3, 2 * NH])
        bias = s.sb("bias", [2 * NH, 1])
        gates = s.sb("gates", [2 * NH, NB * P])
        ig, fg, size, low, cum, a, top, neg, em = (s.sb(n, [P, P]) for n in (
            "ig", "fg", "size", "low", "cum", "a", "top", "neg", "em"))
        ps = [s.ps(f"gate{i}", [P, BANK]) for i in range(8)]
        (loaded, gate_mm, gate_out, spread, chain, sized, softened, ready, turned, copied, neg_out) = (
            s.sem(n) for n in ("loaded", "gate_mm", "gate_out", "spread", "chain", "sized", "softened", "ready",
                               "turned", "copied", "neg_out"))
        with nc.Block() as block:
            zero_last_stage(block, k)

            @block.sync
            def _(sp):
                sp.dma_start(ctx_cols[:, :].rearrange("p (b s) -> p b s", b=NB),
                             k.d["ctxT"].rearrange("b p s -> p b s")).then_inc(loaded, 16)
                sp.dma_start(w[:, :, :], k.d["L1_gates"]).then_inc(loaded, 16)
                sp.dma_start(bias[:, :], k.d["L1_gate_bias"]).then_inc(loaded, 16)
                sp.wait_ge(gate_out, NG)
                for dst, h0 in ((ig, 0), (fg, NH)):
                    for h in range(NH):
                        sp.dma_start(dst[h:P:NH, :],
                                     gates[h0 + h:h0 + h + 1, :].rearrange("o (b s) -> o b s", b=NB)
                                     ).then_inc(spread, 16)
                sp.wait_ge(ready, 1)
                sp.dma_start(k.neg_top, neg[:, :]).then_inc(neg_out, 16)
                sp.wait_ge(neg_out, 16)

            @block.tensor
            def _(pe):
                pe.wait_ge(loaded, 48)
                for g in range(NG):
                    cols = slice(g * BANK, (g + 1) * BANK)
                    pe.matmul(ps[g][0:2 * NH, :], w[:, 0, :], k.cols[:, cols], start=True, stop=False)
                    pe.matmul(ps[g][0:2 * NH, :], w[:, 1, :], ctx_cols[:, cols], start=False, stop=False)
                    pe.matmul(ps[g][0:2 * NH, :], w[:, 2, :], ctx_cols[:, cols], start=False, stop=True
                              ).then_inc(gate_mm, 1)
                pe.wait_ge(ready, 1)
                pe.transpose(ps[0][:, 0:P], a[:, :], k.ident[:, :]).then_inc(turned, 1)
                pe.wait_ge(ready, 2)
                pe.transpose(ps[1][:, 0:P], em[:, :], k.ident[:, :]).then_inc(turned, 1)

            @block.scalar
            def _(act):
                act.wait_ge(sized, 1)
                act.activation(size[:, :], size[:, :], ACT.Exp, scale=-1.0).then_inc(softened, 1)
                act.wait_ge(softened, 1)
                act.activation(size[:, :], size[:, :], ACT.Ln, bias=1.0).then_inc(softened, 1)
                act.wait_ge(ready, 1)
                act.activation(em[:, :], top[:, :], ACT.Exp, scale=-1.0).then_inc(ready, 1)

            @block.vector
            def _(dve):
                dve.wait_ge(loaded, 48)
                for g in range(NG):
                    dve.wait_ge(gate_mm, g + 1)
                    dve.tensor_scalar(gates[:, g * BANK:(g + 1) * BANK], ps[g][0:2 * NH, :], bias[:, 0:1], None,
                                      ALU.add).then_inc(gate_out, 1)
                dve.wait_ge(spread, 16 * 2 * NH)
                link = Chain(dve, chain)
                link(dve.tensor_scalar(low[:, :], fg[:, :], 0.0, None, ALU.min))
                link(dve.tensor_scalar(size[:, :], fg[:, :], 0.0, None, ALU.max))
                dve.tensor_tensor(size[:, :], size[:, :], low[:, :], ALU.subtract).then_inc(sized, 1)
                dve.wait_ge(softened, 2)
                link(dve.tensor_tensor(low[:, :], low[:, :], size[:, :], ALU.subtract))
                link(dve.tensor_tensor_scan(cum[:, :], k.ones[:, :], low[:, :], 0.0, ALU.mult, ALU.add))
                link(dve.tensor_tensor(a[:, :], ig[:, :], cum[:, :], ALU.subtract))
                link(dve.tensor_tensor_scan(top[:, :], a[:, :], a[:, :], -3e38, ALU.max, ALU.max))
                link(dve.tensor_scalar(neg[:, :], top[:, :], -1.0, None, ALU.mult))
                dve.tensor_tensor(top[:, :], top[:, :], cum[:, :], ALU.add).then_inc(ready, 1)
                for i, dst in enumerate((k.aT, k.emT)):
                    dve.wait_ge(turned, i + 1)
                    dve.tensor_copy(dst[:, :], ps[i][:, 0:P]).then_inc(copied, 1)
                dve.wait_ge(copied, 2)


def l1_attention(nc, k):
    NH, HD = 4, 32
    with ExitStack() as ctx:
        s = Space(nc, ctx, "l1a", k)
        two = range(2)
        k_in = [s.sb(f"k_in{i}", [P, P]) for i in two]
        v_in = [s.sb(f"v_in{i}", [P, NH, HD + 1]) for i in two]
        v_raw = [s.sb(f"v_raw{i}", [P, D]) for i in two]
        m_in = [s.sb(f"m_in{i}", [1, NH * P]) for i in two]
        q_heads = [s.sb(f"q_heads{i}", [P, NH, P]) for i in two]
        head_scale = s.sb("head_scale", [P, NH])
        future = s.sb("future", [P, NH, P], BF16)
        ident16 = s.sb("ident16", [P, P], BF16)
        decay = [s.sb(f"decay{i}", [P, NH, P]) for i in two]
        c = [s.sb(f"c{i}", [P, NH, P]) for i in two]
        rms = s.sb("rms", [P, HD])
        out_scale = s.sb("out_scale", [P, NH, HD])
        den, inv, ss, rs = (s.sb(n, [P, NH]) for n in ("den", "inv", "ss", "rs"))
        hid, sq = s.sb("hid", [P, NH, HD]), s.sb("sq", [P, NH, HD])
        m_ps = s.ps("m", [P, BANK])
        s_ps = [s.ps(f"s{i}", [P, BANK]) for i in two]
        o_ps = [s.ps(f"o{i}", [P, BANK]) for i in two]
        k_loaded, v_loaded, m_loaded = ([s.sem(f"{n}_loaded{i}") for i in two] for n in "kvm")
        (w_in, filled, made, scale_made, q_ready, m_mm, s_mm, av_mm, e_ready, d_ready, c_ready, v_ready,
         n1_done, var_ready, rs_ready, chain) = (s.sem(n) for n in (
             "w_in", "filled", "made", "scale_made", "q_ready", "m_mm", "s_mm", "av_mm", "e_ready", "d_ready",
             "c_ready", "v_ready", "n1_done", "var_ready", "rs_ready", "chain"))

        def loads_by(n, i):
            return (n - i) * 8 + 16

        def schedule(eng, a_step, c_step, n1_step, n2_step):
            a_step(0, 0)
            a_step(1, 1)
            c_step(0, 0)
            with eng.Fori(0, NB // 2) as q:
                for u in two:
                    b = q * 2 + (u + 1)
                    n1_step(q * 2 + u, u)
                    a_step(q * 2 + (u + 2), u)
                    c_step(b, 1 - u)
                    n2_step(q * 2 + u, u)

        def before(n, m):
            return None if isinstance(n, int) and n - m < 1 else n - m

        def nothing(n, i):
            pass

        with nc.Block() as block:
            zero_last_stage(block, k)

            @block.sync
            def _(sp):
                sp.dma_start(rms[:, :], k.d["L1_xattn_rms_scale"].partition_broadcast(P)).then_inc(w_in, 16)

                def load(n, i):
                    if before(n, 1) is not None:
                        sp.wait_ge(s_mm, n - 1)
                        sp.wait_ge(v_ready, n - 1)
                        sp.wait_ge(m_mm, n - 1)
                    sp.dma_start(k_in[i][:, :], k.d["ctxT"][ds(n % NB, 1), :, :].rearrange("o p s -> (o p) s")
                                 ).then_inc(k_loaded[i], 16)
                    sp.dma_start(m_in[i][:, :], k.neg_top[ds((n % NB) * NH, NH), :].rearrange("(o h) s -> o (h s)", o=1)
                                 ).then_inc(m_loaded[i], 16)
                    sp.dma_start(v_raw[i][:, :], k.d["ctx"][ds(n % NB, 1), :, :].rearrange("o p d -> (o p) d")
                                 ).then_inc(v_loaded[i], 16)
                schedule(sp, load, nothing, nothing, nothing)

            @block.gpsimd
            def _(pool):
                for i in two:
                    pool.memset(v_in[i][:, :, :], 1.0).then_inc(filled, 1)
                pool.memset(head_scale[:, :], HD ** -0.5).then_inc(filled, 1)
                pool.memset(future[:, :, :], 0.0).then_inc(filled, 1)
                pool.tensor_copy(ident16[:, :], k.ident[:, :]).then_inc(filled, 1)
                pool.wait_ge(filled, 5)
                pool.affine_select(out=head_scale[:, :], in_=head_scale[:, :], compare_op=ALU.is_ge, fill=0.0,
                                   base=0, pattern=[[-HD, NH]], channel_multiplier=1).then_inc(made, 1)
                pool.wait_ge(made, 1)
                pool.affine_select(out=head_scale[:, :], in_=head_scale[:, :], compare_op=ALU.is_ge, fill=0.0,
                                   base=HD - 1, pattern=[[HD, NH]], channel_multiplier=-1).then_inc(made, 1)
                pool.affine_select(out=future[:, :, :], in_=future[:, :, :], compare_op=ALU.is_ge, fill=-1e30,
                                   base=0, pattern=[[0, NH], [1, P]], channel_multiplier=-1).then_inc(made, 1)
                pool.wait_ge(made, 3)

                def a_step(n, i):
                    if before(n, 1) is not None:
                        pool.wait_ge(s_mm, n - 1)
                        pool.wait_ge(av_mm, n - 1)
                    pool.tensor_tensor(q_heads[i][:, :, :],
                                       per_group(k.cols[:, ds((n % NB) * P, P)], NH),
                                       per_row(head_scale[:, :], P), ALU.mult).then_inc(q_ready, 1)
                    pool.wait_ge(v_loaded[i], loads_by(n, i))
                    wait_apart(pool, k.waited_pool)
                    pool.tensor_copy(v_in[i][:, :, 0:HD], v_raw[i][:, :].rearrange("p (h d) -> p h d", h=NH)
                                     ).then_inc(v_ready, 1)

                def n1_step(n, i):
                    pool.wait_ge(var_ready, n + 1)
                    pool.tensor_tensor(rs[:, :], ss[:, :], k.neg_half[:, 0:NH], ALU.pow).then_inc(rs_ready, 1)
                schedule(pool, a_step, nothing, n1_step, nothing)

            @block.tensor
            def _(pe):
                pe.wait_ge(made, 3)

                def a_step(n, i):
                    pe.wait_ge(m_loaded[i], loads_by(n, i))
                    pe.wait_ge(e_ready, n)
                    pe.matmul(m_ps[:, :], k.ones[0:1, :], m_in[i][:, :], start=True, stop=False)
                    pe.matmul(m_ps[:, :], ident16[:, :], future[:, :, :].rearrange("p h s -> p (h s)"),
                              start=False, stop=True).then_inc(m_mm, 1)
                    pe.wait_ge(k_loaded[i], loads_by(n, i))
                    pe.wait_ge(q_ready, n + 1)
                    if before(n, 1) is not None:
                        pe.wait_ge(c_ready, n - 1)
                    pe.matmul(s_ps[i][:, :], k_in[i][:, :], q_heads[i][:, :, :].rearrange("p h s -> p (h s)"),
                              start=True, stop=True).then_inc(s_mm, 1)

                def c_step(n, i):
                    pe.wait_ge(c_ready, n + 1)
                    pe.wait_ge(v_ready, n + 1)
                    if before(n, 1) is not None:
                        pe.wait_ge(n1_done, n - 1)
                    for h in range(NH):
                        ins = pe.matmul(o_ps[i][:, h * (HD + 1):(h + 1) * (HD + 1)], c[i][:, h, :], v_in[i][:, h, :],
                                        start=True, stop=True)
                    ins.then_inc(av_mm, 1)
                schedule(pe, a_step, c_step, nothing, nothing)

            @block.scalar
            def _(act):
                def a_step(n, i):
                    act.wait_ge(e_ready, n + 1)
                    act.activation(decay[i][:, :, :], decay[i][:, :, :], ACT.Exp).then_inc(d_ready, 1)
                schedule(act, a_step, nothing, nothing, nothing)

            @block.vector
            def _(dve):
                dve.wait_ge(w_in, 16)
                dve.tensor_scalar(out_scale[:, 0, :], rms[:, :], 1.0, k.tg[:, 1:2], ALU.add, ALU.mult
                                  ).then_inc(scale_made, 1)
                dve.wait_ge(scale_made, 1)
                for h in range(1, NH):
                    dve.tensor_copy(out_scale[:, h, :], out_scale[:, 0, :]).then_inc(scale_made, 1)
                dve.wait_ge(scale_made, NH)
                STEPS = 8

                def a_step(n, i):
                    dve.wait_ge(m_mm, n + 1)
                    dve.tensor_tensor(decay[i][:, :, :], m_ps[:, :].rearrange("p (h s) -> p h s", h=NH),
                                      per_row(k.aT[:, ds((n % NB) * NH, NH)], P), ALU.add).then_inc(e_ready, 1)

                def c_step(n, i):
                    dve.wait_ge(d_ready, n + 1)
                    dve.wait_ge(s_mm, n + 1)
                    if before(n, 1) is not None:
                        dve.wait_ge(av_mm, n - 1)
                    dve.tensor_tensor(c[i][:, :, :], s_ps[i][:, :].rearrange("p (h s) -> p h s", h=NH),
                                      decay[i][:, :, :], ALU.mult).then_inc(c_ready, 1)

                def n1_step(n, i):
                    link = Chain(dve, chain, n * STEPS)
                    o = o_ps[i][:, 0:NH * (HD + 1)].rearrange("p (h d) -> p h d", h=NH)
                    dve.wait_ge(av_mm, n + 1)
                    link(dve.tensor_tensor(den[:, :], o[:, :, HD:HD + 1].rearrange("p h o -> p (h o)"),
                                           k.emT[:, ds(n * NH, NH)], ALU.max))
                    link(dve.tensor_scalar(den[:, :], den[:, :], 1e-6, None, ALU.add))
                    link(dve.reciprocal(inv[:, :], den[:, :]))
                    dve.tensor_tensor(hid[:, :, :], o[:, :, 0:HD], per_row(inv[:, :], HD), ALU.mult
                                      ).then_inc(n1_done, 1)
                    dve.wait_ge(n1_done, n + 1)
                    link(dve.tensor_tensor(sq[:, :, :], hid[:, :, :], hid[:, :, :], ALU.mult))
                    link(dve.tensor_reduce(ss[:, :], sq[:, :, :], AX.X, ALU.add))
                    dve.tensor_scalar(ss[:, :], ss[:, :], 1.0 / HD, 1e-6, ALU.mult, ALU.add).then_inc(var_ready, 1)
                    link(dve.tensor_tensor(hid[:, :, :], hid[:, :, :], out_scale[:, :, :], ALU.mult))

                def n2_step(n, i):
                    link = Chain(dve, chain, n * STEPS + 6)
                    dve.wait_ge(rs_ready, n + 1)
                    link(dve.tensor_tensor(hid[:, :, :], hid[:, :, :], per_row(rs[:, :], HD), ALU.mult))
                    xt = k.x[:, ds(n, 1), :].rearrange("p o d -> p (o d)")
                    link(dve.tensor_tensor(xt, xt, hid[:, :, :].rearrange("p h d -> p (h d)"), ALU.add))
                schedule(dve, a_step, c_step, n1_step, n2_step)


def l1_route(nc, k):
    with ExitStack() as ctx:
        s = Space(nc, ctx, "l1r", k)
        p, rest, eq, mask = (s.sb(n, [P, NB, E]) for n in ("p", "rest", "eq", "mask"))
        sel = [s.sb(f"sel{i}", [P, NB, E]) for i in range(2)]
        best = [s.sb(f"best{i}", [P, NB]) for i in range(2)]
        red = s.sb("red", [P, NB])
        lb = s.sb("lb", [P, E])
        part = s.sb("part", [P, 2, E])
        total = s.sb("total", [P, 2, E])
        turned_ps = [s.ps(f"turned{i}", [P, BANK]) for i in range(6)]
        sum_ps = s.ps("sum", [P, BANK])
        w_in, chain, biased, squashed, mask_ready, part_ready, turned, summed, used = (s.sem(n) for n in (
            "w_in", "chain", "biased", "squashed", "mask_ready", "part_ready", "turned", "summed", "used"))
        with nc.Block() as block:
            zero_last_stage(block, k)

            @block.sync
            def _(sp):
                sp.dma_start(lb[:, :], k.d["L1_ffn_lb_bias"].partition_broadcast(P)).then_inc(w_in, 16)

            @block.scalar
            def _(act):
                act.wait_ge(biased, 1)
                act.activation(p[:, :, :], p[:, :, :], ACT.Sigmoid).then_inc(squashed, 1)

            @block.vector
            def _(dve):
                link = Chain(dve, chain)
                dve.wait_ge(w_in, 16)
                dve.tensor_tensor(p[:, :, :], k.logits[:, :, :], per_group(lb[:, :], NB), ALU.add).then_inc(biased, 1)
                dve.wait_ge(squashed, 1)
                top_two(link, dve, k, p, rest, eq, red, best, sel)
                link(dve.tensor_tensor(mask[:, :, :], sel[0][:, :, :], sel[1][:, :, :], ALU.add))
                link(dve.tensor_tensor(red[:, :], best[0][:, :], best[1][:, :], ALU.add))
                link(dve.tensor_scalar(red[:, :], red[:, :], 1e-8, None, ALU.add))
                link(dve.reciprocal(red[:, :], red[:, :]))
                link(dve.tensor_tensor(p[:, :, :], p[:, :, :], mask[:, :, :], ALU.mult))
                link(dve.tensor_tensor(p[:, :, :], p[:, :, :], per_row(red[:, :], E), ALU.mult))
                link(dve.tensor_reduce(part[:, 0, :], p[:, :, :].rearrange("p t e -> p e t"), AX.X, ALU.add))
                link(dve.tensor_reduce(part[:, 1, :], mask[:, :, :].rearrange("p t e -> p e t"), AX.X, ALU.add))
                dve.sem_inc(part_ready, 1)
                dve.sem_inc(mask_ready, 1)
                dve.wait_ge(summed, 1)
                link(dve.tensor_copy(total[:, :, :], sum_ps[:, 0:2 * E].rearrange("p (a e) -> p a e", a=2)))
                link(dve.tensor_scalar(total[:, 1, :], total[:, 1, :], 1.0, None, ALU.max))
                link(dve.reciprocal(total[:, 1, :], total[:, 1, :]))
                link(dve.tensor_tensor(k.expert_weight[:, :], total[:, 0, :], total[:, 1, :], ALU.mult))
                for g in range(NG):
                    dve.wait_ge(turned, g + 1)
                    dve.tensor_copy(k.mask_rows[:, g * BANK:(g + 1) * BANK], turned_ps[g % 6][0:E, :]
                                    ).then_inc(used, 1)
                dve.wait_ge(used, NG)

            @block.tensor
            def _(pe):
                pe.wait_ge(part_ready, 1)
                pe.matmul(sum_ps[:, 0:2 * E], k.ones[:, :], part[:, :, :].rearrange("p a e -> p (a e)"),
                          start=True, stop=True).then_inc(summed, 1)
                for g in range(NG):
                    if g >= 6:
                        pe.wait_ge(used, g - 5)
                    for j in range(G4):
                        ins = pe.transpose(turned_ps[g % 6][0:E, j * P:(j + 1) * P], mask[:, g * G4 + j, :], k.ident[:, :])
                    ins.then_inc(turned, 1)


def l1_mixture(nc, k):
    NC = E // 2 + 1
    with ExitStack() as ctx:
        s = Space(nc, ctx, "l1f", k)
        w_gate, w_up, w_down = (s.sb(n, [P, NC, P]) for n in ("w_gate", "w_up", "w_down"))
        pair = s.sb("pair", [E, E // 2, 2, P // 2], BF16)
        gate = [s.sb(f"gate{i}", [P, BANK]) for i in range(2)]
        prod = [s.sb(f"prod{i}", [P, BANK]) for i in range(2)]
        hidden = s.sb("hidden", [P, NC, BANK])
        g_ps, u_ps, m_ps, y_ps = ([s.ps(f"{n}{i}", [P, BANK]) for i in range(2)] for n in ("g", "u", "m", "y"))
        (w_in, filled, made, scaled, g_mm, u_mm, m_mm, y_mm, silu_done, multiplied, masked, y_used) = (
            s.sem(n) for n in ("w_in", "filled", "made", "scaled", "g_mm", "u_mm", "m_mm", "y_mm", "silu_done",
                               "multiplied", "masked", "y_used"))
        loads = [(w_gate[:, :, :], k.d["L1_gateT"]), (w_up[:, :, :], k.d["L1_upT"]), (w_down[:, :, :], k.d["L1_downT"])]
        with nc.Block() as block:
            zero_last_stage(block, k)

            @block.sync
            def _(sp):
                for dst, src in loads:
                    sp.dma_start(dst, src).then_inc(w_in, 16)

            @block.gpsimd
            def _(pool):
                pool.memset(pair[:, :, :, :], 1.0).then_inc(filled, 1)
                pool.wait_ge(filled, 1)
                pool.affine_select(out=pair[:, :, :, :], in_=pair[:, :, :, :], compare_op=ALU.is_equal, fill=0.0,
                                   base=0, pattern=[[-2, E // 2], [-1, 2], [0, P // 2]], channel_multiplier=1
                                   ).then_inc(made, 1)

            @block.tensor
            def _(pe):
                pe.wait_ge(w_in, 16 * len(loads))
                pe.wait_ge(made, 1)
                pe.wait_ge(scaled, E)
                with pe.Fori(0, NG // 2) as q:
                    for u in range(2):
                        g = q * 2 + u
                        cols = k.cols[:, ds(g * BANK, BANK)]
                        for c in range(NC):
                            i = (u * NC + c) % 2
                            n = g * NC + c
                            first = u == 0 and c < 2
                            pe.wait_ge(silu_done, q * 2 * NC if first else n - 1)
                            pe.wait_ge(multiplied, q * 2 * NC if first else n - 1)
                            pe.matmul(g_ps[i][:, :], w_gate[:, c, :], cols, start=True, stop=True).then_inc(g_mm, 1)
                            pe.matmul(u_ps[i][:, :], w_up[:, c, :], cols, start=True, stop=True).then_inc(u_mm, 1)
                            if c < NC - 1:
                                pe.wait_ge(masked, g * (NC - 1) + max(c - 1, 0))
                                wait_apart(pe, k.waited_pe)
                                pe.matmul(m_ps[c % 2][:, :], pair[:, c, :, :].rearrange("p i n -> p (i n)"),
                                          k.mask_rows[:, ds(g * BANK, BANK)], start=True, stop=True).then_inc(m_mm, 1)
                        pe.wait_ge(masked, (g + 1) * (NC - 1))
                        pe.wait_ge(multiplied, (g + 1) * NC)
                        pe.wait_ge(y_used, q * 2)
                        for j in range(G4):
                            for c in range(NC):
                                ins = pe.matmul(y_ps[u][:, j * D:(j + 1) * D], hidden[:, c, j * P:(j + 1) * P],
                                                w_down[:, c, :], start=(c == 0), stop=(c == NC - 1))
                        ins.then_inc(y_mm, 1)

            @block.scalar
            def _(act):
                with act.Fori(0, NG // 2) as q:
                    for u in range(2):
                        for c in range(NC):
                            i = (u * NC + c) % 2
                            n = (q * 2 + u) * NC + c
                            first = u == 0 and c < 2
                            act.wait_ge(g_mm, n + 1)
                            act.wait_ge(multiplied, q * 2 * NC if first else n - 1)
                            act.activation(gate[i][:, :], g_ps[i][:, :], ACT.Silu).then_inc(silu_done, 1)

            @block.vector
            def _(dve):
                dve.wait_ge(w_in, 16 * len(loads))
                for e in range(E):
                    rows = slice(64 * (e % 2), 64 * (e % 2) + 64)
                    dve.tensor_scalar(w_down[rows, e // 2, :], w_down[rows, e // 2, :],
                                      k.expert_weight[rows, e:e + 1], None, ALU.mult).then_inc(scaled, 1)
                with dve.Fori(0, NG // 2) as q:
                    for u in range(2):
                        g = q * 2 + u
                        for c in range(NC):
                            i = (u * NC + c) % 2
                            n = g * NC + c
                            if c == 0:
                                dve.wait_ge(y_mm, g)
                            dve.wait_ge(silu_done, n + 1)
                            dve.wait_ge(u_mm, n + 1)
                            if c < NC - 1:
                                dve.wait_ge(masked, g * (NC - 1) + max(c - 1, 0))
                            dve.tensor_tensor(prod[c % 2][:, :] if c < NC - 1 else hidden[:, c, :], u_ps[i][:, :], gate[i][:, :],
                                              ALU.mult).then_inc(multiplied, 1)
                            if c < NC - 1:
                                dve.wait_ge(m_mm, g * (NC - 1) + c + 1)
                                dve.wait_ge(multiplied, n + 1)
                                dve.tensor_tensor(hidden[:, c, :], prod[c % 2][:, :], m_ps[c % 2][:, :], ALU.mult
                                                  ).then_inc(masked, 1)
                        dve.wait_ge(y_mm, g + 1)
                        xt = k.x[:, ds(g * G4, G4), :]
                        dve.scalar_tensor_tensor(out=xt, in0=y_ps[u][:, :].rearrange("p (t d) -> p t d", t=G4),
                                                 scalar=k.tg[:, 5:6], in1=xt, op0=ALU.mult, op1=ALU.add
                                                 ).then_inc(y_used, 1)


def l2_fold(nc, k):
    H, DK = 16, 64
    with ExitStack() as ctx:
        s = Space(nc, ctx, "l2w", k)
        w = [s.sb(n, [P, H // 2, P]) for n in ("wqT", "wkT", "wvT", "wout")]
        ps = [s.ps(f"fold{i}", [P, BANK]) for i in range(8)]
        w_in, folded, copied = (s.sem(n) for n in ("w_in", "folded", "copied"))
        with nc.Block() as block:
            zero_last_stage(block, k)

            @block.sync
            def _(sp):
                for t, n in zip(w, ("L2_WqT", "L2_WkT", "L2_WvT", "L2_Wout")):
                    sp.dma_start(t[:, :, :], k.d[n]).then_inc(w_in, 16)

            @block.tensor
            def _(pe):
                pe.wait_ge(w_in, 64)
                for n in range(8):
                    left, right = (w[0], w[1]) if n < 4 else (w[2], w[3])
                    for i in range(4):
                        h = 8 * (n % 4 // 2) + 2 * i + n % 2
                        rows = slice(DK * (h % 2), DK * (h % 2) + DK)
                        ins = pe.matmul(ps[n][:, i * P:(i + 1) * P], left[rows, h // 2, :], right[rows, h // 2, :],
                                        start=True, stop=True)
                    ins.then_inc(folded, 1)

            @block.vector
            def _(dve):
                for n in range(8):
                    dst = k.qk_w if n < 4 else k.vo_w
                    dve.wait_ge(folded, n + 1)
                    first = 8 * (n % 4 // 2) + n % 2
                    dve.tensor_copy(dst[:, first:first + 7:2, :],
                                    ps[n][:, :].rearrange("p (h c) -> p h c", h=4)).then_inc(copied, 1)
                dve.wait_ge(copied, 8)


def l2_attention(nc, k):
    H, Q4, KV = 16, 4, 2 * P
    SC = 64.0 ** -0.5
    BODY = 8
    with ExitStack() as ctx:
        s = Space(nc, ctx, "l2a", k)
        kvT = [s.sb(f"kvT{i}", [P, KV]) for i in range(2)]
        kv = [s.sb(f"kv{i}", [P, 2, D]) for i in range(2)]
        tT = [s.sb(f"tT{i}", [P, Q4, P]) for i in range(2)]
        probs = [s.sb(f"probs{i}", [P, Q4, KV]) for i in range(4)]
        pT = [s.sb(f"pT{i}", [P, 2, Q4, P]) for i in range(2)]
        uT = [s.sb(f"uT{i}", [P, Q4, P]) for i in range(2)]
        mx, nm, sums, inv = ([s.sb(f"{n}{i}", [P, Q4]) for i in range(4)] for n in ("mx", "nm", "sums", "inv"))
        t_ps, u_ps, y_ps, kv_ps = (s.ps(n, [P, BANK]) for n in ("t", "u", "y", "kvn"))
        s_ps = [s.ps(f"s{i}", [P, BANK]) for i in range(2)]
        p_ps = [s.ps(f"p{i}", [P, BANK]) for i in range(2)]
        (kvT_ready, kv_mm, kv_ready, t_mm, t_ready, s_mm, maxed, nm_ready, probs_done, inv_ready, scaled, x_mm,
         p0_ready, p1_ready, u_mm, u_ready, o_mm, y_used) = (s.sem(n) for n in (
             "kvT_ready", "kv_mm", "kv_ready", "t_mm", "t_ready", "s_mm", "maxed", "nm_ready", "probs_done",
             "inv_ready", "scaled", "x_mm", "p0_ready", "p1_ready", "u_mm", "u_ready", "o_mm", "y_used"))

        def wait(eng, sem, q, value_per_q, value):
            if not isinstance(q, int):
                eng.wait_ge(sem, q * value_per_q + value)
            elif q * value_per_q + value >= 1:
                eng.wait_ge(sem, q * value_per_q + value)

        def schedule(eng, steps):
            for c in range(-1, 4):
                for step, behind in steps:
                    if c - behind >= 0:
                        step(0, c - behind)
            with eng.Fori(0, NB * H // Q4 // BODY) as q:
                for c in range(4, 4 + BODY):
                    for step, behind in steps:
                        step(q, c - behind)

        def element_before(step, at):
            def run(q, c):
                if (c + BODY) % 4 == at:
                    step(q, c // 4 + 1)
            return run

        def tile(q, e):
            return (q * 2 + e) % NB

        with nc.Block() as block:
            zero_last_stage(block, k)

            @block.gpsimd
            def _(pool):
                def stage_kv(q, e):
                    wait(pool, s_mm, q, 16, 8 * e - 8)
                    wait(pool, kv_mm, q, 2, e - 1)
                    t = tile(q, e)
                    pool.tensor_copy(kvT[e % 2][:, 0:P], k.ctx_cols[:, ds(t * P, P)]).then_inc(kvT_ready, 1)
                    pool.tensor_copy(kvT[e % 2][:, P:KV], k.cols[:, ds(t * P, P)]).then_inc(kvT_ready, 1)

                def scale(q, c):
                    wait(pool, inv_ready, q, 8, c + 1)
                    p = probs[c % 4]
                    pool.tensor_tensor(p[:, :, :], p[:, :, :], per_row(inv[c % 4][:, :], KV), ALU.mult
                                       ).then_inc(scaled, 1)

                stage_kv(0, 0)
                schedule(pool, [(element_before(stage_kv, 2), 0), (scale, 0)])

            @block.tensor
            def _(pe):
                def queries(q, c):
                    wait(pe, kvT_ready, q, 4, 2 * (c // 4) + 2)
                    wait(pe, t_ready, q, 8, c)
                    for i in range(Q4):
                        ins = pe.matmul(t_ps[:, i * P:(i + 1) * P], k.qk_w[:, 4 * (c % 4) + i, :],
                                        kvT[c // 4 % 2][:, P:KV], start=True, stop=True)
                    ins.then_inc(t_mm, 1)

                def scores(q, c):
                    wait(pe, t_ready, q, 8, c + 1)
                    wait(pe, probs_done, q, 32, 4 * c)
                    for pair in range(2):
                        for i in range(2):
                            ins = pe.matmul(s_ps[pair][:, i * KV:(i + 1) * KV], tT[c % 2][:, 2 * pair + i, :],
                                            kvT[c // 4 % 2][:, :], start=True, stop=True)
                        ins.then_inc(s_mm, 1)

                def turn_kv(q, e):
                    wait(pe, kvT_ready, q, 4, 2 * e + 2)
                    wait(pe, kv_ready, q, 2, e)
                    for j in range(2):
                        ins = pe.transpose(kv_ps[:, j * D:(j + 1) * D], kvT[e % 2][:, j * P:(j + 1) * P], k.ident[:, :])
                    ins.then_inc(kv_mm, 1)

                def times_kv(q, c):
                    wait(pe, p0_ready, q, 8, c + 1)
                    wait(pe, p1_ready, q, 8, c + 1)
                    wait(pe, kv_ready, q, 2, c // 4 + 1)
                    wait(pe, u_ready, q, 8, c)
                    for j in range(2):
                        ins = pe.matmul(u_ps[:, :], kv[c // 4 % 2][:, j, :],
                                        pT[c % 2][:, j, :, :].rearrange("p h s -> p (h s)"), start=(j == 0), stop=(j == 1))
                    ins.then_inc(u_mm, 1)

                def output(q, c):
                    wait(pe, u_ready, q, 8, c + 1)
                    if c % 4 == 0:
                        wait(pe, y_used, q, 2, c // 4)
                    for i in range(Q4):
                        h = 4 * (c % 4) + i
                        ins = pe.matmul(y_ps[:, 0:D], uT[c % 2][:, i, :], k.vo_w[:, h, :], start=(h == 0), stop=(h == H - 1))
                    ins.then_inc(o_mm, 1)

                def turn_probs(q, c):
                    wait(pe, scaled, q, 8, c + 1)
                    wait(pe, p0_ready, q, 8, c)
                    wait(pe, p1_ready, q, 8, c)
                    for j in range(2):
                        for i in range(Q4):
                            ins = pe.transpose(p_ps[j][:, i * P:(i + 1) * P], probs[c % 4][:, i, j * P:(j + 1) * P],
                                               k.ident[:, :])
                    ins.then_inc(x_mm, 1)

                turn_kv(0, 0)
                schedule(pe, [(queries, -1), (scores, 0), (element_before(turn_kv, 3), 0), (times_kv, 3), (output, 4),
                              (turn_probs, 2)])

            @block.scalar
            def _(act):
                def exps(q, c):
                    wait(act, x_mm, q, 8, c - 3)
                    for i in range(Q4):
                        if i % 2 == 0:
                            wait(act, nm_ready, q, 16, 2 * c + i // 2 + 1)
                        act.activation(probs[c % 4][:, i, :], s_ps[i // 2][:, (i % 2) * KV:(i % 2 + 1) * KV], ACT.Exp,
                                       bias=nm[c % 4][:, i:i + 1], scale=SC, accum_out=sums[c % 4][:, i:i + 1]
                                       ).then_inc(probs_done, 1)

                def take_u(q, c):
                    wait(act, u_mm, q, 8, c + 1)
                    wait(act, o_mm, q, 8, c - 1)
                    act.activation(uT[c % 2][:, :, :], u_ps[:, :].rearrange("p (h s) -> p h s", h=Q4), ACT.Copy
                                   ).then_inc(u_ready, 1)

                def take_p(q, c):
                    wait(act, x_mm, q, 8, c + 1)
                    wait(act, u_mm, q, 8, c - 1)
                    act.activation(pT[c % 2][:, 0, :, :], p_ps[0][:, :].rearrange("p (h s) -> p h s", h=Q4), ACT.Copy
                                   ).then_inc(p0_ready, 1)
                schedule(act, [(exps, 0), (take_u, 3), (take_p, 2)])

            @block.vector
            def _(dve):
                def take_t(q, c):
                    wait(dve, t_mm, q, 8, c + 1)
                    wait(dve, s_mm, q, 16, 2 * (c - 1))
                    dve.tensor_copy(tT[c % 2][:, :, :], t_ps[:, :].rearrange("p (h s) -> p h s", h=Q4)
                                    ).then_inc(t_ready, 1)

                def maxima(q, c):
                    for pair in range(2):
                        m = slice(2 * pair, 2 * pair + 2)
                        wait(dve, s_mm, q, 16, 2 * c + pair + 1)
                        dve.tensor_reduce(mx[c % 4][:, m], s_ps[pair][:, :].rearrange("p (h s) -> p h s", h=2),
                                          AX.X, ALU.max).then_inc(maxed, 1)
                        wait(dve, maxed, q, 16, 2 * c + pair + 1)
                        dve.tensor_scalar(nm[c % 4][:, m], mx[c % 4][:, m], -SC, None, ALU.mult).then_inc(nm_ready, 1)

                def take_kv(q, e):
                    wait(dve, kv_mm, q, 2, e + 1)
                    wait(dve, u_mm, q, 8, 4 * e - 4)
                    dve.tensor_copy(kv[e % 2][:, :, :], kv_ps[:, 0:KV].rearrange("p (j d) -> p j d", j=2)
                                    ).then_inc(kv_ready, 1)

                def add_output(q, c):
                    if c % 4 == 3:
                        wait(dve, o_mm, q, 8, c + 1)
                        xt = k.x[:, ds(tile(q, c // 4), 1), :].rearrange("p o d -> p (o d)")
                        dve.scalar_tensor_tensor(out=xt, in0=y_ps[:, 0:D], scalar=k.tg[:, 2:3], in1=xt,
                                                 op0=ALU.mult, op1=ALU.add).then_inc(y_used, 1)

                def take_p(q, c):
                    wait(dve, x_mm, q, 8, c + 1)
                    wait(dve, u_mm, q, 8, c - 1)
                    dve.tensor_copy(pT[c % 2][:, 1, :, :], p_ps[1][:, :].rearrange("p (h s) -> p h s", h=Q4)
                                    ).then_inc(p1_ready, 1)

                def invert(q, c):
                    wait(dve, probs_done, q, 32, 4 * c + 4)
                    dve.reciprocal(inv[c % 4][:, :], sums[c % 4][:, :]).then_inc(inv_ready, 1)

                take_kv(0, 0)
                schedule(dve, [(take_t, -1), (maxima, 0), (element_before(take_kv, 3), 0), (add_output, 4), (take_p, 2),
                               (invert, 0)])


def capacity_route(nc, k, name, gate, capacity, by_choice, bias=None, floor=None, add_eps=0.0):
    with ExitStack() as ctx:
        s = Space(nc, ctx, name, k)
        p, rest, eq = (s.sb(n, [P, NB, E]) for n in ("p", "rest", "eq"))
        sel = [s.sb(f"sel{i}", [P, NB, E]) for i in range(2)]
        best = [s.sb(f"best{i}", [P, NB]) for i in range(2)]
        red = s.sb("red", [P, NB])
        n_q = 2 if by_choice else 1
        LQ = n_q * NB
        router_bias = s.sb("router_bias", [P, E])
        queued = s.sb("queued", [P, n_q, NB, E])
        carry = s.sb("carry", [P, E, LQ])
        total = s.sb("total", [P, E, LQ])
        until = s.sb("until", [P, E, LQ])
        place = s.sb("place", [P, E, LQ])
        prefix_ps, total_ps = s.ps("prefix", [P, BANK]), s.ps("total", [P, BANK])
        w_in, chain, filled, shifted, exped, queue_ready, counted = (s.sem(n) for n in (
            "w_in", "chain", "filled", "shifted", "exped", "queue_ready", "counted"))
        with nc.Block() as block:
            zero_last_stage(block, k)

            @block.sync
            def _(sp):
                if bias is not None:
                    sp.dma_start(router_bias[:, :], bias.partition_broadcast(P)).then_inc(w_in, 16)

            @block.gpsimd
            def _(pool):
                pool.memset(carry[:, :, :], 1.0).then_inc(filled, 1)
                pool.wait_ge(filled, 1)
                pool.memset(carry[:, :, 0:1], 0.0).then_inc(filled, 1)

            @block.scalar
            def _(act):
                act.wait_ge(shifted, 1)
                act.activation(p[:, :, :], p[:, :, :], ACT.Exp).then_inc(exped, 1)

            @block.tensor
            def _(pe):
                pe.wait_ge(queue_ready, 1)
                flat = queued[:, :, :, :].rearrange("p i t e -> p (i t e)")
                n = n_q * NB * E
                pe.matmul(prefix_ps[:, 0:n], k.upto[:, :], flat, start=True, stop=True).then_inc(counted, 1)
                pe.matmul(total_ps[:, 0:n], k.ones[:, :], flat, start=True, stop=True).then_inc(counted, 1)

            @block.vector
            def _(dve):
                link = Chain(dve, chain)
                if bias is not None:
                    dve.wait_ge(w_in, 16)
                    link(dve.tensor_tensor(k.logits[:, :, :], k.logits[:, :, :], per_group(router_bias[:, :], NB),
                                           ALU.add))
                link(dve.tensor_reduce(red[:, :], k.logits[:, :, :], AX.X, ALU.max))
                dve.tensor_tensor(p[:, :, :], k.logits[:, :, :], per_row(red[:, :], E), ALU.subtract).then_inc(shifted, 1)
                dve.wait_ge(exped, 1)
                link(dve.tensor_reduce(red[:, :], p[:, :, :], AX.X, ALU.add))
                link(dve.reciprocal(red[:, :], red[:, :]))
                link(dve.tensor_tensor(p[:, :, :], p[:, :, :], per_row(red[:, :], E), ALU.mult))
                top_two(link, dve, k, p, rest, eq, red, best, sel)
                link(dve.tensor_tensor(red[:, :], best[0][:, :], best[1][:, :], ALU.add))
                if add_eps:
                    link(dve.tensor_scalar(red[:, :], red[:, :], add_eps, None, ALU.add))
                link(dve.reciprocal(red[:, :], red[:, :]))
                for i in range(2):
                    link(dve.tensor_tensor(best[i][:, :], best[i][:, :], red[:, :], ALU.mult))
                    if floor is not None:
                        link(dve.tensor_scalar(red[:, :] if i else rest[:, :, 0:1].rearrange("p t o -> p (t o)"),
                                               best[i][:, :], floor, None, ALU.is_gt))
                        link(dve.tensor_tensor(sel[i][:, :, :], sel[i][:, :, :],
                                               per_row(red[:, :], E) if i else rest[:, :, 0:1].to_broadcast([P, NB, E]),
                                               ALU.mult))
                if by_choice:
                    for i in range(2):
                        link(dve.tensor_copy(queued[:, i, :, :], sel[i][:, :, :]))
                else:
                    link(dve.tensor_tensor(queued[:, 0, :, :], sel[0][:, :, :], sel[1][:, :, :], ALU.add))
                dve.sem_inc(queue_ready, 1)
                dve.wait_ge(counted, 2)
                dve.wait_ge(filled, 2)

                def by_expert(ps):
                    return ps[:, 0:LQ * E].rearrange("p (l e) -> p e l", e=E)
                link(dve.tensor_copy(total[:, :, :], by_expert(total_ps)))
                link(dve.tensor_tensor_scan(until[:, :, :].rearrange("p e l -> p (e l)"),
                                            carry[:, :, :].rearrange("p e l -> p (e l)"),
                                            total[:, :, :].rearrange("p e l -> p (e l)"), 0.0, ALU.mult, ALU.add))
                link(dve.tensor_tensor(until[:, :, :], until[:, :, :], total[:, :, :], ALU.subtract))
                link(dve.tensor_tensor(place[:, :, :], by_expert(prefix_ps), until[:, :, :], ALU.add))
                link(dve.tensor_scalar(place[:, :, :], place[:, :, :], float(capacity), None, ALU.is_le))
                for i in range(2):
                    kept = place[:, :, i * NB:(i + 1) * NB] if by_choice else place[:, :, :]
                    link(dve.tensor_tensor(sel[i][:, :, :], sel[i][:, :, :], kept.rearrange("p e t -> p t e"), ALU.mult))
                    link(dve.tensor_tensor(sel[i][:, :, :], sel[i][:, :, :], per_row(best[i][:, :], E), ALU.mult))
                link(dve.tensor_tensor(sel[0][:, :, :], sel[0][:, :, :], sel[1][:, :, :], ALU.add))
                link(dve.tensor_scalar(k.weight[:, :, :], sel[0][:, :, :], gate, None, ALU.mult))


def row_mixture(nc, k, name, chunks, func, w1_src, w2_src, b1_src=None, out_scale=None, out_bias=None):
    full = out_scale is not None
    with ExitStack() as ctx:
        s = Space(nc, ctx, name, k)
        w1, w2 = (s.sb(n, [P, E, chunks, P]) for n in ("w1", "w2"))
        hidden = [s.sb(f"hidden{i}", [P, chunks, BANK]) for i in range(2)]
        h_ps = [s.ps(f"h{i}", [P, BANK]) for i in range(chunks)]
        o_ps = [s.ps(f"o{i}", [P, BANK]) for i in range(2)]
        (w_in, scaled, h_mm, act_done, o_mm, added, w_staged, w_turned, wT_ready, bias_mm, sum_ready, tmp_ready,
         bias_added) = (s.sem(n) for n in (
             "w_in", "scaled", "h_mm", "act_done", "o_mm", "added", "w_staged", "w_turned", "wT_ready", "bias_mm",
             "sum_ready", "tmp_ready", "bias_added"))
        loads = [(w1[:, :, :, :], w1_src), (w2[:, :, :, :], w2_src)]
        if full:
            b1 = s.sb("b1", [P, E, chunks])
            scale_all, scale8, bias8 = s.sb("scale_all", [P, E, D]), s.sb("scale8", [E, D]), s.sb("bias8", [E, D])
            w_stage, w_sum, tmp = s.sb("w_stage", [P, G4, E]), s.sb("w_sum", [P, G4]), s.sb("tmp", [P, G4, D])
            wT = s.sb("wT", [E, BANK])
            bias_ps, wT_ps = s.ps("bias", [P, BANK]), s.ps("wT", [P, BANK])
            loads += [(b1[:, :, :], b1_src), (scale8[:, :], out_scale), (bias8[:, :], out_bias),
                      (scale_all[:, :, :], out_scale.partition_broadcast(P))]

        def wait(eng, sem, q, per_q, value):
            if not isinstance(q, int) or q * per_q + value >= 1:
                eng.wait_ge(sem, q * per_q + value)

        def schedule(eng, steps):
            for step, behind in steps:
                if behind == 0:
                    step(0, 0)
            with eng.Fori(0, NG) as q:
                for c in range(1, E + 1):
                    for step, behind in steps:
                        step(q, c - behind)

        def once(step, at):
            return lambda q, c: step(q) if c == at else None

        with nc.Block() as block:
            zero_last_stage(block, k)

            @block.sync
            def _(sp):
                for dst, src in loads:
                    sp.dma_start(dst, src).then_inc(w_in, 16)

            @block.gpsimd
            def _(pool):
                if full:
                    def stage(q):
                        pool.wait_ge(w_turned, q)
                        pool.wait_ge(sum_ready, q)
                        pool.tensor_copy(w_stage[:, :, :], k.weight[:, ds(q * G4, G4), :]).then_inc(w_staged, 1)
                    with pool.Fori(0, NG) as q:
                        stage(q)

            @block.tensor
            def _(pe):
                pe.wait_ge(w_in, 16 * len(loads))

                def hide(q, c):
                    g = (q + c // E) % NG
                    for i in range(chunks):
                        wait(pe, act_done, q, E * chunks, chunks * (c - 1) + i + 1)
                        pe.matmul(h_ps[i][:, :], w1[:, c % E, i, :], k.cols[:, ds(g * BANK, BANK)],
                                  start=True, stop=True).then_inc(h_mm, 1)

                def output(q, c):
                    wait(pe, act_done, q, E * chunks, chunks * (c + 1))
                    if full and c % E == 0:
                        pe.wait_ge(scaled, E + 1)
                    wait(pe, added, q, E * G4, G4 * max(c - 1, 0))
                    for j in range(G4):
                        for i in range(chunks):
                            ins = pe.matmul(o_ps[c % 2][:, j * D:(j + 1) * D], hidden[c % 2][:, i, j * P:(j + 1) * P],
                                            w2[:, c % E, i, :], start=(i == 0), stop=(i == chunks - 1))
                    ins.then_inc(o_mm, 1)

                def bias_rows(q):
                    pe.wait_ge(w_staged, q + 1)
                    pe.wait_ge(wT_ready, q)
                    for j in range(G4):
                        ins = pe.transpose(wT_ps[0:E, j * P:(j + 1) * P], w_stage[:, j, :], k.ident[:, :])
                    ins.then_inc(w_turned, 1)

                def bias_out(q):
                    pe.wait_ge(wT_ready, q + 1)
                    pe.wait_ge(bias_added, q)
                    for j in range(G4):
                        ins = pe.matmul(bias_ps[:, j * D:(j + 1) * D], wT[:, j * P:(j + 1) * P], bias8[:, :],
                                        start=True, stop=True)
                    ins.then_inc(bias_mm, 1)
                steps = [(hide, 0), (output, 1)]
                if full:
                    steps += [(once(bias_rows, 2), 0), (once(bias_out, 4), 0)]
                schedule(pe, steps)

            @block.scalar
            def _(act):
                act.wait_ge(w_in, 16 * len(loads))

                def activate(q, c):
                    wait(act, o_mm, q, E, c - 1)
                    for i in range(chunks):
                        wait(act, h_mm, q, E * chunks, chunks * c + i + 1)
                        if full:
                            ins = act.activation(hidden[c % 2][:, i, :], h_ps[i][:, :], func, bias=b1[:, c % E, i:i + 1])
                        else:
                            ins = act.activation(hidden[c % 2][:, i, :], h_ps[i][:, :], func)
                        ins.then_inc(act_done, 1)
                schedule(act, [(activate, 0)])

            @block.vector
            def _(dve):
                dve.wait_ge(w_in, 16 * len(loads))
                if full:
                    for e in range(E):
                        dve.tensor_tensor(w2[:, e, :, :], w2[:, e, :, :], per_group(scale_all[:, e, :], chunks), ALU.mult
                                          ).then_inc(scaled, 1)
                    dve.tensor_tensor(bias8[:, :], bias8[:, :], scale8[:, :], ALU.mult).then_inc(scaled, 1)

                def add(q, c):
                    wait(dve, o_mm, q, E, c + 1)
                    wait(dve, added, q, E * G4, G4 * c)
                    if full:
                        wait(dve, bias_added, q, 1, 1 if c >= 4 else 0)
                    for j in range(G4):
                        xt = k.x[:, ds(q * G4 + j, 1), :].rearrange("p o d -> p (o d)")
                        dve.scalar_tensor_tensor(out=xt, in0=o_ps[c % 2][:, j * D:(j + 1) * D],
                                                 scalar=k.weight[:, ds(q * G4 + j, 1), c % E:c % E + 1].rearrange(
                                                     "p o e -> p (o e)"),
                                                 in1=xt, op0=ALU.mult, op1=ALU.add).then_inc(added, 1)

                def take_wT(q):
                    dve.wait_ge(w_turned, q + 1)
                    dve.wait_ge(bias_mm, q)
                    dve.tensor_copy(wT[:, :], wT_ps[0:E, :]).then_inc(wT_ready, 1)
                    dve.wait_ge(w_staged, q + 1)
                    dve.tensor_reduce(w_sum[:, :], w_stage[:, :, :], AX.X, ALU.add).then_inc(sum_ready, 1)
                    dve.wait_ge(sum_ready, q + 1)
                    dve.wait_ge(bias_added, q)
                    dve.tensor_tensor(tmp[:, :, :], k.rows[:, ds(q * G4, G4), :], per_row(w_sum[:, :], D), ALU.mult
                                      ).then_inc(tmp_ready, 1)
                    dve.wait_ge(tmp_ready, q * 3 + 1)

                def add_bias(q):
                    dve.wait_ge(bias_mm, q + 1)
                    dve.tensor_tensor(tmp[:, :, :], tmp[:, :, :], bias_ps[:, :].rearrange("p (t d) -> p t d", t=G4),
                                      ALU.add).then_inc(tmp_ready, 1)
                    dve.wait_ge(tmp_ready, q * 3 + 2)
                    wait(dve, added, q, E * G4, G4 * 4)
                    xt = k.x[:, ds(q * G4, G4), :]
                    dve.tensor_tensor(xt, xt, tmp[:, :, :], ALU.add).then_inc(bias_added, 1)
                    dve.sem_inc(tmp_ready, 1)
                steps = [(add, 1)]
                if full:
                    steps += [(once(take_wT, 2), 0), (once(add_bias, 4), 0)]
                schedule(dve, steps)


def l3_attention(nc, k):
    H, DA, ROUNDS = 16, 8, 4
    Q4, NQ = 4, 4
    SC = DA ** -0.5
    BODY = 4
    LOWEST = -3e38
    with ExitStack() as ctx:
        s = Space(nc, ctx, "l3a", k)
        wq = s.sb("wq", [P, P])
        wk = s.sb("wk", [P, Q4, P])
        two = range(2)
        k_in = [s.sb(f"k_in{i}", [P, P]) for i in two]
        v_raw = [s.sb(f"v_raw{i}", [P, D]) for i in two]
        v = [s.sb(f"v{i}", [P, H, DA + 1]) for i in range(4)]
        qT, kT = s.sb("qT", [P, P]), s.sb("kT", [P, Q4, P])
        score = [s.sb(f"score{i}", [P, H, P]) for i in range(4)]
        work = s.sb("work", [P, H, P])
        top = [s.sb(f"top{i}", [P, ROUNDS, H, 8]) for i in two]
        nm = [s.sb(f"nm{i}", [P, H]) for i in two]
        probs = s.sb("probs", [P, H, P])
        above = s.sb("above", [P, H, P])
        pT = [s.sb(f"pT{i}", [P, Q4, P]) for i in two]
        inv = s.sb("inv", [P, H])
        o_norm = s.sb("o_norm", [P, H, DA])
        q_ps, k_ps, p_ps, o_ps = (s.ps(n, [P, BANK]) for n in ("q", "k", "p", "o"))
        s_ps = [s.ps(f"s{i}", [P, BANK]) for i in range(NQ)]
        k_loaded, v_loaded = ([s.sem(f"{n}_loaded{i}") for i in two] for n in "kv")
        (w_in, filled, v_ready, q_mm, k_mm, q_ready, k_ready, s_mm, s_ready, found, nm_ready, probs_done, compared,
         masked, p_mm, p_ready, av_mm, inv_ready, o_ready, x_done) = (s.sem(n) for n in (
             "w_in", "filled", "v_ready", "q_mm", "k_mm", "q_ready", "k_ready", "s_mm", "s_ready", "found", "nm_ready",
             "probs_done", "compared", "masked", "p_mm", "p_ready", "av_mm", "inv_ready", "o_ready", "x_done"))
        FINDS = (2 * ROUNDS - 1) * H

        def wait(eng, sem, q, per_element, value):
            n = q * (BODY * per_element) + value
            if not isinstance(q, int) or n >= 1:
                eng.wait_ge(sem, n)

        def schedule(eng, steps):
            for c in range(-1, 2):
                for step, behind in steps:
                    if c - behind >= 0:
                        step(0, c - behind)
            with eng.Fori(0, NB // BODY) as q:
                for c in range(2, 2 + BODY):
                    for step, behind in steps:
                        step(q, c - behind)

        def tile(q, c):
            return (q * BODY + c) % NB

        with nc.Block() as block:
            zero_last_stage(block, k)

            @block.sync
            def _(sp):
                sp.dma_start(wq[:, :], k.d["L3_WqT"]).then_inc(w_in, 16)
                sp.dma_start(wk[:, :, :], k.d["L3_WkT"]).then_inc(w_in, 16)

                def load(q, c):
                    i = c % 2
                    wait(sp, k_mm, q, 1, c - 1)
                    wait(sp, v_ready, q, 1, c - 1)
                    sp.dma_start(k_in[i][:, :], k.d["ctxT"][ds(tile(q, c), 1), :, :].rearrange("o p s -> (o p) s")
                                 ).then_inc(k_loaded[i], 16)
                    sp.dma_start(v_raw[i][:, :], k.d["ctx"][ds(tile(q, c), 1), :, :].rearrange("o p d -> (o p) d")
                                 ).then_inc(v_loaded[i], 16)
                schedule(sp, [(load, -1)])

            @block.gpsimd
            def _(pool):
                for t in v:
                    pool.memset(t[:, :, :], 1.0).then_inc(filled, 1)
                pool.wait_ge(filled, 4)

                def take_v(q, c):
                    wait(pool, v_loaded[c % 2], q, 8, 16 * (c // 2 + 1))
                    wait(pool, av_mm, q, 1, c - 3)
                    wait_apart(pool, k.waited_pool)
                    pool.tensor_copy(v[c % 4][:, :, 0:DA], v_raw[c % 2][:, :].rearrange("p (h d) -> p h d", h=H)
                                     ).then_inc(v_ready, 1)

                def mask(q, c):
                    wait(pool, nm_ready, q, 1, c + 1)
                    for n in range(NQ):
                        hs = slice(Q4 * n, Q4 * n + Q4)
                        wait(pool, masked, q, NQ, NQ * c + n - NQ + 1)
                        wait_apart(pool, k.waited_pool)
                        for h in range(Q4 * n, Q4 * n + Q4):
                            ins = pool.tensor_scalar(above[:, h, :], score[c % 4][:, h, :],
                                                     top[c % 2][:, ROUNDS - 1, h, 7:8], None, ALU.is_ge)
                        ins.then_inc(compared, 1)
                        wait(pool, compared, q, NQ, NQ * c + n + 1)
                        wait(pool, probs_done, q, H, H * c + Q4 * n + Q4)
                        pool.tensor_tensor(probs[:, hs, :], probs[:, hs, :], above[:, hs, :], ALU.mult
                                           ).then_inc(masked, 1)
                schedule(pool, [(take_v, -1), (mask, 1)])

            @block.tensor
            def _(pe):
                pe.wait_ge(w_in, 32)

                def scores(q, c):
                    wait(pe, q_ready, q, 1, c)
                    pe.matmul(q_ps[:, 0:P], wq[:, :], k.cols[:, ds(tile(q, c) * P, P)], start=True, stop=True
                              ).then_inc(q_mm, 1)
                    wait(pe, k_loaded[c % 2], q, 8, 16 * (c // 2 + 1))
                    wait(pe, k_ready, q, 1, c)
                    for r in range(Q4):
                        ins = pe.matmul(k_ps[:, r * P:(r + 1) * P], wk[:, r, :], k_in[c % 2][:, :], start=True, stop=True)
                    ins.then_inc(k_mm, 1)
                    wait(pe, q_ready, q, 1, c + 1)
                    wait(pe, k_ready, q, 1, c + 1)
                    wait(pe, s_ready, q, NQ, NQ * c)
                    for n in range(NQ):
                        rows = slice(32 * n, 32 * n + 32)
                        pe.matmul(s_ps[n][:, :], qT[rows, :], kT[rows, :, :].rearrange("p r s -> p (r s)"),
                                  start=True, stop=True).then_inc(s_mm, 1)

                def apply(q, c):
                    for n in range(NQ + 1):
                        if n < NQ:
                            wait(pe, masked, q, NQ, NQ * c + n + 1)
                            wait(pe, p_ready, q, NQ, NQ * c + n)
                            for i in range(Q4):
                                ins = pe.transpose(p_ps[:, i * P:(i + 1) * P], probs[:, Q4 * n + i, :], k.ident[:, :])
                            ins.then_inc(p_mm, 1)
                        if n > 0:
                            m = n - 1
                            wait(pe, p_ready, q, NQ, NQ * c + m + 1)
                            if m == 0:
                                wait(pe, v_ready, q, 1, c + 1)
                                wait(pe, o_ready, q, 1, c)
                            for i in range(Q4):
                                h = Q4 * m + i
                                ins = pe.matmul(o_ps[:, h * (DA + 1):(h + 1) * (DA + 1)], pT[m % 2][:, i, :],
                                                v[c % 4][:, h, :], start=True, stop=True)
                    ins.then_inc(av_mm, 1)
                schedule(pe, [(scores, -1), (apply, 1)])

            @block.scalar
            def _(act):
                def take_scores(q, c):
                    wait(act, q_mm, q, 1, c + 1)
                    act.activation(qT[:, :], q_ps[:, 0:P], ACT.Copy).then_inc(q_ready, 1)
                    wait(act, k_mm, q, 1, c + 1)
                    act.activation(kT[:, :, :], k_ps[:, :].rearrange("p (r s) -> p r s", r=Q4), ACT.Copy
                                   ).then_inc(k_ready, 1)
                    wait(act, compared, q, NQ, NQ * (c - 3))
                    for n in range(NQ):
                        wait(act, s_mm, q, NQ, NQ * c + n + 1)
                        act.activation(score[c % 4][:, Q4 * n:Q4 * n + Q4, :],
                                       s_ps[n][:, :].rearrange("p (r s) -> p r s", r=Q4), ACT.Copy, scale=SC
                                       ).then_inc(s_ready, 1)

                def exps(q, c):
                    wait(act, nm_ready, q, 1, c + 1)
                    wait(act, p_mm, q, NQ, NQ * c)
                    for h in range(H):
                        act.activation(probs[:, h, :], score[c % 4][:, h, :], ACT.Exp, bias=nm[c % 2][:, h:h + 1]
                                       ).then_inc(probs_done, 1)

                def take_p(q, c):
                    for n in range(NQ):
                        wait(act, p_mm, q, NQ, NQ * c + n + 1)
                        if n < 2:
                            wait(act, av_mm, q, 1, c)
                        act.activation(pT[n % 2][:, :, :], p_ps[:, :].rearrange("p (h s) -> p h s", h=Q4), ACT.Copy
                                       ).then_inc(p_ready, 1)
                schedule(act, [(take_scores, -1), (exps, 1), (take_p, 1)])

            @block.vector
            def _(dve):
                def cutoffs(q, c):
                    t = top[c % 2]
                    wait(dve, masked, q, NQ, NQ * (c - 1))
                    n = 0
                    for first in range(0, H, 2 * Q4):
                        wait(dve, s_ready, q, NQ, NQ * c + first // Q4 + 2)
                        for step in range(2 * ROUNDS - 1):
                            for h in range(first, first + 2 * Q4):
                                src = score[c % 4][:, h, :] if step < 2 else work[:, h, :]
                                if h % Q4 == 0:
                                    wait(dve, found, q, FINDS, FINDS * c + n - Q4)
                                    wait_apart(dve, k.waited_dve)
                                if step % 2 == 0:
                                    ins = dve.max(t[:, step // 2, h, :], src)
                                else:
                                    ins = dve.match_replace(work[:, h, :], t[:, step // 2, h, :], src, LOWEST)
                                ins.then_inc(found, 1)
                                n += 1
                    wait(dve, found, q, FINDS, FINDS * (c + 1))
                    dve.tensor_scalar(nm[c % 2][:, :], t[:, 0, :, 0:1].rearrange("p h o -> p (h o)"), -1.0, None,
                                      ALU.mult).then_inc(nm_ready, 1)

                def add(q, c):
                    wait(dve, av_mm, q, 1, c + 1)
                    o = o_ps[:, 0:H * (DA + 1)].rearrange("p (h d) -> p h d", h=H)
                    dve.reciprocal(inv[:, :], o[:, :, DA:DA + 1].rearrange("p h o -> p (h o)")).then_inc(inv_ready, 1)
                    wait(dve, inv_ready, q, 1, c + 1)
                    dve.tensor_tensor(o_norm[:, :, :], o[:, :, 0:DA], per_row(inv[:, :], DA), ALU.mult
                                      ).then_inc(o_ready, 1)
                    wait(dve, o_ready, q, 1, c + 1)
                    xt = k.x[:, ds(tile(q, c), 1), :].rearrange("p o d -> p (o d)")
                    dve.scalar_tensor_tensor(out=xt, in0=o_norm[:, :, :].rearrange("p h d -> p (h d)"),
                                             scalar=k.tg[:, 3:4], in1=xt, op0=ALU.mult, op1=ALU.add).then_inc(x_done, 1)
                    wait(dve, x_done, q, 1, c + 1)
                schedule(dve, [(cutoffs, 0), (add, 2)])


def l3_block_attention(nc, k):
    H, GK, R, HD, S, PJ = 16, 4, 4, 8, NB, 4
    SC = HD ** -0.5
    BODY = 4
    with ExitStack() as ctx:
        s = Space(nc, ctx, "l3b", k)
        wq, proj = s.sb("wq", [P, P]), s.sb("proj", [P, D])
        wk = s.sb("wk", [P, P])
        wv = s.sb("wv", [P, P])
        two = range(2)
        stage = [s.sb(f"stage{i}", [P, PJ, S]) for i in two]
        stage4 = [s.sb(f"stage4{i}", [P, PJ, R, S]) for i in two]
        qT, kT = s.sb("qT", [P, P]), s.sb("kT", [P, R, P])
        v = [s.sb(f"v{i}", [P, PJ, P]) for i in two]
        head_of = s.sb("head_of", [P, R])
        own_head = s.sb("own_head", [P, R])
        own_cols = s.sb("own_cols", [P, PJ, P])
        causal = s.sb("causal", [P, GK, P])
        score = [s.sb(f"score{i}", [P, H, S]) for i in two]
        mx, sums, inv = ([s.sb(f"{n}{i}", [P, H]) for i in two] for n in ("mx", "sums", "inv"))
        pT = s.sb("pT", [P, GK, P])
        ao, aoT = s.sb("ao", [P, H, HD]), s.sb("aoT", [P, P])
        y = [s.sb(f"y{i}", [P, D]) for i in two]
        s_ps = s.ps("s", [P, GK, BANK])
        qk_ps, v_ps, p_ps, out_ps = (s.ps(n, [P, BANK]) for n in ("qk", "v", "p", "out"))
        q_ps, k_ps = (qk_ps[:, i * P:(i + 1) * P] for i in range(2))
        o_ps, aoT_ps, y_ps = (out_ps[:, i * P:(i + 1) * P] for i in range(3))
        y_stored = [s.sem(f"y_stored{i}") for i in two]
        (w_in, filled, made, staged, k_mm, v_mm, q_ready, k_ready, v_ready, s_mm, s_out, maxed, shifted, exped,
         summed, inv_ready, p_mm, p_ready, o_mm, ao_ready, aoT_mm, aoT_ready, y_mm, y_ready) = (s.sem(n) for n in (
             "w_in", "filled", "made", "staged", "k_mm", "v_mm", "q_ready", "k_ready", "v_ready", "s_mm",
             "s_out", "maxed", "shifted", "exped", "summed", "inv_ready", "p_mm", "p_ready", "o_mm", "ao_ready",
             "aoT_mm", "aoT_ready", "y_mm", "y_ready"))
        NN = P // PJ
        loads = [(wq[:, :], k.d["L3b_WqT"]), (wk[:, :], k.d["L3b_WkT"]), (wv[:, :], k.d["L3b_WvT"]),
                 (proj[:, :], k.d["L3b_projT"]), (head_of[:, :], k.d["L3b_head_of"])]

        def wait(eng, sem, q, per_n, value):
            n = q * (BODY * per_n) + value
            if not isinstance(q, int) or n >= 1:
                eng.wait_ge(sem, n)

        def schedule(eng, steps):
            for c in range(-1, 2):
                for step, behind in steps:
                    if c - behind >= 0:
                        step(0, c - behind)
            with eng.Fori(0, NN // BODY) as q:
                for c in range(2, 2 + BODY):
                    for step, behind in steps:
                        step(q, c - behind)

        def first_position(q, c):
            return ((q * BODY + c) % NN) * PJ

        with nc.Block() as block:
            zero_last_stage(block, k)

            @block.sync
            def _(sp):
                for dst, src in loads:
                    sp.dma_start(dst, src).then_inc(w_in, 16)

                def store(q, c):
                    wait(sp, y_ready, q, 1, c + 1)
                    dst = k.block_out[:, ds(first_position(q, c), PJ), :].rearrange("s j d -> j s d")
                    sp.dma_start(dst, y[c % 2][:, :]).then_inc(y_stored[c % 2], 16)
                schedule(sp, [(store, 2)])
                for i in two:
                    sp.wait_ge(y_stored[i], 16 * NN // 2)

            @block.gpsimd
            def _(pool):
                pool.memset(own_head[:, :], 1.0).then_inc(filled, 1)
                pool.memset(causal[:, :, :], 0.0).then_inc(filled, 1)
                pool.wait_ge(filled, 2)
                pool.affine_select(out=own_head[:, :], in_=own_head[:, :], compare_op=ALU.is_ge, fill=0.0,
                                   base=0, pattern=[[-S, R]], channel_multiplier=1).then_inc(made, 1)
                pool.wait_ge(made, 1)
                pool.affine_select(out=own_head[:, :], in_=own_head[:, :], compare_op=ALU.is_ge, fill=0.0,
                                   base=S - 1, pattern=[[S, R]], channel_multiplier=-1).then_inc(made, 1)
                pool.wait_ge(made, 2)
                pool.tensor_copy(own_cols[:, :, :].rearrange("p j (g r d) -> p (j g) r d", g=GK, r=R),
                                 own_head[:, :].unsqueeze(1).unsqueeze(3).to_broadcast([P, PJ * GK, R, HD])
                                 ).then_inc(made, 1)
                for j in range(PJ):
                    pool.wait_ge(made, 3 + j)
                    part = causal[S * j:S * j + S, :, :].rearrange("p g (r t) -> p (g r) t", r=R)
                    pool.affine_select(out=part, in_=part, compare_op=ALU.is_ge, fill=-3e38,
                                       base=0, pattern=[[0, H], [-1, S]], channel_multiplier=1).then_inc(made, 1)
                pool.wait_ge(made, 3 + PJ)

                def gather(q, c):
                    wait(pool, v_mm, q, 1, c - 1)
                    src = k.cols[:, :].rearrange("p (s t) -> p t s", s=S)[:, ds(first_position(q, c), PJ), :]
                    pool.tensor_copy(stage[c % 2][:, :, :], src).then_inc(staged, 1)
                    wait(pool, staged, q, 2, 2 * c + 1)
                    wait_apart(pool, k.waited_pool)
                    pool.tensor_copy(stage4[c % 2][:, :, :, :],
                                     stage[c % 2][:, :, :].unsqueeze(2).to_broadcast([P, PJ, R, S])).then_inc(staged, 1)
                schedule(pool, [(gather, -1)])

            @block.tensor
            def _(pe):
                pe.wait_ge(w_in, 16 * len(loads))

                def project(q, c):
                    tokens = stage[c % 2][:, :, :].rearrange("p j s -> p (j s)")
                    wait(pe, staged, q, 2, 2 * c + 2)
                    wait(pe, k_ready, q, 1, c)
                    pe.matmul(q_ps, wq[:, :], tokens, start=True, stop=True)
                    pe.matmul(k_ps, wk[:, :], tokens, start=True, stop=True).then_inc(k_mm, 1)
                    wait(pe, v_ready, q, 1, c)
                    for j in range(PJ):
                        ins = pe.matmul(v_ps[:, j * P:(j + 1) * P],
                                        stage4[c % 2][:, j, :, :].rearrange("p r s -> p (r s)"), wv[:, :],
                                        start=True, stop=True)
                    ins.then_inc(v_mm, 1)

                def scores(q, c):
                    wait(pe, q_ready, q, 1, c + 1)
                    wait(pe, k_ready, q, 1, c + 1)
                    wait(pe, s_out, q, 1, c)
                    wait_apart(pe, k.waited_pe)
                    for j in range(PJ):
                        for g in range(GK):
                            rows = slice(32 * g, 32 * g + 32)
                            ins = pe.matmul(s_ps[S * j:S * j + S, g, 0:P], qT[rows, S * j:S * j + S],
                                            kT[rows, :, S * j:S * j + S], start=True, stop=True)
                    ins.then_inc(s_mm, 1)

                def apply(q, c):
                    wait(pe, exped, q, 1, c + 1)
                    wait(pe, p_ready, q, 1, c)
                    for g in range(GK):
                        ins = pe.transpose(p_ps[:, g * P:(g + 1) * P],
                                           score[c % 2][:, g * R:(g + 1) * R, :].rearrange("p r t -> p (r t)"), k.ident[:, :])
                    ins.then_inc(p_mm, 1)
                    wait(pe, p_ready, q, 1, c + 1)
                    wait(pe, v_ready, q, 1, c + 1)
                    wait(pe, y_ready, q, 1, c)
                    for j in range(PJ):
                        for g in range(GK):
                            ins = pe.matmul(o_ps[S * j:S * j + S, 32 * g:32 * g + 32], pT[:, g, S * j:S * j + S],
                                            v[c % 2][:, j, 32 * g:32 * g + 32], start=True, stop=True)
                    ins.then_inc(o_mm, 1)

                def output(q, c):
                    wait(pe, ao_ready, q, 1, c + 1)
                    pe.transpose(aoT_ps, ao[:, :, :].rearrange("p h d -> p (h d)"), k.ident[:, :]).then_inc(aoT_mm, 1)
                    wait(pe, aoT_ready, q, 1, c + 1)
                    pe.matmul(y_ps, aoT[:, :], proj[:, :], start=True, stop=True).then_inc(y_mm, 1)
                schedule(pe, [(project, -1), (scores, 0), (output, 2), (apply, 1)])

            @block.scalar
            def _(act):
                def exps(q, c):
                    wait(act, shifted, q, 1, c + 1)
                    act.activation(score[c % 2][:, :, :], score[c % 2][:, :, :], ACT.Exp).then_inc(exped, 1)

                def take_p(q, c):
                    wait(act, p_mm, q, 1, c + 1)
                    wait(act, o_mm, q, 1, c)
                    act.activation(pT[:, :, :], p_ps[:, :].rearrange("p (g s) -> p g s", g=GK), ACT.Copy
                                   ).then_inc(p_ready, 1)

                def take_out(q, c):
                    wait(act, aoT_mm, q, 1, c + 1)
                    wait(act, y_mm, q, 1, c)
                    act.activation(aoT[:, :], aoT_ps, ACT.Copy).then_inc(aoT_ready, 1)
                    wait(act, y_mm, q, 1, c + 1)
                    wait(act, y_stored[c % 2], q, 8, 16 * (c // 2))
                    act.activation(y[c % 2][:, :], y_ps, ACT.Copy).then_inc(y_ready, 1)
                schedule(act, [(take_out, 2), (take_p, 1), (exps, 0)])

            @block.vector
            def _(dve):
                dve.wait_ge(made, 3 + PJ)
                dve.wait_ge(w_in, 16 * len(loads))

                def take_qk(q, c):
                    wait(dve, k_mm, q, 1, c + 1)
                    wait(dve, s_mm, q, 1, c)
                    dve.tensor_copy(qT[:, :], q_ps).then_inc(q_ready, 1)
                    dve.tensor_tensor(kT[:, :, :], per_group(k_ps, R), per_row(head_of[:, :], P), ALU.mult
                                      ).then_inc(k_ready, 1)

                def take_v(q, c):
                    wait(dve, v_mm, q, 1, c + 1)
                    wait(dve, o_mm, q, 1, c - 1)
                    dve.tensor_tensor(v[c % 2][:, :, :], v_ps[:, :].rearrange("p (j n) -> p j n", j=PJ), own_cols[:, :, :],
                                      ALU.mult).then_inc(v_ready, 1)

                def soften(q, c):
                    t = score[c % 2]
                    wait(dve, s_mm, q, 1, c + 1)
                    wait(dve, p_mm, q, 1, c - 1)
                    wait(dve, summed, q, 1, c - 1)
                    dve.scalar_tensor_tensor(out=t[:, :, :].rearrange("p (g r) t -> p g (r t)", g=GK), in0=s_ps[:, :, 0:P],
                                             scalar=SC, in1=causal[:, :, :], op0=ALU.mult, op1=ALU.add).then_inc(s_out, 1)
                    wait(dve, s_out, q, 1, c + 1)
                    dve.tensor_reduce(mx[c % 2][:, :], t[:, :, :], AX.X, ALU.max).then_inc(maxed, 1)
                    wait(dve, maxed, q, 1, c + 1)
                    dve.tensor_tensor(t[:, :, :], t[:, :, :], per_row(mx[c % 2][:, :], S), ALU.subtract
                                      ).then_inc(shifted, 1)

                def total(q, c):
                    wait(dve, exped, q, 1, c + 1)
                    dve.tensor_reduce(sums[c % 2][:, :], score[c % 2][:, :, :], AX.X, ALU.add).then_inc(summed, 1)
                    wait(dve, summed, q, 1, c + 1)
                    dve.reciprocal(inv[c % 2][:, :], sums[c % 2][:, :]).then_inc(inv_ready, 1)

                def divide(q, c):
                    wait(dve, o_mm, q, 1, c + 1)
                    wait(dve, inv_ready, q, 1, c + 1)
                    wait(dve, aoT_mm, q, 1, c)
                    dve.tensor_tensor(ao[:, :, :], o_ps.rearrange("p (h d) -> p h d", h=H), per_row(inv[c % 2][:, :], HD),
                                      ALU.mult).then_inc(ao_ready, 1)
                schedule(dve, [(soften, 0), (take_qk, -1), (take_v, -1), (total, 1), (divide, 1)])


def l3_block_residual(nc, k):
    with ExitStack() as ctx:
        s = Space(nc, ctx, "l3h", k)
        att = s.sb("att", [P, NB, D])
        att_in, summed, x_done = (s.sem(n) for n in ("att_in", "summed", "x_done"))
        with nc.Block() as block:
            zero_last_stage(block, k)

            @block.sync
            def _(sp):
                sp.dma_start(att[:, :, :], k.block_out.rearrange("b p d -> p b d")).then_inc(att_in, 16)

            @block.vector
            def _(dve):
                dve.wait_ge(att_in, 16)
                with dve.Fori(0, NG) as g:
                    tiles = ds(g * G4, G4)
                    dve.tensor_tensor(k.rows[:, tiles, :], k.rows[:, tiles, :], att[:, tiles, :], ALU.add
                                      ).then_inc(summed, 1)
                    dve.wait_ge(summed, g + 1)
                    dve.scalar_tensor_tensor(out=k.x[:, tiles, :], in0=k.rows[:, tiles, :], scalar=k.tg[:, 7:8],
                                             in1=k.x[:, tiles, :], op0=ALU.mult, op1=ALU.add).then_inc(x_done, 1)


def program(nc, d, out, first=0, last=99):
    with ExitStack() as ctx:
        s = Space(nc, ctx, "net")
        k = Shared()
        k.d, k.stages, k.finals = d, [], ctx.enter_context(ExitStack())
        k.x = s.sb("x", [P, NB, D])
        k.rows = s.sb("rows", [P, NB, D])
        k.cols = s.sb("cols", [P, NB * P])
        k.tg = s.sb("tg", [P, 8])
        k.ident, k.lower, k.upto, k.ones = (s.sb(n, [P, P]) for n in ("ident", "lower", "upto", "ones"))
        k.neg_half = s.sb("neg_half", [P, NB])
        k.rank = s.sb("rank", [P, E])
        k.gates_w = s.sb("gates_w", [P, 4, E])
        k.logits, k.weight = (s.sb(n, [P, NB, E]) for n in ("logits", "weight"))
        k.mask_rows = s.sb("mask_rows", [E, NB * P], BF16)
        k.aT, k.emT = s.sb("aT", [P, P]), s.sb("emT", [P, P])
        k.expert_weight = s.sb("expert_weight", [P, E])
        k.neg_top = nc.dram_tensor("neg_top", (P, P), F32, kind="Internal").ap()
        k.waited_pe, k.waited_pool, k.waited_dve = (s.sem(f"waited_{n}") for n in ("pe", "pool", "dve"))
        setup(nc, k)
        layers = [
            lambda: (normalise(nc, k, "n0a"), l0_attention(nc, k)),
            lambda: (normalise(nc, k, "n0f", keep_rows=True, gate_w=k.gates_w[:, 0, :], logits=k.logits),
                     l0_route(nc, k), l0_mixture(nc, k)),
            lambda: (normalise(nc, k, "n1a"), l1_gates(nc, k), l1_attention(nc, k)),
            lambda: (normalise(nc, k, "n1f", gate_w=k.gates_w[:, 1, :], logits=k.logits),
                     l1_route(nc, k), l1_mixture(nc, k)),
            lambda: l2_cross(nc, k),
            lambda: (normalise(nc, k, "n2f", keep_rows=True, gate_w=k.gates_w[:, 2, :], logits=k.logits),
                     capacity_route(nc, k, "l2r", k.tg[:, 6:7], int(1.2 * (NB * P // E + 1)), True,
                                    bias=k.d["L2_ffn_router_b"], floor=1e-9, add_eps=1e-9),
                     row_mixture(nc, k, "l2f", 4, ACT.Gelu, k.d["L2_w1T"], k.d["L2_w2T"], k.d["L2_b1T"],
                                 k.d["L2_ffn_layer_scale"], k.d["L2_ffn_fc2_b"])),
            lambda: (normalise(nc, k, "n3a"), l3_attention(nc, k)),
            lambda: l3_block(nc, k),
        ]
        for layer in layers[first:last]:
            layer()
        finish(nc, k, out)


def l2_cross(nc, k):
    with ExitStack() as ctx:
        s = Space(nc, ctx, "l2")
        k.ctx_cols = s.sb("ctx_cols", [P, NB * P])
        k.qk_w, k.vo_w = s.sb("qk_w", [P, 16, P]), s.sb("vo_w", [P, 16, P])
        norms = s.sb("norms", [P, 4])
        load_weights(nc, k, "l2n", [(norms[:, :], k.d["L2_norms"])])
        normalise(nc, k, "n2c", source=k.d["ctx"], gain=norms[:, 0:1], shift=norms[:, 1:2], columns=k.ctx_cols)
        normalise(nc, k, "n2a", twice=True, gain=norms[:, 2:3], shift=norms[:, 3:4])
        l2_fold(nc, k)
        l2_attention(nc, k)


def l3_block(nc, k):
    with ExitStack() as ctx:
        s = Space(nc, ctx, "l3")
        norms = s.sb("norms", [P, 4])
        k.block_out = nc.dram_tensor("block_out", (NB, P, D), F32, kind="Internal").ap()
        load_weights(nc, k, "l3n", [(norms[:, :], k.d["L3_norms"])])
        normalise(nc, k, "n3f", twice=True, gain=norms[:, 0:1], shift=norms[:, 1:2], keep_rows=True)
        l3_block_attention(nc, k)
        l3_block_residual(nc, k)
        normalise(nc, k, "n3m", source="rows", gain=norms[:, 2:3], shift=norms[:, 3:4],
                  gate_w=k.gates_w[:, 3, :], logits=k.logits)
        capacity_route(nc, k, "l3r", k.tg[:, 7:8], -(-NB * P * 2 * 5 // (E * 4)), False)
        row_mixture(nc, k, "l3f", 2, ACT.Gelu_apprx_tanh, k.d["L3_w1T"], k.d["L3_w2T"])


def finish(nc, k, out):
    with ExitStack() as ctx:
        s = Space(nc, ctx, "end", k)
        stored = s.sem("stored")
        with nc.Block() as block:
            zero_last_stage(block, k)

            @block.sync
            def _(sp):
                sp.dma_start(out.rearrange("b p d -> p b d"), k.x[:, :, :]).then_inc(stored, 16)
                sp.wait_ge(stored, 16)


def layouts(inputs):
    import numpy as np
    a = {n: np.asarray(v) for n, v in inputs.items()}
    a["ctx"] = a.pop("ctx_1024")
    a["ctxT"] = a["ctx"].transpose(0, 2, 1)
    for n in ("bq", "bk"):
        a[f"L0_xattn_{n}_cols"] = a[f"L0_xattn_{n}"].reshape(8, 128).T
    for n in ("w1", "w2", "w3"):
        a[f"L0_{n}T"] = a.pop(f"L0_ffn_{n}").transpose(2, 0, 1)
    for n in ("b1", "b2", "b3"):
        a[f"L0_{n}T"] = a.pop(f"L0_ffn_{n}").T
    for n in ("sw1", "sw2"):
        a[f"L0_{n}T"] = a.pop(f"L0_ffn_{n}").reshape(2, 128, 128).transpose(2, 0, 1)
    a["L0_sw3T"] = a.pop("L0_ffn_sw3").T.reshape(2, 128, 128).transpose(1, 0, 2)
    a["L1_gates"] = np.concatenate([a.pop("L1_xattn_igate_kernel"), a.pop("L1_xattn_fgate_kernel")], axis=1
                                   ).reshape(3, 128, 8).transpose(1, 0, 2)
    a["L1_gate_bias"] = np.concatenate([a.pop("L1_xattn_igate_bias"), a.pop("L1_xattn_fgate_bias")]).reshape(8, 1)
    for n in ("gate", "up"):
        both = np.concatenate([a.pop(f"L1_ffn_expert_{n}_w").reshape(4, 128, 128),
                               a.pop(f"L1_ffn_shared_{n}_w")[None]])
        a[f"L1_{n}T"] = both.transpose(2, 0, 1)
    a["L1_downT"] = np.concatenate([a.pop("L1_ffn_expert_down_w").transpose(0, 2, 1).reshape(4, 128, 128),
                                    a.pop("L1_ffn_shared_down_w").T[None]]).transpose(1, 0, 2)
    a["L2_norms"] = np.stack([a.pop(f"L2_xattn_ln_{n}") for n in ("m_g", "m_b", "l_g", "l_b")], axis=1)
    wkv = a.pop("L2_xattn_Wkv")
    for n, w in (("WqT", a.pop("L2_xattn_Wq").T), ("WkT", wkv[:, :1024].T), ("WvT", wkv[:, 1024:].T),
                 ("Wout", a.pop("L2_xattn_Wout"))):
        a[f"L2_{n}"] = w.reshape(8, 128, 128).transpose(1, 0, 2)
    a["L2_w1T"] = a.pop("L2_ffn_fc1_w").reshape(8, 4, 128, 128).transpose(3, 0, 1, 2)
    a["L2_w2T"] = a.pop("L2_ffn_fc2_w").reshape(8, 128, 4, 128).transpose(3, 0, 2, 1)
    a["L2_b1T"] = a.pop("L2_ffn_fc1_b").reshape(8, 4, 128).transpose(2, 0, 1)
    def for_head(w, heads, mine):
        kept = np.zeros_like(w).reshape(128, -1, heads, 8)
        kept[:, :, mine, :] = w.reshape(128, -1, heads, 8)[:, :, mine, :]
        return kept.reshape(128, 128)
    a["L3_WqT"] = a.pop("L3_xattn_Wq").T
    wk = a.pop("L3_xattn_Wk").T
    a["L3_WkT"] = np.stack([for_head(wk, 4, r) for r in range(4)], axis=1)
    qkv = a.pop("L3_ffn_qkv_weight").reshape(4, 48, 128)
    a["L3b_WqT"] = qkv[:, :32].reshape(128, 128).T
    k4, v4 = (np.repeat(qkv[:, None, lo:lo + 8], 4, axis=1).reshape(128, 128).T for lo in (32, 40))
    a["L3b_WkT"] = k4
    a["L3b_head_of"] = np.tile(np.repeat(np.eye(4, dtype=np.float32), 8, axis=0), (4, 1))
    a["L3b_WvT"] = v4
    a["L3b_projT"] = a.pop("L3_ffn_proj_weight").T
    a["L3_norms"] = np.stack([a.pop(f"L3_ffn_{n}") for n in ("ln1_weight", "ln1_bias", "ln2_weight", "ln2_bias")], axis=1)
    a["L3_w1T"] = a.pop("L3_ffn_moe_w1").reshape(8, 128, 2, 128).transpose(1, 0, 2, 3)
    a["L3_w2T"] = a.pop("L3_ffn_moe_w2").reshape(8, 2, 128, 128).transpose(2, 0, 1, 3)
    a["routers"] = np.stack([a.pop("L0_ffn_gate_w").T, a.pop("L1_ffn_gate_w").T, a.pop("L2_ffn_router_w").T,
                             a.pop("L3_ffn_router_weight")], axis=1)
    return {n: np.ascontiguousarray(v) for n, v in a.items()}


def kernel(**inputs):
    import numpy as _np
    import concourse.bacc as _bacc
    from concourse import mybir as _mybir
    from concourse.bass_utils import run_bass_kernel_spmd as _run

    nc = _bacc.Bacc("TRN2", target_bir_lowering=False, num_devices=1)
    arrays = layouts(inputs)
    d = {n: nc.dram_tensor(n, a.shape, _mybir.dt.from_np(a.dtype), kind="ExternalInput").ap()
         for n, a in arrays.items()}
    out = nc.dram_tensor("out", arrays["x"].shape, _mybir.dt.float32, kind="ExternalOutput").ap()
    program(nc, d, out)
    r = _run(nc, [arrays], core_ids=[0])
    return r.results[0]["out"]
```

```python
from contextlib import ExitStack

import numpy as np

import concourse.bass as bass
from concourse import mybir

F32 = mybir.dt.float32
BF16 = mybir.dt.bfloat16
ALU = mybir.AluOpType
ACT = mybir.ActivationFunctionType
AX = mybir.AxisListType
ds = bass.ds

P = 128
NB = 32
D = 128
G4 = 4
NG = NB // G4
E = 8
BANK = 512
LN_EPS = 1e-5


class Chain:

    def __init__(self, eng, sem, base=0):
        self.eng, self.sem, self.base, self.n = eng, sem, base, 0

    def __call__(self, ins):
        ins.then_inc(self.sem, 1)
        self.n += 1
        self.eng.wait_ge(self.sem, self.base + self.n)

    def steps(self, n):
        assert self.n == n, (self.n, n)


def wait_apart(eng, sem):
    eng.sem_inc(sem, 1)


def per_row(ap, n):
    return ap.unsqueeze(2).to_broadcast([ap.shape[0], ap.shape[1], n])


def per_group(ap, n):
    return ap.unsqueeze(1).to_broadcast([ap.shape[0], n, ap.shape[1]])


class Shared:
    pass


class Stage:

    def __init__(self, held):
        self.sems, self.held = [], held


class Space:

    def __init__(self, nc, ctx, name, k=None):
        self.nc, self.ctx, self.name = nc, ctx, name
        self.sem_ctx = ctx
        if k is not None:
            self.sem_ctx = k.finals.enter_context(ExitStack())
            k.stages.append(Stage(self.sem_ctx))
            self.stage = k.stages[-1]

    def sb(self, name, shape, dt=F32):
        return self.ctx.enter_context(self.nc.sbuf_tensor(f"{self.name}_{name}", shape, dt))

    def ps(self, name, shape, dt=F32):
        return self.ctx.enter_context(self.nc.psum_tensor(f"{self.name}_{name}_ps", shape, dt))

    def sem(self, name):
        sem = self.sem_ctx.enter_context(self.nc.semaphore(f"{self.name}_{name}"))
        if self.sem_ctx is not self.ctx:
            self.stage.sems.append(sem)
        return sem


def zero_last_stage(block, k):
    if len(k.stages) < 2:
        return
    if len(k.stages) > 2:
        k.stages.pop(0).held.close()
    last = k.stages[0].sems

    @block.sync
    def _(sp):
        for sem in last:
            sp.sem_clear(sem)


def setup(nc, k):
    with ExitStack() as ctx:
        s = Space(nc, ctx, "setup", k)
        gates_raw = s.sb("gates_raw", [P, 8])
        x_in, gates_in, filled, made, tanh_done = (s.sem(n) for n in (
            "x_in", "gates_in", "filled", "made", "tanh_done"))
        with nc.Block() as block:
            zero_last_stage(block, k)

            @block.sync
            def _(sp):
                sp.dma_start(k.x[:, :, :], k.d["x"].rearrange("b p d -> p b d")).then_inc(x_in, 16)
                sp.dma_start(gates_raw[:, 0:4], k.d["g_xattn"].partition_broadcast(P)).then_inc(gates_in, 16)
                sp.dma_start(gates_raw[:, 4:8], k.d["g_ffn"].partition_broadcast(P)).then_inc(gates_in, 16)
                sp.dma_start(k.gates_w[:, :, :], k.d["routers"]).then_inc(x_in, 16)
                for f in (k.l0a_w, k.l0f_w, k.l1f_w, k.l3a_w, k.l3b_w):
                    f.start(sp)
                sp.wait_ge(x_in, 32)

            @block.scalar
            def _(act):
                act.wait_ge(gates_in, 32)
                act.activation(k.tg[:, :], gates_raw[:, :], ACT.Tanh).then_inc(tanh_done, 1)
                act.wait_ge(tanh_done, 1)

            @block.gpsimd
            def _(pool):
                pool.memset(k.ident[:, :], 0.0).then_inc(filled, 1)
                pool.memset(k.lower[:, :], 1.0).then_inc(filled, 1)
                pool.memset(k.upto[:, :], 1.0).then_inc(filled, 1)
                pool.memset(k.ones[:, :], 1.0).then_inc(filled, 1)
                pool.memset(k.neg_half[:, :], -0.5).then_inc(filled, 1)
                for e in range(E):
                    pool.memset(k.rank[:, e:e + 1], float(E - e)).then_inc(filled, 1)
                pool.wait_ge(filled, 5 + E)
                pool.affine_select(out=k.ident[:, :], in_=k.ident[:, :], compare_op=ALU.not_equal, fill=1.0,
                                   base=0, pattern=[[-1, P]], channel_multiplier=1).then_inc(made, 1)
                pool.affine_select(out=k.upto[:, :], in_=k.upto[:, :], compare_op=ALU.is_ge, fill=0.0,
                                   base=0, pattern=[[1, P]], channel_multiplier=-1).then_inc(made, 1)
                pool.affine_select(out=k.lower[:, :], in_=k.lower[:, :], compare_op=ALU.is_ge, fill=0.0,
                                   base=0, pattern=[[-1, P]], channel_multiplier=1).then_inc(made, 1)
                pool.wait_ge(made, 3)


class Fetched:

    def __init__(self, s, k, name):
        k.fetches.append(self)
        self.arrived, self.loads, self.started = s.sem(f"{name}_weights"), [], False

    def add(self, tile, src):
        self.loads.append((tile, src))
        return tile

    def start(self, eng):
        self.started = True
        for tile, src in self.loads:
            eng.dma_start(tile, src).then_inc(self.arrived, 16)

    def wait(self, eng):
        eng.wait_ge(self.arrived, 16 * len(self.loads))


def place_weights(s, k):
    d = k.d
    arena = s.sb("arena", [P, E * D + 2 * E * 4 * P])
    arena2 = s.sb("arena2", [P, 4 * 8 * P])

    def part(start, *shape, arena=arena):
        size = int(np.prod(shape))
        letters = "abc"[:len(shape)]
        flat = arena[:, start:start + size]
        if len(shape) == 1:
            return flat
        names = " ".join(letters)
        return flat.rearrange(f"p ({names}) -> p {names}", **dict(zip(letters, shape)))

    f = k.l0a_w = Fetched(s, k, "l0a")
    f.wq, f.wk, f.wv = (f.add(part(i * 8 * P, 8 * P), d[f"L0_xattn_W{n}"]) for i, n in enumerate("qkv"))
    f.wo = f.add(part(3 * 8 * P, 8, D), d["L0_xattn_Wo"].rearrange("(c p) n -> p c n", p=P))
    f.bv = f.add(part(4 * 8 * P, 8 * P), d["L0_xattn_bv"].partition_broadcast(P))
    f.bq, f.bk = (f.add(s.sb(f"l0a_b{n}", [P, 8])[:, :], d[f"L0_xattn_b{n}_cols"]) for n in "qk")
    f.bo = f.add(s.sb("l0a_bo", [1, D])[:, :], d["L0_xattn_bo"].rearrange("(o n) -> o n", o=1))

    f = k.l0f_w = Fetched(s, k, "l0f")
    f.w1, f.w2, f.w3 = (f.add(part(i * E * P, E, P, arena=arena2), d[f"L0_w{i + 1}T"]) for i in range(3))
    f.sw1, f.sw2, f.sw3 = (f.add(part((3 * E + 2 * i) * P, 2, P, arena=arena2), d[f"L0_sw{i + 1}T"]) for i in range(3))
    f.b1, f.b2, f.b3 = (f.add(s.sb(f"l0f_b{i}", [P, E])[:, :], d[f"L0_b{i}T"]) for i in (1, 2, 3))

    f = k.l1f_w = Fetched(s, k, "l1f")
    f.w_gate, f.w_up, f.w_down = (f.add(s.sb(f"l1f_{n}", [P, E // 2 + 1, P])[:, :, :], d[f"L1_{n}T"])
                                  for n in ("gate", "up", "down"))

    f = k.l2w_w = Fetched(s, k, "l2w")
    f.w = [f.add(part(i * 8 * P, 8, P, arena=arena2), d[n])
           for i, n in enumerate(("L2_WqT", "L2_WkT", "L2_WvT", "L2_Wout"))]
    f.norms = f.add(s.sb("l2_norms", [P, 4])[:, :], d["L2_norms"])

    f = k.l2f_w = Fetched(s, k, "l2f")
    f.w1, f.w2 = (f.add(part(E * D + i * E * 4 * P, E, 4, P), d[f"L2_w{i + 1}T"]) for i in range(2))
    f.scale_all = f.add(part(0, E, D), d["L2_ffn_layer_scale"].partition_broadcast(P))
    f.b1 = f.add(s.sb("l2f_b1", [P, E, 4])[:, :, :], d["L2_b1T"])
    f.scale8 = f.add(s.sb("l2f_scale8", [E, D])[:, :], d["L2_ffn_layer_scale"])
    f.bias8 = f.add(s.sb("l2f_bias8", [E, D])[:, :], d["L2_ffn_fc2_b"])

    f = k.l3a_w = Fetched(s, k, "l3a")
    f.wq = f.add(s.sb("l3a_wq", [P, P])[:, :], d["L3_WqT"])
    f.wk = f.add(s.sb("l3a_wk", [P, 4, P])[:, :, :], d["L3_WkT"])

    f = k.l3b_w = Fetched(s, k, "l3b")
    f.wq, f.wk, f.wv, f.proj = (f.add(s.sb(f"l3b_{n}", [P, P])[:, :], d[f"L3b_{n}T"]) for n in ("Wq", "Wk", "Wv", "proj"))
    f.head_of = f.add(s.sb("l3b_head_of", [P, 4])[:, :], d["L3b_head_of"])
    f.norms = f.add(s.sb("l3_norms", [P, 4])[:, :], d["L3_norms"])

    f = k.l3f_w = Fetched(s, k, "l3f")
    f.w1, f.w2 = (f.add(part(E * D + i * E * 4 * P, E, 2, P), d[f"L3_w{i + 1}T"]) for i in range(2))

    f = k.ctx_cols_w = Fetched(s, k, "ctx_cols")
    f.cols = k.rows[:, :, :].rearrange("p b d -> p (b d)")
    f.add(k.rows[:, :, :], d["ctxT"].rearrange("b p s -> p b s"))
    f = k.ctx_v_w = Fetched(s, k, "ctx_v")
    f.rows = f.add(part(0, NB, D), d["ctx"].rearrange("b p d -> p b d"))
    f = k.ctx_rows_w = Fetched(s, k, "ctx_rows")
    f.add(k.rows[:, :, :], d["ctx"].rearrange("b p d -> p b d"))


def normalise(nc, k, name, source="x", twice=False, gain=None, shift=None, keep_rows=False,
              gate_w=None, columns=None, logits=None, fetch=(), after=None, gains=None):
    columns = k.cols if columns is None else columns
    with ExitStack() as ctx:
        s = Space(nc, ctx, name, k)
        raw = {"x": k.x, "rows": k.rows}[source]
        stats = s.sb("stats", [P, NB, 6])
        mean, var, dif, rstd, rstd2, veps, veps2 = (s.sb(n, [P, NB]) for n in (
            "mean", "var", "dif", "rstd", "rstd2", "veps", "veps2"))
        halves = [slice(0, NB // 2), slice(NB // 2, NB)]
        stage = [s.sb(f"stage{i}", [P, G4, D]) for i in range(2)]
        BANKS = 4
        turned_ps = [s.ps(f"turned{i}", [P, BANK]) for i in range(BANKS)]
        logit_ps = [s.ps(f"logit{i}", [P, BANK]) for i in range(2)]
        (chain, veps_ready, rstd_ready, normed, turned, evacuated, logit_mm, logit_out, stats_done,
         apart, mean_ready) = (s.sem(n) for n in (
             "chain", "veps_ready", "rstd_ready", "normed", "turned", "evacuated", "logit_mm", "logit_out",
             "stats_done", "apart", "mean_ready"))
        in_rows = keep_rows and not twice and source != "rows"

        def normed_at(g):
            return k.rows[:, g * G4:(g + 1) * G4, :] if in_rows else stage[g % 2][:, :, :]

        with nc.Block() as block:
            zero_last_stage(block, k)

            @block.sync
            def _(sp):
                for f in fetch:
                    f.start(sp)

            @block.vector
            def _(dve):
                if after is not None:
                    after.wait(dve)
                link = Chain(dve, chain)
                for half in halves:
                    for t in range(half.start, half.stop):
                        dve.bn_stats(stats[:, t, :], raw[:, t, :]).then_inc(stats_done, 1)
                    dve.wait_ge(stats_done, half.stop)
                    even_mean, even_m2, odd_mean, odd_m2 = (stats[:, half, i] for i in (1, 2, 4, 5))
                    dve.tensor_tensor(dif[:, half], even_mean, odd_mean, ALU.subtract).then_inc(apart, 1)
                    dve.tensor_tensor(mean[:, half], even_mean, odd_mean, ALU.add).then_inc(apart, 1)
                    link(dve.tensor_tensor(var[:, half], even_m2, odd_m2, ALU.add))
                    dve.wait_ge(apart, 4 if half.start else 2)
                    dve.tensor_scalar(mean[:, half], mean[:, half], 0.5, None, ALU.mult).then_inc(mean_ready, 1)
                    link(dve.scalar_tensor_tensor(out=dif[:, half], in0=dif[:, half], scalar=0.25, in1=dif[:, half],
                                                  op0=ALU.mult, op1=ALU.mult))
                    link(dve.scalar_tensor_tensor(out=var[:, half], in0=var[:, half], scalar=1.0 / D,
                                                  in1=dif[:, half], op0=ALU.mult, op1=ALU.add))
                    dve.tensor_scalar(veps[:, half], var[:, half], LN_EPS, None, ALU.add).then_inc(veps_ready, 1)
                scale = rstd
                if twice:
                    for i, half in enumerate(halves):
                        dve.wait_ge(rstd_ready, i + 1)
                        link(dve.tensor_tensor(dif[:, half], var[:, half], rstd[:, half], ALU.mult))
                        link(dve.tensor_tensor(dif[:, half], dif[:, half], rstd[:, half], ALU.mult))
                        dve.tensor_scalar(veps2[:, half], dif[:, half], LN_EPS, None, ALU.add).then_inc(veps_ready, 1)
                        if keep_rows:
                            for t in range(half.start, half.stop):
                                if t == half.start:
                                    dve.wait_ge(mean_ready, i + 1)
                                dve.tensor_scalar(k.rows[:, t, :], raw[:, t, :], mean[:, t:t + 1], rstd[:, t:t + 1],
                                                  ALU.subtract, ALU.mult).then_inc(stats_done, 1)
                    scale = rstd2
                for g in range(NG):
                    if g % (NG // 2) == 0:
                        i = g // (NG // 2)
                        dve.wait_ge(mean_ready, i + 1)
                        dve.wait_ge(rstd_ready, i + 3 if twice else i + 1)
                        if twice:
                            link(dve.tensor_tensor(rstd2[:, halves[i]], rstd2[:, halves[i]], rstd[:, halves[i]], ALU.mult))
                    if not in_rows and g >= 2:
                        dve.wait_ge(turned, g - 1)
                    for j in range(G4):
                        t = g * G4 + j
                        dve.tensor_scalar(normed_at(g)[:, j, :], raw[:, t, :], mean[:, t:t + 1], scale[:, t:t + 1],
                                          ALU.subtract, ALU.mult).then_inc(normed, 1)
                if gate_w is not None:
                    for half in range(2):
                        dve.wait_ge(logit_mm, NG // 2 * (half + 1))
                        dve.tensor_copy(logits[:, half * NB // 2:(half + 1) * NB // 2, :],
                                        logit_ps[half][:, 0:NB // 2 * E].rearrange("p (t e) -> p t e", e=E)
                                        ).then_inc(logit_out, 1)

            @block.tensor
            def _(pe):
                def turn(g):
                    pe.wait_ge(normed, (g + 1) * G4)
                    if g >= BANKS:
                        pe.wait_ge(evacuated, g - BANKS + 1)
                    for j in range(G4):
                        ins = pe.transpose(turned_ps[g % BANKS][:, j * P:(j + 1) * P], normed_at(g)[:, j, :], k.ident[:, :])
                    ins.then_inc(turned, 1)

                def route(g):
                    pe.wait_ge(evacuated, g + 1)
                    for t in range(g * G4, (g + 1) * G4):
                        at = t % (NB // 2)
                        ins = pe.matmul(logit_ps[t // (NB // 2)][:, at * E:(at + 1) * E], columns[:, t * P:(t + 1) * P],
                                        gate_w, start=True, stop=True)
                    ins.then_inc(logit_mm, 1)
                for g in range(NG):
                    turn(g)
                    if gate_w is not None and g:
                        route(g - 1)
                if gate_w is not None:
                    route(NG - 1)

            @block.scalar
            def _(act):
                if gain is not None:
                    gains.wait(act)
                for g in range(NG):
                    act.wait_ge(turned, g + 1)
                    place = columns[:, g * BANK:(g + 1) * BANK]
                    if gain is None:
                        act.activation(place, turned_ps[g % BANKS][:, :], ACT.Copy).then_inc(evacuated, 1)
                    else:
                        act.activation(place, turned_ps[g % BANKS][:, :], ACT.Identity,
                                       scale=gain, bias=shift).then_inc(evacuated, 1)

            @block.gpsimd
            def _(pool):
                for i, half in enumerate(halves):
                    pool.wait_ge(veps_ready, i + 1)
                    pool.tensor_tensor(rstd[:, half], veps[:, half], k.neg_half[:, half], ALU.pow
                                       ).then_inc(rstd_ready, 1)
                if twice:
                    for i, half in enumerate(halves):
                        pool.wait_ge(veps_ready, i + 3)
                        pool.tensor_tensor(rstd2[:, half], veps2[:, half], k.neg_half[:, half], ALU.pow
                                           ).then_inc(rstd_ready, 1)


def l0_attention(nc, k):
    H, DK = 16, 64
    C = H * DK // P
    SC = 1.0 / DK ** 0.5
    with ExitStack() as ctx:
        s = Space(nc, ctx, "l0a", k)
        w = k.l0a_w
        wq, wk, wv, wo, bq, bk, bv, bo = w.wq, w.wk, w.wv, w.wo, w.bq, w.bk, w.bv, w.bo
        k_in = s.sb("k_in", [P, P])
        v_in = s.sb("v_in", [P, P])
        qT, kT = s.sb("qT", [P, C, P]), s.sb("kT", [P, C, P])
        v = s.sb("v", [P, H, DK])
        probs = s.sb("probs", [P, H, P])
        oT = s.sb("oT", [P, C, P])
        mx, nm, sums, inv = (s.sb(n, [P, H]) for n in ("mx", "nm", "sums", "inv"))
        score = [s.ps(f"score{i}", [P, BANK]) for i in range(4)]
        proj = [s.ps(f"proj{i}", [P, BANK]) for i in range(2)]
        y_ps = s.ps("y", [P, BANK])
        (kin_in, vin_in, s_mm, v_mm, q_mm, k_mm, av_mm, y_mm, nm_ready, probs_done, v_out, q_ready,
         k_ready, v_ready, o_ready, y_used, chain) = (s.sem(n) for n in (
             "kin_in", "vin_in", "s_mm", "v_mm", "q_mm", "k_mm", "av_mm", "y_mm", "nm_ready",
             "probs_done", "v_out", "q_ready", "k_ready", "v_ready", "o_ready", "y_used", "chain"))

        def heads(g):
            half, odd = g // 2, g % 2
            return [(8 * half + 2 * i + odd, 4 * half + i, i, 64 * odd) for i in range(4)]

        with nc.Block() as block:
            zero_last_stage(block, k)

            @block.sync
            def _(sp):
                with sp.Fori(0, NB) as b:
                    sp.wait_ge(k_mm, 2 * b)
                    sp.dma_start(k_in[:, :], k.d["ctxT"][ds(b, 1), :, :].rearrange("o p d -> (o p) d")
                                 ).then_inc(kin_in, 16)
                    sp.wait_ge(v_mm, 2 * b)
                    sp.dma_start(v_in[:, :], k.d["ctxT"][ds(b, 1), :, :].rearrange("o p d -> (o p) d")
                                 ).then_inc(vin_in, 16)
                sp.wait_ge(k_mm, 2 * NB)
                sp.dma_start(k_in[:, :], k.d["ctxT"][0, :, :]).then_inc(kin_in, 16)

            @block.tensor
            def _(pe):
                def project_q(n, first):
                    for half in range(2):
                        if not first:
                            pe.wait_ge(v_out, 2 * (n - 1) + half + 1)
                        for i in range(4):
                            c = 4 * half + i
                            ins = pe.matmul(proj[half][:, i * P:(i + 1) * P], wq[:, c * P:(c + 1) * P],
                                            k.cols[:, ds((n % NB) * P, P)], start=True, stop=True)
                        ins.then_inc(q_mm, 1)

                def project_k(n):
                    pe.wait_ge(kin_in, 16 * (n + 1))
                    for half in range(2):
                        pe.wait_ge(q_ready, 2 * n + half + 1)
                        for i in range(4):
                            c = 4 * half + i
                            ins = pe.matmul(proj[half][:, i * P:(i + 1) * P], wk[:, c * P:(c + 1) * P],
                                            k_in[:, :], start=True, stop=True)
                        ins.then_inc(k_mm, 1)

                w.wait(pe)
                project_q(0, True)
                project_k(0)
                with pe.Fori(0, NB) as b:
                    pe.wait_ge(q_ready, 2 * (b + 1))
                    pe.wait_ge(k_ready, 2 * (b + 1))
                    for g in range(4):
                        for h, c, i, p0 in heads(g):
                            ins = pe.matmul(score[g][:, i * P:(i + 1) * P], kT[p0:p0 + DK, c, :],
                                            qT[p0:p0 + DK, c, :], start=True, stop=True)
                        ins.then_inc(s_mm, 1)
                    pe.wait_ge(vin_in, 16 * (b + 1))
                    for half in range(2):
                        pe.matmul(proj[half][:, :], v_in[:, :], wv[:, half * BANK:(half + 1) * BANK],
                                  start=True, stop=True).then_inc(v_mm, 1)
                    project_q(b + 1, False)
                    project_k(b + 1)
                    pe.wait_ge(probs_done, H * (b + 1))
                    pe.wait_ge(v_ready, b + 1)
                    for half in range(2):
                        for i in range(4):
                            c = 4 * half + i
                            for odd in range(2):
                                ins = pe.matmul(score[half][64 * odd:64 * odd + DK, i * P:(i + 1) * P],
                                                v[:, 2 * c + odd, :], probs[:, 2 * c + odd, :], start=True, stop=True)
                        ins.then_inc(av_mm, 1)
                    pe.wait_ge(y_used, b)
                    pe.matmul(y_ps[:, 0:D], k.ones[0:1, :], bo[:, :], start=True, stop=False)
                    for c in range(C):
                        if c % 4 == 0:
                            pe.wait_ge(o_ready, 2 * b + c // 4 + 1)
                        ins = pe.matmul(y_ps[:, 0:D], oT[:, c, :], wo[:, c, :], start=False, stop=(c == C - 1))
                    ins.then_inc(y_mm, 1)

            @block.scalar
            def _(act):
                def evacuate_k(n):
                    for c in range(C):
                        if c % 4 == 0:
                            act.wait_ge(k_mm, 2 * n + c // 4 + 1)
                        ins = act.activation(kT[:, c, :], proj[c // 4][:, (c % 4) * P:(c % 4 + 1) * P],
                                             ACT.Identity, bias=bk[:, c:c + 1])
                        if c % 4 == 3:
                            ins.then_inc(k_ready, 1)

                w.wait(act)
                evacuate_k(0)
                with act.Fori(0, NB) as b:
                    act.wait_ge(av_mm, 2 * b)
                    for g in range(4):
                        act.wait_ge(nm_ready, 4 * b + g + 1)
                        for h, c, i, p0 in heads(g):
                            act.activation(probs[:, h, :], score[g][:, i * P:(i + 1) * P], ACT.Exp,
                                           bias=nm[:, h:h + 1], scale=SC, accum_out=sums[:, h:h + 1]
                                           ).then_inc(probs_done, 1)
                    evacuate_k(b + 1)
                    for half in range(2):
                        act.wait_ge(av_mm, 2 * b + half + 1)
                        act.activation(oT[:, 4 * half:4 * half + 4, :],
                                       score[half][:, :].rearrange("p (c n) -> p c n", c=4), ACT.Copy
                                       ).then_inc(o_ready, 1)

            @block.vector
            def _(dve):
                def evacuate_q(n):
                    for half in range(2):
                        dve.wait_ge(q_mm, 2 * n + half + 1)
                        dve.tensor_tensor(qT[:, 4 * half:4 * half + 4, :],
                                          proj[half][:, :].rearrange("p (c n) -> p c n", c=4),
                                          per_row(bq[:, 4 * half:4 * half + 4], P), ALU.add).then_inc(q_ready, 1)

                w.wait(dve)
                evacuate_q(0)
                STEPS = 5
                with dve.Fori(0, NB) as b:
                    link = Chain(dve, chain, b * STEPS)
                    for g in range(4):
                        first = 8 * (g // 2) + g % 2
                        dve.wait_ge(s_mm, 4 * b + g + 1)
                        link(dve.tensor_reduce(mx[:, first:first + 7:2],
                                               score[g][:, :].rearrange("p (h n) -> p h n", h=4), AX.X, ALU.max))
                        dve.tensor_scalar(nm[:, first:first + 7:2], mx[:, first:first + 7:2], -SC, None, ALU.mult
                                          ).then_inc(nm_ready, 1)
                    for half in range(2):
                        dve.wait_ge(v_mm, 2 * b + half + 1)
                        dve.tensor_tensor(v[:, 8 * half:8 * half + 8, :],
                                          proj[half][:, :].rearrange("p (h n) -> p h n", h=8),
                                          bv[:, half * BANK:(half + 1) * BANK].rearrange("p (h n) -> p h n", h=8),
                                          ALU.add).then_inc(v_out, 1)
                    evacuate_q(b + 1)
                    dve.wait_ge(probs_done, H * (b + 1))
                    link(dve.reciprocal(inv[:, :], sums[:, :]))
                    dve.wait_ge(v_out, 2 * (b + 1))
                    dve.tensor_tensor(v[:, :, :], v[:, :, :], per_row(inv[:, :], DK), ALU.mult).then_inc(v_ready, 1)
                    dve.wait_ge(y_mm, b + 1)
                    xt = k.x[:, ds(b, 1), :].rearrange("p o d -> p (o d)")
                    dve.scalar_tensor_tensor(out=xt, in0=y_ps[:, 0:D], scalar=k.tg[:, 0:1], in1=xt,
                                             op0=ALU.mult, op1=ALU.add).then_inc(y_used, 1)
                    link.steps(STEPS)


def top_two(link, dve, k, p, rest, eq, first, best, sel):
    for i, src in enumerate((p, rest)):
        link(dve.tensor_reduce(best[i][:, :], src[:, :, :], AX.X, ALU.max))
        link(dve.tensor_tensor(eq[:, :, :], src[:, :, :], per_row(best[i][:, :], E), ALU.is_equal))
        link(dve.tensor_tensor(eq[:, :, :], eq[:, :, :], per_group(k.rank[:, :], NB), ALU.mult))
        link(dve.tensor_reduce(first[:, :], eq[:, :, :], AX.X, ALU.max))
        link(dve.tensor_tensor(sel[i][:, :, :], eq[:, :, :], per_row(first[:, :], E), ALU.is_equal))
        if i == 0:
            link(dve.scalar_tensor_tensor(out=rest[:, :, :], in0=sel[0][:, :, :], scalar=-1e9, in1=p[:, :, :],
                                          op0=ALU.mult, op1=ALU.add))


def l0_route(nc, k):
    with ExitStack() as ctx:
        s = Space(nc, ctx, "l0r", k)
        p, work, eq, mask = (s.sb(n, [P, NB, E]) for n in ("p", "work", "eq", "mask"))
        sel = [s.sb(f"sel{i}", [P, NB, E]) for i in range(2)]
        best = [s.sb(f"best{i}", [P, NB]) for i in range(2)]
        red = s.sb("red", [P, NB])
        turned_ps = [s.ps(f"turned{i}", [P, BANK]) for i in range(8)]
        chain, shifted, exped, mask_ready, turned = (s.sem(n) for n in (
            "chain", "shifted", "exped", "mask_ready", "turned"))
        with nc.Block() as block:
            zero_last_stage(block, k)

            @block.vector
            def _(dve):
                link = Chain(dve, chain)
                link(dve.tensor_reduce(red[:, :], k.logits[:, :, :], AX.X, ALU.max))
                dve.tensor_tensor(p[:, :, :], k.logits[:, :, :], per_row(red[:, :], E), ALU.subtract).then_inc(shifted, 1)
                dve.wait_ge(exped, 1)
                link(dve.tensor_reduce(red[:, :], p[:, :, :], AX.X, ALU.add))
                link(dve.reciprocal(red[:, :], red[:, :]))
                link(dve.tensor_tensor(p[:, :, :], p[:, :, :], per_row(red[:, :], E), ALU.mult))
                top_two(link, dve, k, p, work, eq, red, best, sel)
                link(dve.tensor_tensor(mask[:, :, :], sel[0][:, :, :], sel[1][:, :, :], ALU.add))
                dve.tensor_tensor(k.weight[:, :, :], p[:, :, :], mask[:, :, :], ALU.mult).then_inc(mask_ready, 1)
                dve.wait_ge(mask_ready, 1)
                for g in range(NG):
                    dve.wait_ge(turned, g + 1)
                    ins = dve.tensor_copy(k.mask_rows[:, g * BANK:(g + 1) * BANK], turned_ps[g][0:E, :])
                ins.then_inc(mask_ready, 1)
                dve.wait_ge(mask_ready, 2)

            @block.scalar
            def _(act):
                act.wait_ge(shifted, 1)
                act.activation(p[:, :, :], p[:, :, :], ACT.Exp).then_inc(exped, 1)

            @block.tensor
            def _(pe):
                pe.wait_ge(mask_ready, 1)
                for g in range(NG):
                    for j in range(G4):
                        ins = pe.transpose(turned_ps[g][0:E, j * P:(j + 1) * P], mask[:, g * G4 + j, :], k.ident[:, :])
                    ins.then_inc(turned, 1)


def l0_mixture(nc, k):
    SH = 2
    HU = SH + E
    with ExitStack() as ctx:
        s = Space(nc, ctx, "l0f", k)
        w = k.l0f_w
        w1, w2, w3, sw1, sw2, sw3, b1, b2, b3 = w.w1, w.w2, w.w3, w.sw1, w.sw2, w.sw3, w.b1, w.b2, w.b3
        picker = s.sb("picker", [E, E, P], BF16)
        xs = [s.sb(f"xs{i}", [P, G4, D]) for i in range(2)]
        xsT = [s.sb(f"xsT{i}", [P, BANK]) for i in range(2)]
        hidden, x3, z, acc = (s.sb(n, [P, BANK]) for n in ("hidden", "x3", "z", "acc"))
        s_gate = s.sb("s_gate", [P, SH, BANK])
        s_hidden = s.sb("s_hidden", [P, SH, BANK])
        xsT_ps, h_ps, x3_ps, x2_ps, m_ps, y_ps = (s.ps(n, [P, BANK]) for n in (
            "xsT", "h", "x3", "x2", "m", "y"))
        (picker_filled, picker_made, xs_ready, xsT_mm, h_mm, x3_mm, x2_mm, m_mm, y_mm, silu_done,
         xsT_ready, x3_ready, shared_ready, x2_out, masked, summed, y_used) = (s.sem(n) for n in (
             "picker_filled", "picker_made", "xs_ready", "xsT_mm", "h_mm", "x3_mm", "x2_mm", "m_mm",
             "y_mm", "silu_done", "xsT_ready", "x3_ready", "shared_ready", "x2_out", "masked", "summed",
             "y_used"))
        with nc.Block() as block:
            zero_last_stage(block, k)

            @block.gpsimd
            def _(pool):
                pool.memset(picker[:, :, :], 1.0).then_inc(picker_filled, 1)
                pool.wait_ge(picker_filled, 1)
                pool.affine_select(out=picker[:, :, :], in_=picker[:, :, :], compare_op=ALU.is_equal, fill=0.0,
                                   base=0, pattern=[[-1, E], [0, P]], channel_multiplier=1).then_inc(picker_made, 1)
                with pool.Fori(0, NG) as g:
                    for e in range(E):
                        pool.wait_ge(xsT_mm, g * E + max(e - 1, 0))
                        pool.tensor_tensor(xs[e % 2][:, :, :], k.rows[:, ds(g * G4, G4), :],
                                           k.weight[:, ds(g * G4, G4), e:e + 1].to_broadcast([P, G4, D]), ALU.mult
                                           ).then_inc(xs_ready, 1)

            @block.tensor
            def _(pe):
                w.wait(pe)
                pe.wait_ge(picker_made, 1)
                with pe.Fori(0, NG) as g:
                    cols = k.cols[:, ds(g * BANK, BANK)]

                    def turn(e):
                        pe.wait_ge(xs_ready, g * E + e + 1)
                        pe.wait_ge(xsT_ready, g * E + e)
                        for j in range(G4):
                            ins = pe.transpose(xsT_ps[:, j * P:(j + 1) * P], xs[e % 2][:, j, :], k.ident[:, :])
                        ins.then_inc(xsT_mm, 1)

                    for c in range(SH):
                        pe.wait_ge(silu_done, g * HU + c)
                        pe.matmul(h_ps[:, :], sw1[:, c, :], cols, start=True, stop=True).then_inc(h_mm, 1)
                        if c == 0:
                            pe.wait_ge(x3_ready, g * E)
                        else:
                            pe.wait_ge(shared_ready, g * SH + c)
                        pe.matmul(x3_ps[:, :], sw2[:, c, :], cols, start=True, stop=True).then_inc(x3_mm, 1)
                    turn(0)
                    pe.wait_ge(x2_out, g * (E + 1))
                    for c in range(SH):
                        pe.wait_ge(shared_ready, g * SH + c + 1)
                        ins = pe.matmul(x2_ps[:, :], sw3[:, c, :], s_hidden[:, c, :], start=(c == 0), stop=(c == SH - 1))
                    ins.then_inc(x2_mm, 1)
                    for e in range(E):
                        pe.wait_ge(xsT_ready, g * E + e + 1)
                        pe.wait_ge(silu_done, g * HU + SH + e)
                        pe.matmul(h_ps[:, :], w1[:, e, :], xsT[e % 2][:, :], start=True, stop=True).then_inc(h_mm, 1)
                        if e + 1 < E:
                            turn(e + 1)
                        pe.wait_ge(x3_ready, g * E + e)
                        pe.matmul(x3_ps[:, :], w3[:, e, :], xsT[e % 2][:, :], start=True, stop=True).then_inc(x3_mm, 1)
                        pe.wait_ge(masked, g * E + e)
                        wait_apart(pe, k.waited_pe)
                        pe.matmul(m_ps[:, :], picker[:, e, :], k.mask_rows[:, ds(g * BANK, BANK)],
                                  start=True, stop=True).then_inc(m_mm, 1)
                        pe.wait_ge(silu_done, g * HU + SH + e + 1)
                        pe.wait_ge(x2_out, g * (E + 1) + e + 1)
                        pe.matmul(x2_ps[:, :], w2[:, e, :], hidden[:, :], start=True, stop=True).then_inc(x2_mm, 1)
                    pe.wait_ge(summed, (g + 1) * (E + 1))
                    pe.wait_ge(y_used, g)
                    for j in range(G4):
                        ins = pe.transpose(y_ps[:, j * P:(j + 1) * P], acc[:, j * P:(j + 1) * P], k.ident[:, :])
                    ins.then_inc(y_mm, 1)

            @block.scalar
            def _(act):
                w.wait(act)
                with act.Fori(0, NG) as g:
                    def evacuate_xs(e):
                        act.wait_ge(xsT_mm, g * E + e + 1)
                        act.wait_ge(x3_mm, g * HU + (SH + e - 1 if e >= 2 else 0))
                        act.activation(xsT[e % 2][:, :], xsT_ps[:, :], ACT.Copy).then_inc(xsT_ready, 1)

                    for c in range(SH):
                        act.wait_ge(h_mm, g * HU + c + 1)
                        act.activation(s_gate[:, c, :], h_ps[:, :], ACT.Silu).then_inc(silu_done, 1)
                    evacuate_xs(0)
                    for e in range(E):
                        act.wait_ge(h_mm, g * HU + SH + e + 1)
                        act.activation(hidden[:, :], h_ps[:, :], ACT.Silu, bias=b1[:, e:e + 1]).then_inc(silu_done, 1)
                        if e + 1 < E:
                            evacuate_xs(e + 1)
                        act.wait_ge(x3_mm, g * HU + SH + e + 1)
                        act.wait_ge(x2_out, g * (E + 1) + e + 1)
                        act.activation(x3[:, :], x3_ps[:, :], ACT.Identity, bias=b3[:, e:e + 1]).then_inc(x3_ready, 1)

            @block.vector
            def _(dve):
                w.wait(dve)
                with dve.Fori(0, NG) as g:
                    for c in range(SH):
                        dve.wait_ge(silu_done, g * HU + c + 1)
                        dve.wait_ge(x3_mm, g * HU + c + 1)
                        dve.tensor_tensor(s_hidden[:, c, :], x3_ps[:, :], s_gate[:, c, :], ALU.mult
                                          ).then_inc(shared_ready, 1)
                    dve.wait_ge(x2_mm, g * (E + 1) + 1)
                    dve.wait_ge(y_mm, g)
                    dve.tensor_copy(acc[:, :], x2_ps[:, :]).then_inc(x2_out, 1)
                    dve.wait_ge(x2_out, g * (E + 1) + 1)
                    dve.sem_inc(summed, 1)
                    for e in range(E):
                        dve.wait_ge(x2_mm, g * (E + 1) + e + 2)
                        dve.wait_ge(x3_ready, g * E + e + 1)
                        dve.wait_ge(summed, g * (E + 1) + e + 1)
                        dve.scalar_tensor_tensor(out=z[:, :], in0=x2_ps[:, :], scalar=b2[:, e:e + 1], in1=x3[:, :],
                                                 op0=ALU.add, op1=ALU.mult).then_inc(x2_out, 1)
                        dve.wait_ge(m_mm, g * E + e + 1)
                        dve.wait_ge(x2_out, g * (E + 1) + e + 2)
                        dve.tensor_tensor(z[:, :], z[:, :], m_ps[:, :], ALU.mult).then_inc(masked, 1)
                        dve.wait_ge(masked, g * E + e + 1)
                        dve.tensor_tensor(acc[:, :], acc[:, :], z[:, :], ALU.add).then_inc(summed, 1)
                    dve.wait_ge(y_mm, g + 1)
                    xt = k.x[:, ds(g * G4, G4), :]
                    dve.scalar_tensor_tensor(out=xt, in0=y_ps[:, :].rearrange("p (t d) -> p t d", t=G4),
                                             scalar=k.tg[:, 4:5], in1=xt, op0=ALU.mult, op1=ALU.add
                                             ).then_inc(y_used, 1)



def l1_gates(nc, k):
    NH = 4
    with ExitStack() as ctx:
        s = Space(nc, ctx, "l1g", k)
        ctx_cols = k.ctx_cols_w.cols
        w = s.sb("w", [P, 3, 2 * NH])
        bias = s.sb("bias", [2 * NH, 1])
        gates = s.sb("gates", [2 * NH, NB * P])
        ig, fg, size, low, cum, a, top, neg, em = (s.sb(n, [P, P]) for n in (
            "ig", "fg", "size", "low", "cum", "a", "top", "neg", "em"))
        ps = [s.ps(f"gate{i}", [P, BANK]) for i in range(8)]
        (loaded, gate_mm, gate_out, spread, chain, sized, softened, ready, turned, copied, neg_out) = (
            s.sem(n) for n in ("loaded", "gate_mm", "gate_out", "spread", "chain", "sized", "softened", "ready",
                               "turned", "copied", "neg_out"))
        with nc.Block() as block:
            zero_last_stage(block, k)

            @block.sync
            def _(sp):
                sp.dma_start(w[:, :, :], k.d["L1_gates"]).then_inc(loaded, 16)
                sp.dma_start(bias[:, :], k.d["L1_gate_bias"]).then_inc(loaded, 16)
                sp.wait_ge(gate_out, NG)
                for dst, h0 in ((ig, 0), (fg, NH)):
                    for h in range(NH):
                        sp.dma_start(dst[h:P:NH, :],
                                     gates[h0 + h:h0 + h + 1, :].rearrange("o (b s) -> o b s", b=NB)
                                     ).then_inc(spread, 16)
                sp.wait_ge(ready, 1)
                sp.dma_start(k.neg_top, neg[:, :]).then_inc(neg_out, 16)
                sp.wait_ge(neg_out, 16)

            @block.tensor
            def _(pe):
                k.ctx_cols_w.wait(pe)
                pe.wait_ge(loaded, 32)
                for g in range(NG):
                    cols = slice(g * BANK, (g + 1) * BANK)
                    pe.matmul(ps[g][0:2 * NH, :], w[:, 0, :], k.cols[:, cols], start=True, stop=False)
                    pe.matmul(ps[g][0:2 * NH, :], w[:, 1, :], ctx_cols[:, cols], start=False, stop=False)
                    pe.matmul(ps[g][0:2 * NH, :], w[:, 2, :], ctx_cols[:, cols], start=False, stop=True
                              ).then_inc(gate_mm, 1)
                pe.wait_ge(ready, 1)
                pe.transpose(ps[0][:, 0:P], a[:, :], k.ident[:, :]).then_inc(turned, 1)
                pe.wait_ge(ready, 2)
                pe.transpose(ps[1][:, 0:P], em[:, :], k.ident[:, :]).then_inc(turned, 1)

            @block.scalar
            def _(act):
                act.wait_ge(sized, 1)
                act.activation(size[:, :], size[:, :], ACT.Exp, scale=-1.0).then_inc(softened, 1)
                act.wait_ge(softened, 1)
                act.activation(size[:, :], size[:, :], ACT.Ln, bias=1.0).then_inc(softened, 1)
                act.wait_ge(ready, 1)
                act.activation(em[:, :], top[:, :], ACT.Exp, scale=-1.0).then_inc(ready, 1)

            @block.vector
            def _(dve):
                dve.wait_ge(loaded, 32)
                for g in range(NG):
                    dve.wait_ge(gate_mm, g + 1)
                    dve.tensor_scalar(gates[:, g * BANK:(g + 1) * BANK], ps[g][0:2 * NH, :], bias[:, 0:1], None,
                                      ALU.add).then_inc(gate_out, 1)
                dve.wait_ge(spread, 16 * 2 * NH)
                link = Chain(dve, chain)
                link(dve.tensor_scalar(low[:, :], fg[:, :], 0.0, None, ALU.min))
                link(dve.tensor_scalar(size[:, :], fg[:, :], 0.0, None, ALU.max))
                dve.tensor_tensor(size[:, :], size[:, :], low[:, :], ALU.subtract).then_inc(sized, 1)
                dve.wait_ge(softened, 2)
                link(dve.tensor_tensor(low[:, :], low[:, :], size[:, :], ALU.subtract))
                link(dve.tensor_tensor_scan(cum[:, :], k.ones[:, :], low[:, :], 0.0, ALU.mult, ALU.add))
                link(dve.tensor_tensor(a[:, :], ig[:, :], cum[:, :], ALU.subtract))
                link(dve.tensor_tensor_scan(top[:, :], a[:, :], a[:, :], -3e38, ALU.max, ALU.max))
                link(dve.tensor_scalar(neg[:, :], top[:, :], -1.0, None, ALU.mult))
                dve.tensor_tensor(top[:, :], top[:, :], cum[:, :], ALU.add).then_inc(ready, 1)
                for i, dst in enumerate((k.aT, k.emT)):
                    dve.wait_ge(turned, i + 1)
                    dve.tensor_copy(dst[:, :], ps[i][:, 0:P]).then_inc(copied, 1)
                dve.wait_ge(copied, 2)


def l1_attention(nc, k):
    NH, HD = 4, 32
    with ExitStack() as ctx:
        s = Space(nc, ctx, "l1a", k)
        two = range(2)
        k_in = [s.sb(f"k_in{i}", [P, P]) for i in two]
        v_in = [s.sb(f"v_in{i}", [P, NH, HD + 1]) for i in two]
        m_in = [s.sb(f"m_in{i}", [1, NH * P]) for i in two]
        q_heads = [s.sb(f"q_heads{i}", [P, NH, P]) for i in two]
        head_scale = s.sb("head_scale", [P, NH])
        future = s.sb("future", [P, NH, P], BF16)
        ident16 = s.sb("ident16", [P, P], BF16)
        decay = [s.sb(f"decay{i}", [P, NH, P]) for i in two]
        c = [s.sb(f"c{i}", [P, NH, P]) for i in two]
        rms = s.sb("rms", [P, HD])
        out_scale = s.sb("out_scale", [P, NH, HD])
        den, inv, ss, rs = (s.sb(n, [P, NH]) for n in ("den", "inv", "ss", "rs"))
        hid, sq = s.sb("hid", [P, NH, HD]), s.sb("sq", [P, NH, HD])
        m_ps = s.ps("m", [P, BANK])
        s_ps = [s.ps(f"s{i}", [P, BANK]) for i in two]
        o_ps = [s.ps(f"o{i}", [P, BANK]) for i in two]
        m_loaded = [s.sem(f"m_loaded{i}") for i in two]
        (w_in, filled, made, scale_made, k_ready, q_ready, m_mm, s_mm, av_mm, e_ready, d_ready, c_ready, v_ready,
         n1_done, var_ready, rs_ready, chain) = (s.sem(n) for n in (
             "w_in", "filled", "made", "scale_made", "k_ready", "q_ready", "m_mm", "s_mm", "av_mm", "e_ready", "d_ready",
             "c_ready", "v_ready", "n1_done", "var_ready", "rs_ready", "chain"))

        def loads_by(n, i):
            return (n - i) * 8 + 16

        def schedule(eng, a_step, c_step, n1_step, n2_step, a_first=False):
            a_step(0, 0)
            a_step(1, 1)
            c_step(0, 0)
            with eng.Fori(0, NB // 2) as q:
                for u in two:
                    b = q * 2 + (u + 1)
                    c_step(b, 1 - u)
                    if a_first:
                        a_step(q * 2 + (u + 2), u)
                    n1_step(q * 2 + u, u)
                    if not a_first:
                        a_step(q * 2 + (u + 2), u)
                    n2_step(q * 2 + u, u)

        def before(n, m):
            return None if isinstance(n, int) and n - m < 1 else n - m

        def nothing(n, i):
            pass

        with nc.Block() as block:
            zero_last_stage(block, k)

            @block.sync
            def _(sp):
                sp.dma_start(rms[:, :], k.d["L1_xattn_rms_scale"].partition_broadcast(P)).then_inc(w_in, 16)

                def load(n, i):
                    if before(n, 1) is not None:
                        sp.wait_ge(m_mm, n - 1)
                    sp.dma_start(m_in[i][:, :], k.neg_top[ds((n % NB) * NH, NH), :].rearrange("(o h) s -> o (h s)", o=1)
                                 ).then_inc(m_loaded[i], 16)
                schedule(sp, load, nothing, nothing, nothing)

            @block.gpsimd
            def _(pool):
                for i in two:
                    pool.memset(v_in[i][:, :, :], 1.0).then_inc(filled, 1)
                pool.memset(head_scale[:, :], HD ** -0.5).then_inc(filled, 1)
                pool.memset(future[:, :, :], 0.0).then_inc(filled, 1)
                pool.tensor_copy(ident16[:, :], k.ident[:, :]).then_inc(filled, 1)
                pool.wait_ge(filled, 5)
                pool.affine_select(out=head_scale[:, :], in_=head_scale[:, :], compare_op=ALU.is_ge, fill=0.0,
                                   base=0, pattern=[[-HD, NH]], channel_multiplier=1).then_inc(made, 1)
                pool.wait_ge(made, 1)
                pool.affine_select(out=head_scale[:, :], in_=head_scale[:, :], compare_op=ALU.is_ge, fill=0.0,
                                   base=HD - 1, pattern=[[HD, NH]], channel_multiplier=-1).then_inc(made, 1)
                pool.affine_select(out=future[:, :, :], in_=future[:, :, :], compare_op=ALU.is_ge, fill=-1e30,
                                   base=0, pattern=[[0, NH], [1, P]], channel_multiplier=-1).then_inc(made, 1)
                pool.wait_ge(made, 3)
                k.ctx_v_w.wait(pool)

                def a_step(n, i):
                    if before(n, 1) is not None:
                        pool.wait_ge(s_mm, n - 1)
                        pool.wait_ge(av_mm, n - 1)
                    pool.tensor_tensor(q_heads[i][:, :, :],
                                       per_group(k.cols[:, ds((n % NB) * P, P)], NH),
                                       per_row(head_scale[:, :], P), ALU.mult).then_inc(q_ready, 1)
                    pool.tensor_copy(v_in[i][:, :, 0:HD],
                                     k.ctx_v_w.rows[:, ds(n % NB, 1), :].rearrange("p o (h d) -> p (o h) d", h=NH)
                                     ).then_inc(v_ready, 1)

                def n1_step(n, i):
                    pool.wait_ge(var_ready, n + 1)
                    pool.tensor_tensor(rs[:, :], ss[:, :], k.neg_half[:, 0:NH], ALU.pow).then_inc(rs_ready, 1)
                schedule(pool, a_step, nothing, n1_step, nothing, a_first=True)

            @block.tensor
            def _(pe):
                pe.wait_ge(made, 3)

                def a_step(n, i):
                    pe.wait_ge(m_loaded[i], loads_by(n, i))
                    pe.wait_ge(e_ready, n)
                    pe.matmul(m_ps[:, :], k.ones[0:1, :], m_in[i][:, :], start=True, stop=False)
                    pe.matmul(m_ps[:, :], ident16[:, :], future[:, :, :].rearrange("p h s -> p (h s)"),
                              start=False, stop=True).then_inc(m_mm, 1)
                    pe.wait_ge(k_ready, n + 1)
                    pe.wait_ge(q_ready, n + 1)
                    if before(n, 1) is not None:
                        pe.wait_ge(c_ready, n - 1)
                    pe.matmul(s_ps[i][:, :], k_in[i][:, :], q_heads[i][:, :, :].rearrange("p h s -> p (h s)"),
                              start=True, stop=True).then_inc(s_mm, 1)

                def c_step(n, i):
                    pe.wait_ge(c_ready, n + 1)
                    pe.wait_ge(v_ready, n + 1)
                    if before(n, 1) is not None:
                        pe.wait_ge(n1_done, n - 1)
                    for h in range(NH):
                        ins = pe.matmul(o_ps[i][:, h * (HD + 1):(h + 1) * (HD + 1)], c[i][:, h, :], v_in[i][:, h, :],
                                        start=True, stop=True)
                    ins.then_inc(av_mm, 1)
                schedule(pe, a_step, c_step, nothing, nothing)

            @block.scalar
            def _(act):
                def a_step(n, i):
                    if before(n, 1) is not None:
                        act.wait_ge(s_mm, n - 1)
                    act.activation(k_in[i][:, :], k.ctx_cols_w.cols[:, ds((n % NB) * P, P)], ACT.Copy
                                   ).then_inc(k_ready, 1)
                    act.wait_ge(e_ready, n + 1)
                    act.activation(decay[i][:, :, :], decay[i][:, :, :], ACT.Exp).then_inc(d_ready, 1)
                schedule(act, a_step, nothing, nothing, nothing)

            @block.vector
            def _(dve):
                dve.wait_ge(w_in, 16)
                dve.tensor_scalar(out_scale[:, 0, :], rms[:, :], 1.0, k.tg[:, 1:2], ALU.add, ALU.mult
                                  ).then_inc(scale_made, 1)
                dve.wait_ge(scale_made, 1)
                for h in range(1, NH):
                    dve.tensor_copy(out_scale[:, h, :], out_scale[:, 0, :]).then_inc(scale_made, 1)
                dve.wait_ge(scale_made, NH)
                STEPS = 8

                def a_step(n, i):
                    dve.wait_ge(m_mm, n + 1)
                    dve.tensor_tensor(decay[i][:, :, :], m_ps[:, :].rearrange("p (h s) -> p h s", h=NH),
                                      per_row(k.aT[:, ds((n % NB) * NH, NH)], P), ALU.add).then_inc(e_ready, 1)

                def c_step(n, i):
                    dve.wait_ge(d_ready, n + 1)
                    dve.wait_ge(s_mm, n + 1)
                    if before(n, 1) is not None:
                        dve.wait_ge(av_mm, n - 1)
                    dve.tensor_tensor(c[i][:, :, :], s_ps[i][:, :].rearrange("p (h s) -> p h s", h=NH),
                                      decay[i][:, :, :], ALU.mult).then_inc(c_ready, 1)

                def n1_step(n, i):
                    link = Chain(dve, chain, n * STEPS)
                    o = o_ps[i][:, 0:NH * (HD + 1)].rearrange("p (h d) -> p h d", h=NH)
                    dve.wait_ge(av_mm, n + 1)
                    link(dve.tensor_tensor(den[:, :], o[:, :, HD:HD + 1].rearrange("p h o -> p (h o)"),
                                           k.emT[:, ds(n * NH, NH)], ALU.max))
                    link(dve.tensor_scalar(den[:, :], den[:, :], 1e-6, None, ALU.add))
                    link(dve.reciprocal(inv[:, :], den[:, :]))
                    dve.tensor_tensor(hid[:, :, :], o[:, :, 0:HD], per_row(inv[:, :], HD), ALU.mult
                                      ).then_inc(n1_done, 1)
                    dve.wait_ge(n1_done, n + 1)
                    link(dve.tensor_tensor(sq[:, :, :], hid[:, :, :], hid[:, :, :], ALU.mult))
                    link(dve.tensor_reduce(ss[:, :], sq[:, :, :], AX.X, ALU.add))
                    dve.tensor_scalar(ss[:, :], ss[:, :], 1.0 / HD, 1e-6, ALU.mult, ALU.add).then_inc(var_ready, 1)
                    link(dve.tensor_tensor(hid[:, :, :], hid[:, :, :], out_scale[:, :, :], ALU.mult))

                def n2_step(n, i):
                    link = Chain(dve, chain, n * STEPS + 6)
                    dve.wait_ge(rs_ready, n + 1)
                    link(dve.tensor_tensor(hid[:, :, :], hid[:, :, :], per_row(rs[:, :], HD), ALU.mult))
                    xt = k.x[:, ds(n, 1), :].rearrange("p o d -> p (o d)")
                    link(dve.tensor_tensor(xt, xt, hid[:, :, :].rearrange("p h d -> p (h d)"), ALU.add))
                schedule(dve, a_step, c_step, n1_step, n2_step)


def l1_route(nc, k):
    with ExitStack() as ctx:
        s = Space(nc, ctx, "l1r", k)
        p, rest, eq, mask = (s.sb(n, [P, NB, E]) for n in ("p", "rest", "eq", "mask"))
        sel = [s.sb(f"sel{i}", [P, NB, E]) for i in range(2)]
        best = [s.sb(f"best{i}", [P, NB]) for i in range(2)]
        red = s.sb("red", [P, NB])
        lb = s.sb("lb", [P, E])
        part = s.sb("part", [P, 2, E])
        total = s.sb("total", [P, 2, E])
        turned_ps = [s.ps(f"turned{i}", [P, BANK]) for i in range(6)]
        sum_ps = s.ps("sum", [P, BANK])
        w_in, chain, biased, squashed, mask_ready, part_ready, turned, summed, used = (s.sem(n) for n in (
            "w_in", "chain", "biased", "squashed", "mask_ready", "part_ready", "turned", "summed", "used"))
        with nc.Block() as block:
            zero_last_stage(block, k)

            @block.sync
            def _(sp):
                sp.dma_start(lb[:, :], k.d["L1_ffn_lb_bias"].partition_broadcast(P)).then_inc(w_in, 16)

            @block.scalar
            def _(act):
                act.wait_ge(biased, 1)
                act.activation(p[:, :, :], p[:, :, :], ACT.Sigmoid).then_inc(squashed, 1)

            @block.vector
            def _(dve):
                link = Chain(dve, chain)
                dve.wait_ge(w_in, 16)
                dve.tensor_tensor(p[:, :, :], k.logits[:, :, :], per_group(lb[:, :], NB), ALU.add).then_inc(biased, 1)
                dve.wait_ge(squashed, 1)
                top_two(link, dve, k, p, rest, eq, red, best, sel)
                link(dve.tensor_tensor(mask[:, :, :], sel[0][:, :, :], sel[1][:, :, :], ALU.add))
                link(dve.tensor_tensor(red[:, :], best[0][:, :], best[1][:, :], ALU.add))
                link(dve.tensor_scalar(red[:, :], red[:, :], 1e-8, None, ALU.add))
                link(dve.reciprocal(red[:, :], red[:, :]))
                link(dve.tensor_tensor(p[:, :, :], p[:, :, :], mask[:, :, :], ALU.mult))
                link(dve.tensor_tensor(p[:, :, :], p[:, :, :], per_row(red[:, :], E), ALU.mult))
                link(dve.tensor_reduce(part[:, 0, :], p[:, :, :].rearrange("p t e -> p e t"), AX.X, ALU.add))
                link(dve.tensor_reduce(part[:, 1, :], mask[:, :, :].rearrange("p t e -> p e t"), AX.X, ALU.add))
                dve.sem_inc(part_ready, 1)
                dve.sem_inc(mask_ready, 1)
                dve.wait_ge(summed, 1)
                link(dve.tensor_copy(total[:, :, :], sum_ps[:, 0:2 * E].rearrange("p (a e) -> p a e", a=2)))
                link(dve.tensor_scalar(total[:, 1, :], total[:, 1, :], 1.0, None, ALU.max))
                link(dve.reciprocal(total[:, 1, :], total[:, 1, :]))
                link(dve.tensor_tensor(k.expert_weight[:, :], total[:, 0, :], total[:, 1, :], ALU.mult))
                for g in range(NG):
                    dve.wait_ge(turned, g + 1)
                    dve.tensor_copy(k.mask_rows[:, g * BANK:(g + 1) * BANK], turned_ps[g % 6][0:E, :]
                                    ).then_inc(used, 1)
                dve.wait_ge(used, NG)

            @block.tensor
            def _(pe):
                pe.wait_ge(part_ready, 1)
                pe.matmul(sum_ps[:, 0:2 * E], k.ones[:, :], part[:, :, :].rearrange("p a e -> p (a e)"),
                          start=True, stop=True).then_inc(summed, 1)
                for g in range(NG):
                    if g >= 6:
                        pe.wait_ge(used, g - 5)
                    for j in range(G4):
                        ins = pe.transpose(turned_ps[g % 6][0:E, j * P:(j + 1) * P], mask[:, g * G4 + j, :], k.ident[:, :])
                    ins.then_inc(turned, 1)


def l1_mixture(nc, k):
    NC = E // 2 + 1
    with ExitStack() as ctx:
        s = Space(nc, ctx, "l1f", k)
        w = k.l1f_w
        w_gate, w_up, w_down = w.w_gate, w.w_up, w.w_down
        pair = s.sb("pair", [E, E // 2, 2, P // 2], BF16)
        gate = [s.sb(f"gate{i}", [P, BANK]) for i in range(2)]
        prod = [s.sb(f"prod{i}", [P, BANK]) for i in range(2)]
        hidden = s.sb("hidden", [P, NC, BANK])
        g_ps, u_ps, m_ps, y_ps = ([s.ps(f"{n}{i}", [P, BANK]) for i in range(2)] for n in ("g", "u", "m", "y"))
        (filled, made, scaled, g_mm, u_mm, m_mm, y_mm, silu_done, multiplied, masked, y_used) = (
            s.sem(n) for n in ("filled", "made", "scaled", "g_mm", "u_mm", "m_mm", "y_mm", "silu_done",
                               "multiplied", "masked", "y_used"))
        with nc.Block() as block:
            zero_last_stage(block, k)

            @block.gpsimd
            def _(pool):
                pool.memset(pair[:, :, :, :], 1.0).then_inc(filled, 1)
                pool.wait_ge(filled, 1)
                pool.affine_select(out=pair[:, :, :, :], in_=pair[:, :, :, :], compare_op=ALU.is_equal, fill=0.0,
                                   base=0, pattern=[[-2, E // 2], [-1, 2], [0, P // 2]], channel_multiplier=1
                                   ).then_inc(made, 1)

            @block.tensor
            def _(pe):
                w.wait(pe)
                pe.wait_ge(made, 1)
                pe.wait_ge(scaled, E)
                with pe.Fori(0, NG // 2) as q:
                    for u in range(2):
                        g = q * 2 + u
                        cols = k.cols[:, ds(g * BANK, BANK)]
                        for c in range(NC):
                            i = (u * NC + c) % 2
                            n = g * NC + c
                            first = u == 0 and c < 2
                            pe.wait_ge(silu_done, q * 2 * NC if first else n - 1)
                            pe.wait_ge(multiplied, q * 2 * NC if first else n - 1)
                            pe.matmul(g_ps[i][:, :], w_gate[:, c, :], cols, start=True, stop=True).then_inc(g_mm, 1)
                            pe.matmul(u_ps[i][:, :], w_up[:, c, :], cols, start=True, stop=True).then_inc(u_mm, 1)
                            if c < NC - 1:
                                pe.wait_ge(masked, g * (NC - 1) + max(c - 1, 0))
                                wait_apart(pe, k.waited_pe)
                                pe.matmul(m_ps[c % 2][:, :], pair[:, c, :, :].rearrange("p i n -> p (i n)"),
                                          k.mask_rows[:, ds(g * BANK, BANK)], start=True, stop=True).then_inc(m_mm, 1)
                        pe.wait_ge(masked, (g + 1) * (NC - 1))
                        pe.wait_ge(multiplied, (g + 1) * NC)
                        pe.wait_ge(y_used, q * 2)
                        for j in range(G4):
                            for c in range(NC):
                                ins = pe.matmul(y_ps[u][:, j * D:(j + 1) * D], hidden[:, c, j * P:(j + 1) * P],
                                                w_down[:, c, :], start=(c == 0), stop=(c == NC - 1))
                        ins.then_inc(y_mm, 1)

            @block.scalar
            def _(act):
                with act.Fori(0, NG // 2) as q:
                    for u in range(2):
                        for c in range(NC):
                            i = (u * NC + c) % 2
                            n = (q * 2 + u) * NC + c
                            first = u == 0 and c < 2
                            act.wait_ge(g_mm, n + 1)
                            act.wait_ge(multiplied, q * 2 * NC if first else n - 1)
                            act.activation(gate[i][:, :], g_ps[i][:, :], ACT.Silu).then_inc(silu_done, 1)

            @block.vector
            def _(dve):
                w.wait(dve)
                for e in range(E):
                    rows = slice(64 * (e % 2), 64 * (e % 2) + 64)
                    dve.tensor_scalar(w_down[rows, e // 2, :], w_down[rows, e // 2, :],
                                      k.expert_weight[rows, e:e + 1], None, ALU.mult).then_inc(scaled, 1)
                with dve.Fori(0, NG // 2) as q:
                    for u in range(2):
                        g = q * 2 + u
                        for c in range(NC):
                            i = (u * NC + c) % 2
                            n = g * NC + c
                            if c == 0:
                                dve.wait_ge(y_mm, g)
                            dve.wait_ge(silu_done, n + 1)
                            dve.wait_ge(u_mm, n + 1)
                            if c < NC - 1:
                                dve.wait_ge(masked, g * (NC - 1) + max(c - 1, 0))
                            dve.tensor_tensor(prod[c % 2][:, :] if c < NC - 1 else hidden[:, c, :], u_ps[i][:, :], gate[i][:, :],
                                              ALU.mult).then_inc(multiplied, 1)
                            if c < NC - 1:
                                dve.wait_ge(m_mm, g * (NC - 1) + c + 1)
                                dve.wait_ge(multiplied, n + 1)
                                dve.tensor_tensor(hidden[:, c, :], prod[c % 2][:, :], m_ps[c % 2][:, :], ALU.mult
                                                  ).then_inc(masked, 1)
                        dve.wait_ge(y_mm, g + 1)
                        xt = k.x[:, ds(g * G4, G4), :]
                        dve.scalar_tensor_tensor(out=xt, in0=y_ps[u][:, :].rearrange("p (t d) -> p t d", t=G4),
                                                 scalar=k.tg[:, 5:6], in1=xt, op0=ALU.mult, op1=ALU.add
                                                 ).then_inc(y_used, 1)


def l2_fold(nc, k):
    H, DK = 16, 64
    with ExitStack() as ctx:
        s = Space(nc, ctx, "l2w", k)
        w = k.l2w_w.w
        ps = [s.ps(f"fold{i}", [P, BANK]) for i in range(8)]
        folded, copied = (s.sem(n) for n in ("folded", "copied"))
        with nc.Block() as block:
            zero_last_stage(block, k)

            @block.tensor
            def _(pe):
                k.l2w_w.wait(pe)
                for n in range(8):
                    left, right = (w[0], w[1]) if n < 4 else (w[2], w[3])
                    for i in range(4):
                        h = 8 * (n % 4 // 2) + 2 * i + n % 2
                        rows = slice(DK * (h % 2), DK * (h % 2) + DK)
                        ins = pe.matmul(ps[n][:, i * P:(i + 1) * P], left[rows, h // 2, :], right[rows, h // 2, :],
                                        start=True, stop=True)
                    ins.then_inc(folded, 1)

            @block.vector
            def _(dve):
                for n in range(8):
                    dst = k.qk_w if n < 4 else k.vo_w
                    dve.wait_ge(folded, n + 1)
                    first = 8 * (n % 4 // 2) + n % 2
                    dve.tensor_copy(dst[:, first:first + 7:2, :],
                                    ps[n][:, :].rearrange("p (h c) -> p h c", h=4)).then_inc(copied, 1)
                dve.wait_ge(copied, 8)


def l2_attention(nc, k):
    H, Q4, KV = 16, 4, 2 * P
    SC = 64.0 ** -0.5
    BODY = 8
    with ExitStack() as ctx:
        s = Space(nc, ctx, "l2a", k)
        kvT = [s.sb(f"kvT{i}", [P, KV]) for i in range(2)]
        kv = [s.sb(f"kv{i}", [P, 2, D]) for i in range(2)]
        tT = [s.sb(f"tT{i}", [P, Q4, P]) for i in range(2)]
        probs = [s.sb(f"probs{i}", [P, Q4, KV]) for i in range(4)]
        pT = [s.sb(f"pT{i}", [P, 2, Q4, P]) for i in range(2)]
        uT = [s.sb(f"uT{i}", [P, Q4, P]) for i in range(2)]
        mx, nm, sums, inv = ([s.sb(f"{n}{i}", [P, Q4]) for i in range(4)] for n in ("mx", "nm", "sums", "inv"))
        t_ps, u_ps, y_ps, kv_ps = (s.ps(n, [P, BANK]) for n in ("t", "u", "y", "kvn"))
        s_ps = [s.ps(f"s{i}", [P, BANK]) for i in range(2)]
        p_ps = [s.ps(f"p{i}", [P, BANK]) for i in range(2)]
        (kvT_ready, kv_mm, kv_ready, t_mm, t_ready, s_mm, maxed, nm_ready, probs_done, inv_ready, scaled, x_mm,
         p0_ready, p1_ready, u_mm, u_ready, o_mm, y_used) = (s.sem(n) for n in (
             "kvT_ready", "kv_mm", "kv_ready", "t_mm", "t_ready", "s_mm", "maxed", "nm_ready", "probs_done",
             "inv_ready", "scaled", "x_mm", "p0_ready", "p1_ready", "u_mm", "u_ready", "o_mm", "y_used"))

        def wait(eng, sem, q, value_per_q, value):
            if not isinstance(q, int):
                eng.wait_ge(sem, q * value_per_q + value)
            elif q * value_per_q + value >= 1:
                eng.wait_ge(sem, q * value_per_q + value)

        def schedule(eng, steps):
            for c in range(-1, 4):
                for step, behind in steps:
                    if c - behind >= 0:
                        step(0, c - behind)
            with eng.Fori(0, NB * H // Q4 // BODY) as q:
                for c in range(4, 4 + BODY):
                    for step, behind in steps:
                        step(q, c - behind)

        def element_before(step, at):
            def run(q, c):
                if (c + BODY) % 4 == at:
                    step(q, c // 4 + 1)
            return run

        def tile(q, e):
            return (q * 2 + e) % NB

        with nc.Block() as block:
            zero_last_stage(block, k)

            @block.gpsimd
            def _(pool):
                def stage_kv(q, e):
                    wait(pool, s_mm, q, 16, 8 * e - 8)
                    wait(pool, kv_mm, q, 2, e - 1)
                    t = tile(q, e)
                    pool.tensor_copy(kvT[e % 2][:, 0:P], k.ctx_cols[:, ds(t * P, P)]).then_inc(kvT_ready, 1)
                    pool.tensor_copy(kvT[e % 2][:, P:KV], k.cols[:, ds(t * P, P)]).then_inc(kvT_ready, 1)

                def scale(q, c):
                    wait(pool, inv_ready, q, 8, c + 1)
                    p = probs[c % 4]
                    pool.tensor_tensor(p[:, :, :], p[:, :, :], per_row(inv[c % 4][:, :], KV), ALU.mult
                                       ).then_inc(scaled, 1)

                stage_kv(0, 0)
                schedule(pool, [(element_before(stage_kv, 2), 0), (scale, 0)])

            @block.tensor
            def _(pe):
                def queries(q, c):
                    wait(pe, kvT_ready, q, 4, 2 * (c // 4) + 2)
                    wait(pe, t_ready, q, 8, c)
                    for i in range(Q4):
                        ins = pe.matmul(t_ps[:, i * P:(i + 1) * P], k.qk_w[:, 4 * (c % 4) + i, :],
                                        kvT[c // 4 % 2][:, P:KV], start=True, stop=True)
                    ins.then_inc(t_mm, 1)

                def scores(q, c):
                    wait(pe, t_ready, q, 8, c + 1)
                    wait(pe, probs_done, q, 32, 4 * c)
                    for pair in range(2):
                        for i in range(2):
                            ins = pe.matmul(s_ps[pair][:, i * KV:(i + 1) * KV], tT[c % 2][:, 2 * pair + i, :],
                                            kvT[c // 4 % 2][:, :], start=True, stop=True)
                        ins.then_inc(s_mm, 1)

                def turn_kv(q, e):
                    wait(pe, kvT_ready, q, 4, 2 * e + 2)
                    wait(pe, kv_ready, q, 2, e)
                    for j in range(2):
                        ins = pe.transpose(kv_ps[:, j * D:(j + 1) * D], kvT[e % 2][:, j * P:(j + 1) * P], k.ident[:, :])
                    ins.then_inc(kv_mm, 1)

                def times_kv(q, c):
                    wait(pe, p0_ready, q, 8, c + 1)
                    wait(pe, p1_ready, q, 8, c + 1)
                    wait(pe, kv_ready, q, 2, c // 4 + 1)
                    wait(pe, u_ready, q, 8, c)
                    for j in range(2):
                        ins = pe.matmul(u_ps[:, :], kv[c // 4 % 2][:, j, :],
                                        pT[c % 2][:, j, :, :].rearrange("p h s -> p (h s)"), start=(j == 0), stop=(j == 1))
                    ins.then_inc(u_mm, 1)

                def output(q, c):
                    wait(pe, u_ready, q, 8, c + 1)
                    if c % 4 == 0:
                        wait(pe, y_used, q, 2, c // 4)
                    for i in range(Q4):
                        h = 4 * (c % 4) + i
                        ins = pe.matmul(y_ps[:, 0:D], uT[c % 2][:, i, :], k.vo_w[:, h, :], start=(h == 0), stop=(h == H - 1))
                    ins.then_inc(o_mm, 1)

                def turn_probs(q, c):
                    wait(pe, scaled, q, 8, c + 1)
                    wait(pe, p0_ready, q, 8, c)
                    wait(pe, p1_ready, q, 8, c)
                    for j in range(2):
                        for i in range(Q4):
                            ins = pe.transpose(p_ps[j][:, i * P:(i + 1) * P], probs[c % 4][:, i, j * P:(j + 1) * P],
                                               k.ident[:, :])
                    ins.then_inc(x_mm, 1)

                turn_kv(0, 0)
                schedule(pe, [(queries, -1), (scores, 0), (element_before(turn_kv, 3), 0), (times_kv, 3), (output, 4),
                              (turn_probs, 2)])

            @block.scalar
            def _(act):
                def exps(q, c):
                    wait(act, x_mm, q, 8, c - 3)
                    for i in range(Q4):
                        if i % 2 == 0:
                            wait(act, nm_ready, q, 16, 2 * c + i // 2 + 1)
                        act.activation(probs[c % 4][:, i, :], s_ps[i // 2][:, (i % 2) * KV:(i % 2 + 1) * KV], ACT.Exp,
                                       bias=nm[c % 4][:, i:i + 1], scale=SC, accum_out=sums[c % 4][:, i:i + 1]
                                       ).then_inc(probs_done, 1)

                def take_u(q, c):
                    wait(act, u_mm, q, 8, c + 1)
                    wait(act, o_mm, q, 8, c - 1)
                    act.activation(uT[c % 2][:, :, :], u_ps[:, :].rearrange("p (h s) -> p h s", h=Q4), ACT.Copy
                                   ).then_inc(u_ready, 1)

                def take_p(q, c):
                    wait(act, x_mm, q, 8, c + 1)
                    wait(act, u_mm, q, 8, c - 1)
                    act.activation(pT[c % 2][:, 0, :, :], p_ps[0][:, :].rearrange("p (h s) -> p h s", h=Q4), ACT.Copy
                                   ).then_inc(p0_ready, 1)
                schedule(act, [(exps, 0), (take_u, 3), (take_p, 2)])

            @block.vector
            def _(dve):
                def take_t(q, c):
                    wait(dve, t_mm, q, 8, c + 1)
                    wait(dve, s_mm, q, 16, 2 * (c - 1))
                    dve.tensor_copy(tT[c % 2][:, :, :], t_ps[:, :].rearrange("p (h s) -> p h s", h=Q4)
                                    ).then_inc(t_ready, 1)

                def maxima(q, c):
                    for pair in range(2):
                        m = slice(2 * pair, 2 * pair + 2)
                        wait(dve, s_mm, q, 16, 2 * c + pair + 1)
                        dve.tensor_reduce(mx[c % 4][:, m], s_ps[pair][:, :].rearrange("p (h s) -> p h s", h=2),
                                          AX.X, ALU.max).then_inc(maxed, 1)
                        wait(dve, maxed, q, 16, 2 * c + pair + 1)
                        dve.tensor_scalar(nm[c % 4][:, m], mx[c % 4][:, m], -SC, None, ALU.mult).then_inc(nm_ready, 1)

                def take_kv(q, e):
                    wait(dve, kv_mm, q, 2, e + 1)
                    wait(dve, u_mm, q, 8, 4 * e - 4)
                    dve.tensor_copy(kv[e % 2][:, :, :], kv_ps[:, 0:KV].rearrange("p (j d) -> p j d", j=2)
                                    ).then_inc(kv_ready, 1)

                def add_output(q, c):
                    if c % 4 == 3:
                        wait(dve, o_mm, q, 8, c + 1)
                        xt = k.x[:, ds(tile(q, c // 4), 1), :].rearrange("p o d -> p (o d)")
                        dve.scalar_tensor_tensor(out=xt, in0=y_ps[:, 0:D], scalar=k.tg[:, 2:3], in1=xt,
                                                 op0=ALU.mult, op1=ALU.add).then_inc(y_used, 1)

                def take_p(q, c):
                    wait(dve, x_mm, q, 8, c + 1)
                    wait(dve, u_mm, q, 8, c - 1)
                    dve.tensor_copy(pT[c % 2][:, 1, :, :], p_ps[1][:, :].rearrange("p (h s) -> p h s", h=Q4)
                                    ).then_inc(p1_ready, 1)

                def invert(q, c):
                    wait(dve, probs_done, q, 32, 4 * c + 4)
                    dve.reciprocal(inv[c % 4][:, :], sums[c % 4][:, :]).then_inc(inv_ready, 1)

                take_kv(0, 0)
                schedule(dve, [(take_t, -1), (maxima, 0), (element_before(take_kv, 3), 0), (add_output, 4), (take_p, 2),
                               (invert, 0)])


def capacity_route(nc, k, name, gate, capacity, by_choice, bias=None, floor=None, add_eps=0.0):
    with ExitStack() as ctx:
        s = Space(nc, ctx, name, k)
        p, rest, eq = (s.sb(n, [P, NB, E]) for n in ("p", "rest", "eq"))
        sel = [s.sb(f"sel{i}", [P, NB, E]) for i in range(2)]
        best = [s.sb(f"best{i}", [P, NB]) for i in range(2)]
        red = s.sb("red", [P, NB])
        n_q = 2 if by_choice else 1
        LQ = n_q * NB
        router_bias = s.sb("router_bias", [P, E])
        queued = s.sb("queued", [P, n_q, NB, E])
        carry = s.sb("carry", [P, E, LQ])
        total = s.sb("total", [P, E, LQ])
        until = s.sb("until", [P, E, LQ])
        place = s.sb("place", [P, E, LQ])
        prefix_ps, total_ps = s.ps("prefix", [P, BANK]), s.ps("total", [P, BANK])
        w_in, chain, filled, shifted, exped, queue_ready, counted = (s.sem(n) for n in (
            "w_in", "chain", "filled", "shifted", "exped", "queue_ready", "counted"))
        with nc.Block() as block:
            zero_last_stage(block, k)

            @block.sync
            def _(sp):
                if bias is not None:
                    sp.dma_start(router_bias[:, :], bias.partition_broadcast(P)).then_inc(w_in, 16)

            @block.gpsimd
            def _(pool):
                pool.memset(carry[:, :, :], 1.0).then_inc(filled, 1)
                pool.wait_ge(filled, 1)
                pool.memset(carry[:, :, 0:1], 0.0).then_inc(filled, 1)

            @block.scalar
            def _(act):
                act.wait_ge(shifted, 1)
                act.activation(p[:, :, :], p[:, :, :], ACT.Exp).then_inc(exped, 1)

            @block.tensor
            def _(pe):
                pe.wait_ge(queue_ready, 1)
                flat = queued[:, :, :, :].rearrange("p i t e -> p (i t e)")
                n = n_q * NB * E
                pe.matmul(prefix_ps[:, 0:n], k.upto[:, :], flat, start=True, stop=True).then_inc(counted, 1)
                pe.matmul(total_ps[:, 0:n], k.ones[:, :], flat, start=True, stop=True).then_inc(counted, 1)

            @block.vector
            def _(dve):
                link = Chain(dve, chain)
                if bias is not None:
                    dve.wait_ge(w_in, 16)
                    link(dve.tensor_tensor(k.logits[:, :, :], k.logits[:, :, :], per_group(router_bias[:, :], NB),
                                           ALU.add))
                link(dve.tensor_reduce(red[:, :], k.logits[:, :, :], AX.X, ALU.max))
                dve.tensor_tensor(p[:, :, :], k.logits[:, :, :], per_row(red[:, :], E), ALU.subtract).then_inc(shifted, 1)
                dve.wait_ge(exped, 1)
                link(dve.tensor_reduce(red[:, :], p[:, :, :], AX.X, ALU.add))
                link(dve.reciprocal(red[:, :], red[:, :]))
                link(dve.tensor_tensor(p[:, :, :], p[:, :, :], per_row(red[:, :], E), ALU.mult))
                top_two(link, dve, k, p, rest, eq, red, best, sel)
                link(dve.tensor_tensor(red[:, :], best[0][:, :], best[1][:, :], ALU.add))
                if add_eps:
                    link(dve.tensor_scalar(red[:, :], red[:, :], add_eps, None, ALU.add))
                link(dve.reciprocal(red[:, :], red[:, :]))
                for i in range(2):
                    link(dve.tensor_tensor(best[i][:, :], best[i][:, :], red[:, :], ALU.mult))
                    if floor is not None:
                        link(dve.tensor_scalar(red[:, :] if i else rest[:, :, 0:1].rearrange("p t o -> p (t o)"),
                                               best[i][:, :], floor, None, ALU.is_gt))
                        link(dve.tensor_tensor(sel[i][:, :, :], sel[i][:, :, :],
                                               per_row(red[:, :], E) if i else rest[:, :, 0:1].to_broadcast([P, NB, E]),
                                               ALU.mult))
                if by_choice:
                    for i in range(2):
                        link(dve.tensor_copy(queued[:, i, :, :], sel[i][:, :, :]))
                else:
                    link(dve.tensor_tensor(queued[:, 0, :, :], sel[0][:, :, :], sel[1][:, :, :], ALU.add))
                dve.sem_inc(queue_ready, 1)
                dve.wait_ge(counted, 2)
                dve.wait_ge(filled, 2)

                def by_expert(ps):
                    return ps[:, 0:LQ * E].rearrange("p (l e) -> p e l", e=E)
                link(dve.tensor_copy(total[:, :, :], by_expert(total_ps)))
                link(dve.tensor_tensor_scan(until[:, :, :].rearrange("p e l -> p (e l)"),
                                            carry[:, :, :].rearrange("p e l -> p (e l)"),
                                            total[:, :, :].rearrange("p e l -> p (e l)"), 0.0, ALU.mult, ALU.add))
                link(dve.tensor_tensor(until[:, :, :], until[:, :, :], total[:, :, :], ALU.subtract))
                link(dve.tensor_tensor(place[:, :, :], by_expert(prefix_ps), until[:, :, :], ALU.add))
                link(dve.tensor_scalar(place[:, :, :], place[:, :, :], float(capacity), None, ALU.is_le))
                for i in range(2):
                    kept = place[:, :, i * NB:(i + 1) * NB] if by_choice else place[:, :, :]
                    link(dve.tensor_tensor(sel[i][:, :, :], sel[i][:, :, :], kept.rearrange("p e t -> p t e"), ALU.mult))
                    link(dve.tensor_tensor(sel[i][:, :, :], sel[i][:, :, :], per_row(best[i][:, :], E), ALU.mult))
                link(dve.tensor_tensor(sel[0][:, :, :], sel[0][:, :, :], sel[1][:, :, :], ALU.add))
                link(dve.tensor_scalar(k.weight[:, :, :], sel[0][:, :, :], gate, None, ALU.mult))


def row_mixture(nc, k, name, chunks, func, w, full=False):
    with ExitStack() as ctx:
        s = Space(nc, ctx, name, k)
        w1, w2 = w.w1, w.w2
        hidden = [s.sb(f"hidden{i}", [P, chunks, BANK]) for i in range(2)]
        h_ps = [s.ps(f"h{i}", [P, BANK]) for i in range(chunks)]
        o_ps = [s.ps(f"o{i}", [P, BANK]) for i in range(2)]
        (scaled, h_mm, act_done, o_mm, added, w_staged, w_turned, wT_ready, bias_mm, sum_ready, tmp_ready,
         bias_added) = (s.sem(n) for n in (
             "scaled", "h_mm", "act_done", "o_mm", "added", "w_staged", "w_turned", "wT_ready", "bias_mm",
             "sum_ready", "tmp_ready", "bias_added"))
        if full:
            b1, scale_all, scale8, bias8 = w.b1, w.scale_all, w.scale8, w.bias8
            w_stage, w_sum, tmp = s.sb("w_stage", [P, G4, E]), s.sb("w_sum", [P, G4]), s.sb("tmp", [P, G4, D])
            wT = s.sb("wT", [E, BANK])
            bias_ps, wT_ps = s.ps("bias", [P, BANK]), s.ps("wT", [P, BANK])

        def wait(eng, sem, q, per_q, value):
            if not isinstance(q, int) or q * per_q + value >= 1:
                eng.wait_ge(sem, q * per_q + value)

        def schedule(eng, steps):
            for step, behind in steps:
                if behind == 0:
                    step(0, 0)
            with eng.Fori(0, NG) as q:
                for c in range(1, E + 1):
                    for step, behind in steps:
                        step(q, c - behind)

        def once(step, at):
            return lambda q, c: step(q) if c == at else None

        with nc.Block() as block:
            zero_last_stage(block, k)

            @block.gpsimd
            def _(pool):
                if full:
                    def stage(q):
                        pool.wait_ge(w_turned, q)
                        pool.wait_ge(sum_ready, q)
                        pool.tensor_copy(w_stage[:, :, :], k.weight[:, ds(q * G4, G4), :]).then_inc(w_staged, 1)
                    with pool.Fori(0, NG) as q:
                        stage(q)

            @block.tensor
            def _(pe):
                w.wait(pe)

                def hide(q, c):
                    g = (q + c // E) % NG
                    for i in range(chunks):
                        wait(pe, act_done, q, E * chunks, chunks * (c - 1) + i + 1)
                        pe.matmul(h_ps[i][:, :], w1[:, c % E, i, :], k.cols[:, ds(g * BANK, BANK)],
                                  start=True, stop=True).then_inc(h_mm, 1)

                def output(q, c):
                    wait(pe, act_done, q, E * chunks, chunks * (c + 1))
                    if full and c % E == 0:
                        pe.wait_ge(scaled, E + 1)
                    wait(pe, added, q, E * G4, G4 * max(c - 1, 0))
                    for j in range(G4):
                        for i in range(chunks):
                            ins = pe.matmul(o_ps[c % 2][:, j * D:(j + 1) * D], hidden[c % 2][:, i, j * P:(j + 1) * P],
                                            w2[:, c % E, i, :], start=(i == 0), stop=(i == chunks - 1))
                    ins.then_inc(o_mm, 1)

                def bias_rows(q):
                    pe.wait_ge(w_staged, q + 1)
                    pe.wait_ge(wT_ready, q)
                    for j in range(G4):
                        ins = pe.transpose(wT_ps[0:E, j * P:(j + 1) * P], w_stage[:, j, :], k.ident[:, :])
                    ins.then_inc(w_turned, 1)

                def bias_out(q):
                    pe.wait_ge(wT_ready, q + 1)
                    pe.wait_ge(bias_added, q)
                    for j in range(G4):
                        ins = pe.matmul(bias_ps[:, j * D:(j + 1) * D], wT[:, j * P:(j + 1) * P], bias8[:, :],
                                        start=True, stop=True)
                    ins.then_inc(bias_mm, 1)
                steps = [(hide, 0), (output, 1)]
                if full:
                    steps += [(once(bias_rows, 2), 0), (once(bias_out, 4), 0)]
                schedule(pe, steps)

            @block.scalar
            def _(act):
                w.wait(act)

                def activate(q, c):
                    wait(act, o_mm, q, E, c - 1)
                    for i in range(chunks):
                        wait(act, h_mm, q, E * chunks, chunks * c + i + 1)
                        if full:
                            ins = act.activation(hidden[c % 2][:, i, :], h_ps[i][:, :], func, bias=b1[:, c % E, i:i + 1])
                        else:
                            ins = act.activation(hidden[c % 2][:, i, :], h_ps[i][:, :], func)
                        ins.then_inc(act_done, 1)
                schedule(act, [(activate, 0)])

            @block.vector
            def _(dve):
                w.wait(dve)
                if full:
                    for e in range(E):
                        dve.tensor_tensor(w2[:, e, :, :], w2[:, e, :, :], per_group(scale_all[:, e, :], chunks), ALU.mult
                                          ).then_inc(scaled, 1)
                    dve.tensor_tensor(bias8[:, :], bias8[:, :], scale8[:, :], ALU.mult).then_inc(scaled, 1)

                def add(q, c):
                    wait(dve, o_mm, q, E, c + 1)
                    wait(dve, added, q, E * G4, G4 * c)
                    if full:
                        wait(dve, bias_added, q, 1, 1 if c >= 4 else 0)
                    for j in range(G4):
                        xt = k.x[:, ds(q * G4 + j, 1), :].rearrange("p o d -> p (o d)")
                        dve.scalar_tensor_tensor(out=xt, in0=o_ps[c % 2][:, j * D:(j + 1) * D],
                                                 scalar=k.weight[:, ds(q * G4 + j, 1), c % E:c % E + 1].rearrange(
                                                     "p o e -> p (o e)"),
                                                 in1=xt, op0=ALU.mult, op1=ALU.add).then_inc(added, 1)

                def take_wT(q):
                    dve.wait_ge(w_turned, q + 1)
                    dve.wait_ge(bias_mm, q)
                    dve.tensor_copy(wT[:, :], wT_ps[0:E, :]).then_inc(wT_ready, 1)
                    dve.wait_ge(w_staged, q + 1)
                    dve.tensor_reduce(w_sum[:, :], w_stage[:, :, :], AX.X, ALU.add).then_inc(sum_ready, 1)
                    dve.wait_ge(sum_ready, q + 1)
                    dve.wait_ge(bias_added, q)
                    dve.tensor_tensor(tmp[:, :, :], k.rows[:, ds(q * G4, G4), :], per_row(w_sum[:, :], D), ALU.mult
                                      ).then_inc(tmp_ready, 1)
                    dve.wait_ge(tmp_ready, q * 3 + 1)

                def add_bias(q):
                    dve.wait_ge(bias_mm, q + 1)
                    dve.tensor_tensor(tmp[:, :, :], tmp[:, :, :], bias_ps[:, :].rearrange("p (t d) -> p t d", t=G4),
                                      ALU.add).then_inc(tmp_ready, 1)
                    dve.wait_ge(tmp_ready, q * 3 + 2)
                    wait(dve, added, q, E * G4, G4 * 4)
                    xt = k.x[:, ds(q * G4, G4), :]
                    dve.tensor_tensor(xt, xt, tmp[:, :, :], ALU.add).then_inc(bias_added, 1)
                    dve.sem_inc(tmp_ready, 1)
                steps = [(add, 1)]
                if full:
                    steps += [(once(take_wT, 2), 0), (once(add_bias, 4), 0)]
                schedule(dve, steps)


def l3_attention(nc, k):
    H, DA, ROUNDS = 16, 8, 4
    Q4, NQ = 4, 4
    SC = DA ** -0.5
    BODY = 4
    LAST_LAG = 3
    LOWEST = -3e38
    with ExitStack() as ctx:
        s = Space(nc, ctx, "l3a", k)
        w = k.l3a_w
        wq, wk = w.wq, w.wk
        two = range(2)
        k_in = [s.sb(f"k_in{i}", [P, P]) for i in two]
        v_raw = [s.sb(f"v_raw{i}", [P, D]) for i in two]
        v = [s.sb(f"v{i}", [P, H, DA + 1]) for i in range(4)]
        qT, kT = s.sb("qT", [P, P]), s.sb("kT", [P, Q4, P])
        score = [s.sb(f"score{i}", [P, H, P]) for i in range(4)]
        work = s.sb("work", [P, H, P])
        top = [s.sb(f"top{i}", [P, ROUNDS, H, 8]) for i in two]
        nm = [s.sb(f"nm{i}", [P, H]) for i in two]
        probs = [s.sb(f"probs{i}", [P, H, P]) for i in two]
        above = s.sb("above", [P, H, P])
        pT = [s.sb(f"pT{i}", [P, Q4, P]) for i in two]
        inv = s.sb("inv", [P, H])
        o_norm = s.sb("o_norm", [P, H, DA])
        q_ps, k_ps, p_ps, o_ps = (s.ps(n, [P, BANK]) for n in ("q", "k", "p", "o"))
        s_ps = [s.ps(f"s{i}", [P, BANK]) for i in range(NQ)]
        k_loaded, v_loaded = ([s.sem(f"{n}_loaded{i}") for i in two] for n in "kv")
        (filled, v_ready, q_mm, k_mm, q_ready, k_ready, s_mm, s_ready, found, nm_ready, probs_done, compared,
         masked, p_mm, p_ready, av_mm, inv_ready, o_ready, x_done) = (s.sem(n) for n in (
             "filled", "v_ready", "q_mm", "k_mm", "q_ready", "k_ready", "s_mm", "s_ready", "found", "nm_ready",
             "probs_done", "compared", "masked", "p_mm", "p_ready", "av_mm", "inv_ready", "o_ready", "x_done"))
        FINDS = (2 * ROUNDS - 1) * H

        def wait(eng, sem, q, per_element, value):
            n = q * (BODY * per_element) + value
            if not isinstance(q, int) or n >= 1:
                eng.wait_ge(sem, n)

        def schedule(eng, steps):
            def run(q, c):
                for step, behind in steps:
                    if not isinstance(q, int) or 0 <= q * BODY + c - behind < NB:
                        step(q, c - behind)

            for c in range(-1, LAST_LAG):
                run(0, c)
            with eng.Fori(0, NB // BODY - 1) as q:
                for c in range(LAST_LAG, LAST_LAG + BODY):
                    run(q, c)
            for c in range(LAST_LAG, LAST_LAG + BODY):
                run(NB // BODY - 1, c)

        def tile(q, c):
            return (q * BODY + c) % NB

        with nc.Block() as block:
            zero_last_stage(block, k)

            @block.sync
            def _(sp):
                def load(q, c):
                    i = c % 2
                    wait(sp, k_mm, q, 1, c - 1)
                    wait(sp, v_ready, q, 1, c - 1)
                    sp.dma_start(k_in[i][:, :], k.d["ctxT"][ds(tile(q, c), 1), :, :].rearrange("o p s -> (o p) s")
                                 ).then_inc(k_loaded[i], 16)
                    sp.dma_start(v_raw[i][:, :], k.d["ctx"][ds(tile(q, c), 1), :, :].rearrange("o p d -> (o p) d")
                                 ).then_inc(v_loaded[i], 16)
                schedule(sp, [(load, -1)])

            @block.gpsimd
            def _(pool):
                for t in v:
                    pool.memset(t[:, :, :], 1.0).then_inc(filled, 1)
                pool.wait_ge(filled, 4)

                def take_v(q, c):
                    wait(pool, v_loaded[c % 2], q, 8, 16 * (c // 2 + 1))
                    wait(pool, av_mm, q, 1, c - 3)
                    wait_apart(pool, k.waited_pool)
                    pool.tensor_copy(v[c % 4][:, :, 0:DA], v_raw[c % 2][:, :].rearrange("p (h d) -> p h d", h=H)
                                     ).then_inc(v_ready, 1)

                def mask(q, c):
                    wait(pool, nm_ready, q, 1, c + 1)
                    for n in range(NQ):
                        hs = slice(Q4 * n, Q4 * n + Q4)
                        wait(pool, masked, q, NQ, NQ * c + n - NQ + 1)
                        wait_apart(pool, k.waited_pool)
                        for h in range(Q4 * n, Q4 * n + Q4):
                            ins = pool.tensor_scalar(above[:, h, :], score[c % 4][:, h, :],
                                                     top[c % 2][:, ROUNDS - 1, h, 7:8], None, ALU.is_ge)
                        ins.then_inc(compared, 1)
                        wait(pool, compared, q, NQ, NQ * c + n + 1)
                        wait(pool, probs_done, q, H, H * c + Q4 * n + Q4)
                        pool.tensor_tensor(probs[c % 2][:, hs, :], probs[c % 2][:, hs, :], above[:, hs, :], ALU.mult
                                           ).then_inc(masked, 1)
                schedule(pool, [(take_v, -1), (mask, 1)])

            @block.tensor
            def _(pe):
                w.wait(pe)

                def scores(q, c):
                    wait(pe, q_ready, q, 1, c)
                    pe.matmul(q_ps[:, 0:P], wq[:, :], k.cols[:, ds(tile(q, c) * P, P)], start=True, stop=True
                              ).then_inc(q_mm, 1)
                    wait(pe, k_loaded[c % 2], q, 8, 16 * (c // 2 + 1))
                    wait(pe, k_ready, q, 1, c)
                    for r in range(Q4):
                        ins = pe.matmul(k_ps[:, r * P:(r + 1) * P], wk[:, r, :], k_in[c % 2][:, :], start=True, stop=True)
                    ins.then_inc(k_mm, 1)
                    wait(pe, q_ready, q, 1, c + 1)
                    wait(pe, k_ready, q, 1, c + 1)
                    wait(pe, s_ready, q, NQ, NQ * c)
                    for n in range(NQ):
                        rows = slice(32 * n, 32 * n + 32)
                        pe.matmul(s_ps[n][:, :], qT[rows, :], kT[rows, :, :].rearrange("p r s -> p (r s)"),
                                  start=True, stop=True).then_inc(s_mm, 1)

                def apply(q, c):
                    for n in range(NQ + 1):
                        if n < NQ:
                            wait(pe, masked, q, NQ, NQ * c + n + 1)
                            wait(pe, p_ready, q, NQ, NQ * c + n)
                            for i in range(Q4):
                                ins = pe.transpose(p_ps[:, i * P:(i + 1) * P], probs[c % 2][:, Q4 * n + i, :], k.ident[:, :])
                            ins.then_inc(p_mm, 1)
                        if n > 0:
                            m = n - 1
                            wait(pe, p_ready, q, NQ, NQ * c + m + 1)
                            if m == 0:
                                wait(pe, v_ready, q, 1, c + 1)
                                wait(pe, o_ready, q, 1, c)
                            for i in range(Q4):
                                h = Q4 * m + i
                                ins = pe.matmul(o_ps[:, h * (DA + 1):(h + 1) * (DA + 1)], pT[m % 2][:, i, :],
                                                v[c % 4][:, h, :], start=True, stop=True)
                    ins.then_inc(av_mm, 1)
                schedule(pe, [(scores, -1), (apply, 2)])

            @block.scalar
            def _(act):
                def take_scores(q, c):
                    wait(act, q_mm, q, 1, c + 1)
                    act.activation(qT[:, :], q_ps[:, 0:P], ACT.Copy).then_inc(q_ready, 1)
                    wait(act, k_mm, q, 1, c + 1)
                    act.activation(kT[:, :, :], k_ps[:, :].rearrange("p (r s) -> p r s", r=Q4), ACT.Copy
                                   ).then_inc(k_ready, 1)
                    wait(act, compared, q, NQ, NQ * (c - 3))
                    for n in range(NQ):
                        wait(act, s_mm, q, NQ, NQ * c + n + 1)
                        act.activation(score[c % 4][:, Q4 * n:Q4 * n + Q4, :],
                                       s_ps[n][:, :].rearrange("p (r s) -> p r s", r=Q4), ACT.Copy, scale=SC
                                       ).then_inc(s_ready, 1)

                def exps(q, c):
                    wait(act, nm_ready, q, 1, c + 1)
                    wait(act, p_mm, q, NQ, NQ * (c - 1))
                    for h in range(H):
                        act.activation(probs[c % 2][:, h, :], score[c % 4][:, h, :], ACT.Exp, bias=nm[c % 2][:, h:h + 1]
                                       ).then_inc(probs_done, 1)

                def take_p(q, c):
                    for n in range(NQ):
                        wait(act, p_mm, q, NQ, NQ * c + n + 1)
                        if n < 2:
                            wait(act, av_mm, q, 1, c)
                        act.activation(pT[n % 2][:, :, :], p_ps[:, :].rearrange("p (h s) -> p h s", h=Q4), ACT.Copy
                                       ).then_inc(p_ready, 1)
                schedule(act, [(take_scores, -1), (exps, 1), (take_p, 2)])

            @block.vector
            def _(dve):
                def cutoffs(q, c):
                    t = top[c % 2]
                    wait(dve, masked, q, NQ, NQ * (c - 1))
                    n = 0
                    for first in range(0, H, 2 * Q4):
                        wait(dve, s_ready, q, NQ, NQ * c + first // Q4 + 2)
                        for step in range(2 * ROUNDS - 1):
                            for h in range(first, first + 2 * Q4):
                                src = score[c % 4][:, h, :] if step < 2 else work[:, h, :]
                                if h % Q4 == 0:
                                    wait(dve, found, q, FINDS, FINDS * c + n - Q4)
                                    wait_apart(dve, k.waited_dve)
                                if step % 2 == 0:
                                    ins = dve.max(t[:, step // 2, h, :], src)
                                else:
                                    ins = dve.match_replace(work[:, h, :], t[:, step // 2, h, :], src, LOWEST)
                                ins.then_inc(found, 1)
                                n += 1
                    wait(dve, found, q, FINDS, FINDS * (c + 1))
                    dve.tensor_scalar(nm[c % 2][:, :], t[:, 0, :, 0:1].rearrange("p h o -> p (h o)"), -1.0, None,
                                      ALU.mult).then_inc(nm_ready, 1)

                def add(q, c):
                    wait(dve, av_mm, q, 1, c + 1)
                    o = o_ps[:, 0:H * (DA + 1)].rearrange("p (h d) -> p h d", h=H)
                    dve.reciprocal(inv[:, :], o[:, :, DA:DA + 1].rearrange("p h o -> p (h o)")).then_inc(inv_ready, 1)
                    wait(dve, inv_ready, q, 1, c + 1)
                    dve.tensor_tensor(o_norm[:, :, :], o[:, :, 0:DA], per_row(inv[:, :], DA), ALU.mult
                                      ).then_inc(o_ready, 1)
                    wait(dve, o_ready, q, 1, c + 1)
                    xt = k.x[:, ds(tile(q, c), 1), :].rearrange("p o d -> p (o d)")
                    dve.scalar_tensor_tensor(out=xt, in0=o_norm[:, :, :].rearrange("p h d -> p (h d)"),
                                             scalar=k.tg[:, 3:4], in1=xt, op0=ALU.mult, op1=ALU.add).then_inc(x_done, 1)
                    wait(dve, x_done, q, 1, c + 1)
                schedule(dve, [(add, 3), (cutoffs, 0)])


def l3_block_attention(nc, k):
    H, GK, R, HD, S, PJ = 16, 4, 4, 8, NB, 4
    SC = HD ** -0.5
    BODY = 4
    with ExitStack() as ctx:
        s = Space(nc, ctx, "l3b", k)
        w = k.l3b_w
        wq, wk, wv, proj, head_of = w.wq, w.wk, w.wv, w.proj, w.head_of
        two = range(2)
        stage = [s.sb(f"stage{i}", [P, PJ, S]) for i in two]
        stage4 = [s.sb(f"stage4{i}", [P, PJ, R, S]) for i in two]
        qT, kT = [s.sb(f"qT{i}", [P, P]) for i in two], [s.sb(f"kT{i}", [P, R, P]) for i in two]
        v = [s.sb(f"v{i}", [P, PJ, P]) for i in range(4)]
        own_head = s.sb("own_head", [P, R])
        own_cols = s.sb("own_cols", [P, PJ, P])
        causal = s.sb("causal", [P, GK, P])
        score = [s.sb(f"score{i}", [P, H, S]) for i in two]
        mx, sums, inv = ([s.sb(f"{n}{i}", [P, H]) for i in two] for n in ("mx", "sums", "inv"))
        pT = s.sb("pT", [P, GK, P])
        ao, aoT = s.sb("ao", [P, H, HD]), s.sb("aoT", [P, P])
        y = [s.sb(f"y{i}", [P, D]) for i in two]
        s_ps = s.ps("s", [P, GK, BANK])
        qk_ps, v_ps, p_ps, out_ps = (s.ps(n, [P, BANK]) for n in ("qk", "v", "p", "out"))
        q_ps, k_ps = (qk_ps[:, i * P:(i + 1) * P] for i in range(2))
        o_ps, aoT_ps, y_ps = (out_ps[:, i * P:(i + 1) * P] for i in range(3))
        y_stored = [s.sem(f"y_stored{i}") for i in two]
        (filled, made, staged, k_mm, v_mm, q_ready, k_ready, v_ready, s_mm, s_out, maxed, shifted, exped,
         summed, inv_ready, p_mm, p_ready, o_mm, ao_ready, aoT_mm, aoT_ready, y_mm, y_ready) = (s.sem(n) for n in (
             "filled", "made", "staged", "k_mm", "v_mm", "q_ready", "k_ready", "v_ready", "s_mm",
             "s_out", "maxed", "shifted", "exped", "summed", "inv_ready", "p_mm", "p_ready", "o_mm", "ao_ready",
             "aoT_mm", "aoT_ready", "y_mm", "y_ready"))
        NN = P // PJ

        def wait(eng, sem, q, per_n, value):
            n = q * (BODY * per_n) + value
            if not isinstance(q, int) or n >= 1:
                eng.wait_ge(sem, n)

        def schedule(eng, steps):
            for c in range(-1, 2):
                for step, behind in steps:
                    if c - behind >= 0:
                        step(0, c - behind)
            with eng.Fori(0, NN // BODY) as q:
                for c in range(2, 2 + BODY):
                    for step, behind in steps:
                        step(q, c - behind)

        def first_position(q, c):
            return ((q * BODY + c) % NN) * PJ

        with nc.Block() as block:
            zero_last_stage(block, k)

            @block.sync
            def _(sp):
                def store(q, c):
                    wait(sp, y_ready, q, 1, c + 1)
                    dst = k.block_out[:, ds(first_position(q, c), PJ), :].rearrange("s j d -> j s d")
                    sp.dma_start(dst, y[c % 2][:, :]).then_inc(y_stored[c % 2], 16)
                schedule(sp, [(store, 2)])
                for i in two:
                    sp.wait_ge(y_stored[i], 16 * NN // 2)

            @block.gpsimd
            def _(pool):
                pool.memset(own_head[:, :], 1.0).then_inc(filled, 1)
                pool.memset(causal[:, :, :], 0.0).then_inc(filled, 1)
                pool.wait_ge(filled, 2)
                pool.affine_select(out=own_head[:, :], in_=own_head[:, :], compare_op=ALU.is_ge, fill=0.0,
                                   base=0, pattern=[[-S, R]], channel_multiplier=1).then_inc(made, 1)
                pool.wait_ge(made, 1)
                pool.affine_select(out=own_head[:, :], in_=own_head[:, :], compare_op=ALU.is_ge, fill=0.0,
                                   base=S - 1, pattern=[[S, R]], channel_multiplier=-1).then_inc(made, 1)
                pool.wait_ge(made, 2)
                pool.tensor_copy(own_cols[:, :, :].rearrange("p j (g r d) -> p (j g) r d", g=GK, r=R),
                                 own_head[:, :].unsqueeze(1).unsqueeze(3).to_broadcast([P, PJ * GK, R, HD])
                                 ).then_inc(made, 1)
                for j in range(PJ):
                    pool.wait_ge(made, 3 + j)
                    part = causal[S * j:S * j + S, :, :].rearrange("p g (r t) -> p (g r) t", r=R)
                    pool.affine_select(out=part, in_=part, compare_op=ALU.is_ge, fill=-3e38,
                                       base=0, pattern=[[0, H], [-1, S]], channel_multiplier=1).then_inc(made, 1)
                pool.wait_ge(made, 3 + PJ)

                def gather(q, c):
                    wait(pool, v_mm, q, 1, c - 1)
                    src = k.cols[:, :].rearrange("p (s t) -> p t s", s=S)[:, ds(first_position(q, c), PJ), :]
                    pool.tensor_copy(stage[c % 2][:, :, :], src).then_inc(staged, 1)
                    wait(pool, staged, q, 2, 2 * c + 1)
                    wait_apart(pool, k.waited_pool)
                    pool.tensor_copy(stage4[c % 2][:, :, :, :],
                                     stage[c % 2][:, :, :].unsqueeze(2).to_broadcast([P, PJ, R, S])).then_inc(staged, 1)
                schedule(pool, [(gather, -1)])

            @block.tensor
            def _(pe):
                w.wait(pe)

                def project(q, c):
                    tokens = stage[c % 2][:, :, :].rearrange("p j s -> p (j s)")
                    wait(pe, staged, q, 2, 2 * c + 2)
                    wait(pe, k_ready, q, 1, c)
                    pe.matmul(q_ps, wq[:, :], tokens, start=True, stop=True)
                    pe.matmul(k_ps, wk[:, :], tokens, start=True, stop=True).then_inc(k_mm, 1)
                    wait(pe, v_ready, q, 1, c)
                    for j in range(PJ):
                        ins = pe.matmul(v_ps[:, j * P:(j + 1) * P],
                                        stage4[c % 2][:, j, :, :].rearrange("p r s -> p (r s)"), wv[:, :],
                                        start=True, stop=True)
                    ins.then_inc(v_mm, 1)

                def scores(q, c):
                    wait(pe, q_ready, q, 1, c + 1)
                    wait(pe, k_ready, q, 1, c + 1)
                    wait(pe, s_out, q, 1, c)
                    wait_apart(pe, k.waited_pe)
                    for j in range(PJ):
                        for g in range(GK):
                            rows = slice(32 * g, 32 * g + 32)
                            ins = pe.matmul(s_ps[S * j:S * j + S, g, 0:P], qT[c % 2][rows, S * j:S * j + S],
                                            kT[c % 2][rows, :, S * j:S * j + S], start=True, stop=True)
                    ins.then_inc(s_mm, 1)

                def apply(q, c):
                    wait(pe, exped, q, 1, c + 1)
                    wait(pe, p_ready, q, 1, c)
                    for g in range(GK):
                        ins = pe.transpose(p_ps[:, g * P:(g + 1) * P],
                                           score[c % 2][:, g * R:(g + 1) * R, :].rearrange("p r t -> p (r t)"), k.ident[:, :])
                    ins.then_inc(p_mm, 1)
                    wait(pe, p_ready, q, 1, c + 1)
                    wait(pe, v_ready, q, 1, c + 1)
                    wait(pe, y_ready, q, 1, c)
                    for j in range(PJ):
                        for g in range(GK):
                            ins = pe.matmul(o_ps[S * j:S * j + S, 32 * g:32 * g + 32], pT[:, g, S * j:S * j + S],
                                            v[c % 4][:, j, 32 * g:32 * g + 32], start=True, stop=True)
                    ins.then_inc(o_mm, 1)

                def output(q, c):
                    wait(pe, ao_ready, q, 1, c + 1)
                    pe.transpose(aoT_ps, ao[:, :, :].rearrange("p h d -> p (h d)"), k.ident[:, :]).then_inc(aoT_mm, 1)
                    wait(pe, aoT_ready, q, 1, c + 1)
                    pe.matmul(y_ps, aoT[:, :], proj[:, :], start=True, stop=True).then_inc(y_mm, 1)
                schedule(pe, [(project, -1), (scores, 0), (output, 2), (apply, 1)])

            @block.scalar
            def _(act):
                def exps(q, c):
                    wait(act, shifted, q, 1, c + 1)
                    act.activation(score[c % 2][:, :, :], score[c % 2][:, :, :], ACT.Exp).then_inc(exped, 1)

                def take_p(q, c):
                    wait(act, p_mm, q, 1, c + 1)
                    wait(act, o_mm, q, 1, c)
                    act.activation(pT[:, :, :], p_ps[:, :].rearrange("p (g s) -> p g s", g=GK), ACT.Copy
                                   ).then_inc(p_ready, 1)

                def take_out(q, c):
                    wait(act, aoT_mm, q, 1, c + 1)
                    wait(act, y_mm, q, 1, c)
                    act.activation(aoT[:, :], aoT_ps, ACT.Copy).then_inc(aoT_ready, 1)
                    wait(act, y_mm, q, 1, c + 1)
                    wait(act, y_stored[c % 2], q, 8, 16 * (c // 2))
                    act.activation(y[c % 2][:, :], y_ps, ACT.Copy).then_inc(y_ready, 1)
                schedule(act, [(take_out, 2), (take_p, 1), (exps, 0)])

            @block.vector
            def _(dve):
                dve.wait_ge(made, 3 + PJ)
                w.wait(dve)

                def take_qk(q, c):
                    wait(dve, k_mm, q, 1, c + 1)
                    wait(dve, s_mm, q, 1, c - 1)
                    dve.tensor_copy(qT[c % 2][:, :], q_ps).then_inc(q_ready, 1)
                    dve.tensor_tensor(kT[c % 2][:, :, :], per_group(k_ps, R), per_row(head_of[:, :], P), ALU.mult
                                      ).then_inc(k_ready, 1)

                def take_v(q, c):
                    wait(dve, v_mm, q, 1, c + 1)
                    wait(dve, o_mm, q, 1, c - 3)
                    dve.tensor_tensor(v[c % 4][:, :, :], v_ps[:, :].rearrange("p (j n) -> p j n", j=PJ), own_cols[:, :, :],
                                      ALU.mult).then_inc(v_ready, 1)

                def soften(q, c):
                    t = score[c % 2]
                    wait(dve, s_mm, q, 1, c + 1)
                    wait(dve, p_mm, q, 1, c - 1)
                    wait(dve, summed, q, 1, c - 1)
                    dve.scalar_tensor_tensor(out=t[:, :, :].rearrange("p (g r) t -> p g (r t)", g=GK), in0=s_ps[:, :, 0:P],
                                             scalar=SC, in1=causal[:, :, :], op0=ALU.mult, op1=ALU.add).then_inc(s_out, 1)
                    wait(dve, s_out, q, 1, c + 1)
                    dve.tensor_reduce(mx[c % 2][:, :], t[:, :, :], AX.X, ALU.max).then_inc(maxed, 1)
                    wait(dve, maxed, q, 1, c + 1)
                    dve.tensor_tensor(t[:, :, :], t[:, :, :], per_row(mx[c % 2][:, :], S), ALU.subtract
                                      ).then_inc(shifted, 1)

                def total(q, c):
                    wait(dve, exped, q, 1, c + 1)
                    dve.tensor_reduce(sums[c % 2][:, :], score[c % 2][:, :, :], AX.X, ALU.add).then_inc(summed, 1)
                    wait(dve, summed, q, 1, c + 1)
                    dve.reciprocal(inv[c % 2][:, :], sums[c % 2][:, :]).then_inc(inv_ready, 1)

                def divide(q, c):
                    wait(dve, o_mm, q, 1, c + 1)
                    wait(dve, inv_ready, q, 1, c + 1)
                    wait(dve, aoT_mm, q, 1, c)
                    dve.tensor_tensor(ao[:, :, :], o_ps.rearrange("p (h d) -> p h d", h=H), per_row(inv[c % 2][:, :], HD),
                                      ALU.mult).then_inc(ao_ready, 1)
                schedule(dve, [(take_qk, -1), (take_v, -1), (soften, 0), (total, 1), (divide, 1)])


def l3_block_residual(nc, k):
    with ExitStack() as ctx:
        s = Space(nc, ctx, "l3h", k)
        att = s.sb("att", [P, NB, D])
        att_in = [s.sem(f"att_in{g}") for g in range(NG)]
        summed, x_done = (s.sem(n) for n in ("summed", "x_done"))
        with nc.Block() as block:
            zero_last_stage(block, k)

            @block.sync
            def _(sp):
                for g in range(NG):
                    tiles = slice(g * G4, g * G4 + G4)
                    sp.dma_start(att[:, tiles, :], k.block_out[tiles, :, :].rearrange("b p d -> p b d")
                                 ).then_inc(att_in[g], 16)

            @block.vector
            def _(dve):
                for g in range(NG):
                    tiles = slice(g * G4, g * G4 + G4)
                    dve.wait_ge(att_in[g], 16)
                    dve.tensor_tensor(k.rows[:, tiles, :], k.rows[:, tiles, :], att[:, tiles, :], ALU.add
                                      ).then_inc(summed, 1)
                    dve.wait_ge(summed, g + 1)
                    dve.scalar_tensor_tensor(out=k.x[:, tiles, :], in0=k.rows[:, tiles, :], scalar=k.tg[:, 7:8],
                                             in1=k.x[:, tiles, :], op0=ALU.mult, op1=ALU.add).then_inc(x_done, 1)


def program(nc, d, out, first=0, last=99):
    with ExitStack() as ctx:
        s = Space(nc, ctx, "net")
        k = Shared()
        k.fetches = []
        k.d, k.stages, k.finals = d, [], ctx.enter_context(ExitStack())
        k.x = s.sb("x", [P, NB, D])
        k.rows = s.sb("rows", [P, NB, D])
        k.cols = s.sb("cols", [P, NB * P])
        k.tg = s.sb("tg", [P, 8])
        k.ident, k.lower, k.upto, k.ones = (s.sb(n, [P, P]) for n in ("ident", "lower", "upto", "ones"))
        k.neg_half = s.sb("neg_half", [P, NB])
        k.rank = s.sb("rank", [P, E])
        k.gates_w = s.sb("gates_w", [P, 4, E])
        k.logits, k.weight = (s.sb(n, [P, NB, E]) for n in ("logits", "weight"))
        k.mask_rows = s.sb("mask_rows", [E, NB * P], BF16)
        k.aT, k.emT = s.sb("aT", [P, P]), s.sb("emT", [P, P])
        k.expert_weight = s.sb("expert_weight", [P, E])
        k.neg_top = nc.dram_tensor("neg_top", (P, P), F32, kind="Internal").ap()
        k.waited_pe, k.waited_pool, k.waited_dve = (s.sem(f"waited_{n}") for n in ("pe", "pool", "dve"))
        place_weights(s, k)
        setup(nc, k)
        layers = [
            lambda: (normalise(nc, k, "n0a"), l0_attention(nc, k)),
            lambda: (normalise(nc, k, "n0f", keep_rows=True, gate_w=k.gates_w[:, 0, :], logits=k.logits),
                     l0_route(nc, k), l0_mixture(nc, k)),
            lambda: (normalise(nc, k, "n1a", fetch=(k.ctx_cols_w, k.ctx_v_w)), l1_gates(nc, k), l1_attention(nc, k)),
            lambda: (normalise(nc, k, "n1f", fetch=(k.ctx_rows_w, k.l2w_w, k.l2f_w), gate_w=k.gates_w[:, 1, :], logits=k.logits),
                     l1_route(nc, k), l1_mixture(nc, k)),
            lambda: l2_cross(nc, k),
            lambda: (normalise(nc, k, "n2f", keep_rows=True, gate_w=k.gates_w[:, 2, :], logits=k.logits),
                     capacity_route(nc, k, "l2r", k.tg[:, 6:7], int(1.2 * (NB * P // E + 1)), True,
                                    bias=k.d["L2_ffn_router_b"], floor=1e-9, add_eps=1e-9),
                     row_mixture(nc, k, "l2f", 4, ACT.Gelu, k.l2f_w, full=True)),
            lambda: (normalise(nc, k, "n3a", fetch=(k.l3f_w,)), l3_attention(nc, k)),
            lambda: l3_block(nc, k),
        ]
        for layer in layers[first:last]:
            layer()
        finish(nc, k, out)


def l2_cross(nc, k):
    with ExitStack() as ctx:
        s = Space(nc, ctx, "l2")
        k.ctx_cols = s.sb("ctx_cols", [P, NB * P])
        k.qk_w, k.vo_w = s.sb("qk_w", [P, 16, P]), s.sb("vo_w", [P, 16, P])
        norms = k.l2w_w.norms
        normalise(nc, k, "n2c", gains=k.l2w_w, source="rows", after=k.ctx_rows_w, gain=norms[:, 0:1], shift=norms[:, 1:2], columns=k.ctx_cols)
        normalise(nc, k, "n2a", gains=k.l2w_w, twice=True, gain=norms[:, 2:3], shift=norms[:, 3:4])
        l2_fold(nc, k)
        l2_attention(nc, k)


def l3_block(nc, k):
    with ExitStack() as ctx:
        norms = k.l3b_w.norms
        k.block_out = nc.dram_tensor("block_out", (NB, P, D), F32, kind="Internal").ap()
        normalise(nc, k, "n3f", gains=k.l3b_w, twice=True, gain=norms[:, 0:1], shift=norms[:, 1:2], keep_rows=True)
        l3_block_attention(nc, k)
        l3_block_residual(nc, k)
        normalise(nc, k, "n3m", gains=k.l3b_w, source="rows", gain=norms[:, 2:3], shift=norms[:, 3:4],
                  gate_w=k.gates_w[:, 3, :], logits=k.logits)
        capacity_route(nc, k, "l3r", k.tg[:, 7:8], -(-NB * P * 2 * 5 // (E * 4)), False)
        row_mixture(nc, k, "l3f", 2, ACT.Gelu_apprx_tanh, k.l3f_w)


def finish(nc, k, out):
    with ExitStack() as ctx:
        s = Space(nc, ctx, "end", k)
        stored = s.sem("stored")
        with nc.Block() as block:
            zero_last_stage(block, k)

            @block.sync
            def _(sp):
                sp.dma_start(out.rearrange("b p d -> p b d"), k.x[:, :, :]).then_inc(stored, 16)
                sp.wait_ge(stored, 16)
                for f in k.fetches:
                    if f.started:
                        f.wait(sp)


def layouts(inputs):
    import numpy as np
    a = {n: np.asarray(v) for n, v in inputs.items()}
    a["ctx"] = a.pop("ctx_1024")
    a["ctxT"] = a["ctx"].transpose(0, 2, 1)
    for n in ("bq", "bk"):
        a[f"L0_xattn_{n}_cols"] = a[f"L0_xattn_{n}"].reshape(8, 128).T
    for n in ("w1", "w2", "w3"):
        a[f"L0_{n}T"] = a.pop(f"L0_ffn_{n}").transpose(2, 0, 1)
    for n in ("b1", "b2", "b3"):
        a[f"L0_{n}T"] = a.pop(f"L0_ffn_{n}").T
    for n in ("sw1", "sw2"):
        a[f"L0_{n}T"] = a.pop(f"L0_ffn_{n}").reshape(2, 128, 128).transpose(2, 0, 1)
    a["L0_sw3T"] = a.pop("L0_ffn_sw3").T.reshape(2, 128, 128).transpose(1, 0, 2)
    a["L1_gates"] = np.concatenate([a.pop("L1_xattn_igate_kernel"), a.pop("L1_xattn_fgate_kernel")], axis=1
                                   ).reshape(3, 128, 8).transpose(1, 0, 2)
    a["L1_gate_bias"] = np.concatenate([a.pop("L1_xattn_igate_bias"), a.pop("L1_xattn_fgate_bias")]).reshape(8, 1)
    for n in ("gate", "up"):
        both = np.concatenate([a.pop(f"L1_ffn_expert_{n}_w").reshape(4, 128, 128),
                               a.pop(f"L1_ffn_shared_{n}_w")[None]])
        a[f"L1_{n}T"] = both.transpose(2, 0, 1)
    a["L1_downT"] = np.concatenate([a.pop("L1_ffn_expert_down_w").transpose(0, 2, 1).reshape(4, 128, 128),
                                    a.pop("L1_ffn_shared_down_w").T[None]]).transpose(1, 0, 2)
    a["L2_norms"] = np.stack([a.pop(f"L2_xattn_ln_{n}") for n in ("m_g", "m_b", "l_g", "l_b")], axis=1)
    wkv = a.pop("L2_xattn_Wkv")
    for n, w in (("WqT", a.pop("L2_xattn_Wq").T), ("WkT", wkv[:, :1024].T), ("WvT", wkv[:, 1024:].T),
                 ("Wout", a.pop("L2_xattn_Wout"))):
        a[f"L2_{n}"] = w.reshape(8, 128, 128).transpose(1, 0, 2)
    a["L2_w1T"] = a.pop("L2_ffn_fc1_w").reshape(8, 4, 128, 128).transpose(3, 0, 1, 2)
    a["L2_w2T"] = a.pop("L2_ffn_fc2_w").reshape(8, 128, 4, 128).transpose(3, 0, 2, 1)
    a["L2_b1T"] = a.pop("L2_ffn_fc1_b").reshape(8, 4, 128).transpose(2, 0, 1)
    def for_head(w, heads, mine):
        kept = np.zeros_like(w).reshape(128, -1, heads, 8)
        kept[:, :, mine, :] = w.reshape(128, -1, heads, 8)[:, :, mine, :]
        return kept.reshape(128, 128)
    a["L3_WqT"] = a.pop("L3_xattn_Wq").T
    wk = a.pop("L3_xattn_Wk").T
    a["L3_WkT"] = np.stack([for_head(wk, 4, r) for r in range(4)], axis=1)
    qkv = a.pop("L3_ffn_qkv_weight").reshape(4, 48, 128)
    a["L3b_WqT"] = qkv[:, :32].reshape(128, 128).T
    k4, v4 = (np.repeat(qkv[:, None, lo:lo + 8], 4, axis=1).reshape(128, 128).T for lo in (32, 40))
    a["L3b_WkT"] = k4
    a["L3b_head_of"] = np.tile(np.repeat(np.eye(4, dtype=np.float32), 8, axis=0), (4, 1))
    a["L3b_WvT"] = v4
    a["L3b_projT"] = a.pop("L3_ffn_proj_weight").T
    a["L3_norms"] = np.stack([a.pop(f"L3_ffn_{n}") for n in ("ln1_weight", "ln1_bias", "ln2_weight", "ln2_bias")], axis=1)
    a["L3_w1T"] = a.pop("L3_ffn_moe_w1").reshape(8, 128, 2, 128).transpose(1, 0, 2, 3)
    a["L3_w2T"] = a.pop("L3_ffn_moe_w2").reshape(8, 2, 128, 128).transpose(2, 0, 1, 3)
    a["routers"] = np.stack([a.pop("L0_ffn_gate_w").T, a.pop("L1_ffn_gate_w").T, a.pop("L2_ffn_router_w").T,
                             a.pop("L3_ffn_router_weight")], axis=1)
    return {n: np.ascontiguousarray(v) for n, v in a.items()}


def kernel(**inputs):
    import numpy as _np
    import concourse.bacc as _bacc
    from concourse import mybir as _mybir
    from concourse.bass_utils import run_bass_kernel_spmd as _run

    nc = _bacc.Bacc("TRN2", target_bir_lowering=False, num_devices=1)
    arrays = layouts(inputs)
    d = {n: nc.dram_tensor(n, a.shape, _mybir.dt.from_np(a.dtype), kind="ExternalInput").ap()
         for n, a in arrays.items()}
    out = nc.dram_tensor("out", arrays["x"].shape, _mybir.dt.float32, kind="ExternalOutput").ap()
    program(nc, d, out)
    r = _run(nc, [arrays], core_ids=[0])
    return r.results[0]["out"]
```
